# Optimizing a Trainium2 kernel written in Bass

```python
import numpy as np
import jax
import jax.numpy as jnp

def _softmax(x, axis=-1):
    return jax.nn.softmax(x, axis=axis)

def _gelu(x):
    return jax.nn.gelu(x, approximate=True)

def _silu(x):
    return jax.nn.silu(x)

def _sigmoid(x):
    return jax.nn.sigmoid(x)

def _layernorm(x, axis=-1, eps=1e-05):
    m = jnp.mean(x, axis=axis, keepdims=True)
    v = jnp.var(x, axis=axis, keepdims=True)
    return (x - m) / jnp.sqrt(v + eps)

def _scatter_add(tgt, idx, src, axis=0):
    return tgt.at[idx].add(src)

def _segment_sum(src, seg, n):
    return jax.ops.segment_sum(src, seg, n)
kernel_name = 'mk_gps_d1_gnn_r8_f3b868'

def setup_inputs(seed: int=0):
    np.random.seed(seed)
    _w = jnp.asarray

    def _rec_inputs():
        import jax
        import jax.numpy as jnp
        _gk = jax.random.key(seed)
        x = -0.0003713 + 1 * jax.random.normal(jax.random.fold_in(_gk, 1), (6250, 256), jnp.float32)
        src = jax.random.randint(jax.random.fold_in(_gk, 2), (100000,), 0, 6250, jnp.int32)
        dst = jax.random.randint(jax.random.fold_in(_gk, 3), (100000,), 0, 6250, jnp.int32)
        _o = jnp.argsort(dst, stable=True)
        src = src[_o]
        dst = dst[_o]
        return (x, src, dst)
    x, src, dst = _rec_inputs()

    def _L0_gnn_setup():
        import jax, jax.numpy as jnp
        import numpy as np
        N = 6250
        E = 100000
        DIN = 256
        DOUT = 256
        K = 3
        key = jax.random.key(seed)
        k1, k2, k3 = jax.random.split(key, 3)
        x = jax.random.normal(k1, (N, DIN), dtype=jnp.float32)
        edge_index = jax.random.randint(k2, (2, E), 0, N, dtype=jnp.int32)
        limit = float(np.sqrt(6.0 / (DIN + DOUT)))
        weight = jax.random.uniform(k3, (K + 1, DIN, DOUT), dtype=jnp.float32, minval=-limit, maxval=limit)
        bias = jnp.zeros((DOUT,), dtype=jnp.float32)
        return {'x': x, 'edge_index': edge_index, 'weight': weight, 'bias': bias}
    _L0_gnn_all = _L0_gnn_setup()
    _L0_gnn_in = {k: v for k, v in _L0_gnn_all.items() if k in ('weight', 'bias')}
    del _L0_gnn_all

    def _L0_mix_setup():
        import jax, jax.numpy as jnp
        import numpy as np
        NHEAD = 8
        ATT_EPS = 1e-06
        LN_EPS = 1e-05

        def _layernorm(x, g, b):
            mu = jnp.mean(x, axis=-1, keepdims=True)
            var = jnp.mean(jnp.square(x - mu), axis=-1, keepdims=True)
            return (x - mu) * jax.lax.rsqrt(var + LN_EPS) * g + b
        key = jax.random.key(seed)
        ks = jax.random.split(key, 7)
        N, L, C = (4, 2048, 256)
        s = 1.0 / np.sqrt(C)
        return {'x': jax.random.normal(ks[0], (N, L, C), jnp.float32), 'Wq': jax.random.normal(ks[1], (C, C), jnp.float32) * s, 'Wk': jax.random.normal(ks[2], (C, C), jnp.float32) * s, 'Wv': jax.random.normal(ks[3], (C, C), jnp.float32) * s, 'Wm': jax.random.normal(ks[4], (C, C), jnp.float32) * s, 'W1': jax.random.normal(ks[5], (2 * C, 2 * C), jnp.float32) * (1.0 / np.sqrt(2 * C)), 'W2': jax.random.normal(ks[6], (2 * C, C), jnp.float32) * (1.0 / np.sqrt(2 * C)), 'g1': jnp.ones((C,), jnp.float32), 'b1': jnp.zeros((C,), jnp.float32), 'g2': jnp.ones((C,), jnp.float32), 'b2': jnp.zeros((C,), jnp.float32)}
    _L0_mix_all = _L0_mix_setup()
    _L0_mix_in = {k: v for k, v in _L0_mix_all.items() if k in ('Wq', 'Wk', 'Wv', 'Wm', 'W1', 'W2', 'g1', 'b1', 'g2', 'b2')}
    del _L0_mix_all

    def _L0_ffn_setup():
        import jax, jax.numpy as jnp
        import numpy as np
        B, S, H, F, E, K = (8, 512, 256, 512, 16, 2)
        EPS = 1e-05
        key = jax.random.key(seed)
        ks = jax.random.split(key, 9)
        sc = 0.02
        return {'x': jax.random.normal(ks[0], (B, S, H), dtype=jnp.float32), 'gate_w': jax.random.normal(ks[1], (H, E), dtype=jnp.float32) * sc, 'gate_b': jnp.zeros((E,), dtype=jnp.float32), 'w1': jax.random.normal(ks[2], (E, H, F), dtype=jnp.float32) * sc, 'b1': jnp.zeros((E, F), dtype=jnp.float32), 'w2': jax.random.normal(ks[3], (E, F, H), dtype=jnp.float32) * sc, 'b2': jnp.zeros((E, H), dtype=jnp.float32), 'gamma': jnp.ones((H,), dtype=jnp.float32), 'beta': jnp.zeros((H,), dtype=jnp.float32)}
    _L0_ffn_all = _L0_ffn_setup()
    _L0_ffn_in = {k: v for k, v in _L0_ffn_all.items() if k in ('gate_w', 'gate_b', 'w1', 'b1', 'w2', 'b2', 'gamma', 'beta')}
    del _L0_ffn_all
    return {'x': x, 'src': src, 'dst': dst, 'L0_gnn_weight': _L0_gnn_in['weight'], 'L0_gnn_bias': _L0_gnn_in['bias'], 'L0_mix_Wq': _L0_mix_in['Wq'], 'L0_mix_Wk': _L0_mix_in['Wk'], 'L0_mix_Wv': _L0_mix_in['Wv'], 'L0_mix_Wm': _L0_mix_in['Wm'], 'L0_mix_W1': _L0_mix_in['W1'], 'L0_mix_W2': _L0_mix_in['W2'], 'L0_mix_g1': _L0_mix_in['g1'], 'L0_mix_b1': _L0_mix_in['b1'], 'L0_mix_g2': _L0_mix_in['g2'], 'L0_mix_b2': _L0_mix_in['b2'], 'L0_ffn_gate_w': _L0_ffn_in['gate_w'], 'L0_ffn_gate_b': _L0_ffn_in['gate_b'], 'L0_ffn_w1': _L0_ffn_in['w1'], 'L0_ffn_b1': _L0_ffn_in['b1'], 'L0_ffn_w2': _L0_ffn_in['w2'], 'L0_ffn_b2': _L0_ffn_in['b2'], 'L0_ffn_gamma': _L0_ffn_in['gamma'], 'L0_ffn_beta': _L0_ffn_in['beta']}

def reference(x, src, dst, L0_gnn_weight, L0_gnn_bias, L0_mix_Wq, L0_mix_Wk, L0_mix_Wv, L0_mix_Wm, L0_mix_W1, L0_mix_W2, L0_mix_g1, L0_mix_b1, L0_mix_g2, L0_mix_b2, L0_ffn_gate_w, L0_ffn_gate_b, L0_ffn_w1, L0_ffn_b1, L0_ffn_w2, L0_ffn_b2, L0_ffn_gamma, L0_ffn_beta):
    import jax
    import jax.numpy as jnp

    def _L0_gnn_ref(x, edge_index, weight, bias):
        import jax, jax.numpy as jnp
        import numpy as np
        N = 6250
        E = 100000
        DIN = 256
        DOUT = 256
        K = 3
        num_nodes = x.shape[0]
        loops = jnp.arange(num_nodes, dtype=edge_index.dtype)
        row = jnp.concatenate([edge_index[0], loops])
        col = jnp.concatenate([edge_index[1], loops])
        deg = jax.ops.segment_sum(jnp.ones_like(row, dtype=x.dtype), row, num_segments=num_nodes)
        deg_inv_sqrt = jnp.where(deg > 0, jax.lax.rsqrt(jnp.maximum(deg, 1e-30)), 0.0)
        Lvals = -deg_inv_sqrt[row] * deg_inv_sqrt[col]
        Lvals = jnp.where(row == col, Lvals + 1.0, Lvals)

        def spmm(v):
            return jax.ops.segment_sum(Lvals[:, None] * v[col], row, num_segments=num_nodes)
        out = jnp.matmul(x, weight[0])
        Tx_0 = x
        Tx_1 = spmm(x)
        out = out + jnp.matmul(Tx_1, weight[1])
        for k in range(2, K + 1):
            Tx_2 = 2.0 * spmm(Tx_1) - Tx_0
            out = out + jnp.matmul(Tx_2, weight[k])
            Tx_0, Tx_1 = (Tx_1, Tx_2)
        return out + bias

    def _L0_mix_ref(x, Wq, Wk, Wv, Wm, W1, W2, g1, b1, g2, b2):
        import jax, jax.numpy as jnp
        import numpy as np
        NHEAD = 8
        ATT_EPS = 1e-06
        LN_EPS = 1e-05

        def _layernorm(x, g, b):
            mu = jnp.mean(x, axis=-1, keepdims=True)
            var = jnp.mean(jnp.square(x - mu), axis=-1, keepdims=True)
            return (x - mu) * jax.lax.rsqrt(var + LN_EPS) * g + b
        N, L, C = x.shape
        H = NHEAD
        D = C // H
        q = (x @ Wq).reshape(N, L, H, D)
        k = (x @ Wk).reshape(N, L, H, D)
        v = (x @ Wv).reshape(N, L, H, D)
        Q = jax.nn.elu(q) + 1.0
        K = jax.nn.elu(k) + 1.0
        v = v / L
        KV = jnp.einsum('nshd,nshv->nhdv', K, v)
        Z = 1.0 / (jnp.einsum('nlhd,nhd->nlh', Q, K.sum(axis=1)) + ATT_EPS)
        msg = jnp.einsum('nlhd,nhdv,nlh->nlhv', Q, KV, Z) * L
        msg = msg.reshape(N, L, C) @ Wm
        msg = _layernorm(msg, g1, b1)
        h = jnp.concatenate([x, msg], axis=-1) @ W1
        h = jax.nn.relu(h) @ W2
        msg = _layernorm(h, g2, b2)
        return x + msg

    def _L0_ffn_ref(x, gate_w, gate_b, w1, b1, w2, b2, gamma, beta):
        import jax, jax.numpy as jnp
        import numpy as np
        B, S, H, F, E, K = (8, 512, 256, 512, 16, 2)
        EPS = 1e-05
        gate_logits = x @ gate_w + gate_b
        topk_vals, topk_idx = jax.lax.top_k(gate_logits, K)
        topk_w = jax.nn.softmax(topk_vals, axis=-1)
        h = jax.nn.relu(jnp.einsum('bsh,ehf->bsef', x, w1) + b1)
        expert_out = jnp.einsum('bsef,efh->bseh', h, w2) + b2
        sel = jnp.take_along_axis(expert_out, topk_idx[:, :, :, None], axis=2)
        moe = jnp.sum(topk_w[..., None] * sel, axis=2)
        y = x + moe
        mu = jnp.mean(y, axis=-1, keepdims=True)
        var = jnp.var(y, axis=-1, keepdims=True)
        return (y - mu) / jnp.sqrt(var + EPS) * gamma + beta
    edge_index = jnp.stack([src, dst])
    xn = _layernorm(x, axis=-1)
    x = x + _L0_gnn_ref(xn, edge_index, L0_gnn_weight, L0_gnn_bias) + _L0_mix_ref(xn[None], L0_mix_Wq, L0_mix_Wk, L0_mix_Wv, L0_mix_Wm, L0_mix_W1, L0_mix_W2, L0_mix_g1, L0_mix_b1, L0_mix_g2, L0_mix_b2)[0]
    x = x + _L0_ffn_ref(_layernorm(x, axis=-1)[None], L0_ffn_gate_w, L0_ffn_gate_b, L0_ffn_w1, L0_ffn_b1, L0_ffn_w2, L0_ffn_b2, L0_ffn_gamma, L0_ffn_beta)[0]
    return x

_drawn_inputs = setup_inputs


def setup_inputs(seed=0):
    import zlib

    import numpy as np

    out = dict(_drawn_inputs(seed))
    spreads = {'L0_gnn_bias': (0.0, 0.288),
     'L0_mix_g1': (1.0, 0.2),
     'L0_mix_b1': (0.0, 0.42),
     'L0_mix_g2': (1.0, 0.2),
     'L0_mix_b2': (0.0, 0.294),
     'L0_ffn_gate_b': (0.0, 0.535),
     'L0_ffn_b1': (0.0, 0.8),
     'L0_ffn_b2': (0.0, 0.513),
     'L0_ffn_gamma': (1.0, 0.2),
     'L0_ffn_beta': (0.0, 0.379)}
    factors = {'L0_ffn_gate_w': 2.73, 'L0_ffn_w1': 4.279, 'L0_ffn_w2': 3.409}
    for name, (base, spread) in spreads.items():
        noise = np.random.default_rng([zlib.crc32(name.encode()), seed]).standard_normal(out[name].shape)
        drawn = base * np.exp(spread * noise) if base else spread * noise
        out[name] = jnp.asarray(drawn.astype(out[name].dtype))
    for name, factor in factors.items():
        out[name] = (out[name] * factor).astype(out[name].dtype)
    return out
```

```python
from contextlib import ExitStack

import concourse.bass as bass
from concourse import mybir

F32 = mybir.dt.float32
BF16 = mybir.dt.bfloat16
I32 = mybir.dt.int32
U32 = mybir.dt.uint32
U16 = mybir.dt.uint16
ALU = mybir.AluOpType
ACT = mybir.ActivationFunctionType
AX_X = mybir.AxisListType.X
ds = bass.ds

P = 128
N, C = 6250, 256
CK = C // P
NT = -(-N // P)
NP = NT * P
TAIL = N - (NT - 1) * P
E = 100000
EP = 125
EC = E // EP
RING = 16
TURNS = EC // RING
NCH = -(-(E // P + NT) // RING) * RING
LOC_SHIFT = 13
NO_ROW = 255
LN_EPS, ATT_EPS = 1e-5, 1e-6
HEADS, HD = 8, 32
HH = P // HD
F2 = 512
FK = F2 // P
NE, FE = 16, 512
EK = FE // P
MT = 114
assert MT * P >= 2 * N + NE * (P - 1) and MT % 2 == 0
GB = 8


def flat(ap):
    return ap.rearrange("p a n -> p (a n)")


class Chain:

    def __init__(self, eng, sem, first=0):
        self.eng, self.sem, self.first, self.n = eng, sem, first, 0

    def __call__(self, ins):
        ins.then_inc(self.sem, 1)
        self.n += 1

    def wait(self):
        self.eng.wait_ge(self.sem, self.first + self.n)

    def step(self, ins):
        self(ins)
        self.wait()


def build(nc, x, src, dst, gnn_w, gnn_b, wq, wk, wv, wm, w1, w2, g1, b1, g2, b2,
          gate_w, gate_b, ew1, eb1, ew2, eb2, gamma, beta, out):
    def dram(name, shape, dt=F32):
        return nc.dram_tensor(name, shape, dt).ap()

    edge_list = dram("edge_list", (P * NCH,), I32)
    u_d = [dram(f"u{k}_rows", (NP, C)) for k in range(3)]
    base_d = dram("base_rows", (NP, C))
    base2_d = dram("base2_rows", (NP, C))
    xg_d = dram("xg_rows", (NP, C))
    x1_d = dram("x1_rows", (NP, C))
    slots_in = dram("slots_in", ((MT + 1) * P, C))
    slots_out = dram("slots_out", ((MT + 1) * P, C))

    with ExitStack() as outer:
        def alloc(ctx, label=""):
            sems = []

            def sem(name):
                sems.append(nc.alloc_semaphore(name=name))
                return sems[-1]

            def clear():
                if sems:
                    nc.clear_and_free_semaphores(sems)
                    nc.all_engine_barrier()

            ctx.callback(clear)
            return (lambda name, shape, dt=F32: ctx.enter_context(nc.sbuf_tensor(label + name, shape, dt)),
                    sem)

        sb, sem = alloc(outer)
        bank = [outer.enter_context(nc.psum_tensor(f"bank{i}", [P, 512], F32)) for i in range(8)]
        iota = sb("iota", [P, NCH])
        ones = sb("ones", [P, P])
        ident = sb("ident", [P, P])
        before = sb("before", [P, P])
        valid = sb("valid", [P, NT])
        slot_i = sb("slot_i", [P, 2, NT], I32)
        gate_w2 = sb("gate_w2", [P, 2, NT])
        tile_expert = sb("tile_expert", [1, MT], I32)
        with ExitStack() as graph:
            sb, _ = alloc(graph)
            cols = sb("cols", [P, NCH], U32)
            locs = sb("locs", [P, NCH])
            chunk_tile = sb("chunk_tile", [1, NCH], I32)
            degs = sb("degs", [P, 2, NT])
            dinv = sb("dinv", [P, NT])
            half = sb("half", [P, NT])
            diag = sb("diag", [P, NT])
            ndinv = sb("ndinv", [P, 2, NT])
            rows_a = sb("rows_a", [P, NT, C])
            rows_b = sb("rows_b", [P, NT, C])
            with ExitStack() as edges:
                sb, _ = alloc(edges)
                word = sb("word", [P, EC], I32)
                addr = sb("addr", [P, EC], I32)
                tile_f = sb("tile_f", [P, EC])
                self_f = sb("self_f", [P, EC])
                loc_f = sb("loc_f", [P, EC])
                sort_block(nc, outer, alloc, locals())
                mix_block(nc, outer, alloc, locals())
            for k in range(3):
                cheb_block(nc, outer, alloc, locals(), k)
            gate_block(nc, outer, alloc, locals())
        expert_block(nc, alloc, locals())
        combine_block(nc, alloc, locals())


def sort_block(nc, outer, alloc, v):
    iota, ones, ident, before = v["iota"], v["ones"], v["ident"], v["before"]
    word, addr, tile_f, self_f, loc_f, chunk_tile, bank, edge_list = (
        v[k] for k in ("word", "addr", "tile_f", "self_f", "loc_f", "chunk_tile", "bank", "edge_list"))
    slots_in = v["slots_in"]
    with ExitStack() as ctx:
        sb, sem = alloc(ctx, "sort_")
        iota_i = sb("iota_i", [P, NCH], I32)
        src_i = sb("src_i", [P, EC], I32)
        dst_i = sb("dst_i", [P, EC], I32)
        src_f = sb("src_f", [P, EC])
        dst_f = sb("dst_f", [P, EC])
        loc_i = sb("loc_i", [P, EC], I32)
        mask = sb("mask", [P, EC], BF16)
        ones_e = sb("ones_e", [P, EC], BF16)
        running = sb("running", [P, EC])
        pos_f = sb("pos_f", [P, EC])
        counts = sb("counts", [P, NT])
        small = sb("small", [P, 5, NT])
        small_i = sb("small_i", [P, NT], I32)
        base = sb("base", [P, NT])
        tab_ind = sb("tab_ind", [NT, NCH])
        first_t = sb("first_t", [NT, 1])
        fill = sb("fill", [P, NCH], I32)
        zero = sb("zero", [P, 1024])
        consts_ready, made, loaded, steps = sem("consts_ready"), sem("made"), sem("edges_loaded"), sem("sort_steps")
        stored, counted, sums, firsts, inds = sem("fill_stored"), sem("tiles_counted"), sem("sums"), sem("firsts"), sem("inds")
        scanned, scan_turn = sem("scanned"), sem("scan_turn")
        e = slice(0, EP)
        H = NCH // 2

        with nc.Block() as block:
            @block.sync
            def _(sp):
                sp.dma_start(src_i[e, :], v["src"].rearrange("(p c) -> p c", p=EP)).then_inc(loaded, 16)
                sp.dma_start(dst_i[e, :], v["dst"].rearrange("(p c) -> p c", p=EP)).then_inc(loaded, 16)
                sp.wait_ge(consts_ready, 8)
                sp.dma_start(edge_list.rearrange("(p c) -> p c", p=P), fill[:, :]).then_inc(stored, 16)
                tiles = slots_in.rearrange("(t p) c -> p t c", p=P)
                z = zero[:, :].rearrange("p (t c) -> p t c", c=C)
                n = 1
                for t in range(0, MT, 4):
                    k = min(4, MT - t)
                    sp.dma_start(tiles[:, t:t + k, :], z[:, 0:k, :]).then_inc(stored, 16)
                    n += 1
                sp.dma_start(v["slots_out"][MT * P:(MT + 1) * P, :], zero[:, 0:C]).then_inc(stored, 16)
                sp.wait_ge(stored, 16 * (n + 1))

            @block.gpsimd
            def _(pool):
                pool.iota(iota_i[:, :], pattern=[[1, NCH]], base=0, channel_multiplier=0).then_inc(consts_ready, 1)
                pool.memset(ones[:, :], 1.0).then_inc(consts_ready, 1)
                pool.memset(ones_e[:, :], 1.0).then_inc(consts_ready, 1)
                pool.memset(fill[:, :], NO_ROW << LOC_SHIFT).then_inc(consts_ready, 1)
                pool.memset(zero[:, :], 0.0).then_inc(consts_ready, 1)
                pool.memset(ident[:, :], 0.0).then_inc(made, 1)
                pool.memset(before[:, :], 1.0).then_inc(made, 1)
                pool.memset(v["valid"][:, :], 1.0).then_inc(made, 1)
                pool.wait_ge(made, 3)
                pool.affine_select(out=ident[:, :], in_=ident[:, :], compare_op=ALU.not_equal, fill=1.0, base=0,
                                   pattern=[[-1, P]], channel_multiplier=1).then_inc(consts_ready, 1)
                pool.affine_select(out=before[:, :], in_=before[:, :], compare_op=ALU.is_gt, fill=0.0, base=0,
                                   pattern=[[1, P]], channel_multiplier=-1).then_inc(consts_ready, 1)
                pool.affine_select(out=v["valid"][:, :], in_=v["valid"][:, :], compare_op=ALU.is_gt, fill=0.0, base=N,
                                   pattern=[[-P, NT]], channel_multiplier=-1).then_inc(consts_ready, 1)

            @block.vector
            def _(dve):
                s = Chain(dve, steps).step
                dve.wait_ge(consts_ready, 8)
                s(dve.tensor_copy(iota[:, :], iota_i[:, :]))
                dve.wait_ge(loaded, 32)
                s(dve.tensor_copy(src_f[e, :], src_i[e, :]))
                s(dve.tensor_copy(dst_f[e, :], dst_i[e, :]))
                s(dve.tensor_tensor(self_f[e, :], src_f[e, :], dst_f[e, :], ALU.is_equal))
                s(dve.tensor_scalar(loc_i[e, :], src_i[e, :], P - 1, None, ALU.bitwise_and))
                s(dve.tensor_copy(loc_f[e, :], loc_i[e, :]))
                s(dve.tensor_scalar(word[e, :], loc_i[e, :], LOC_SHIFT, None, ALU.logical_shift_left))
                s(dve.tensor_tensor(word[e, :], word[e, :], dst_i[e, :], ALU.bitwise_or))
                s(dve.tensor_scalar(loc_i[e, :], src_i[e, :], 7, None, ALU.arith_shift_right))
                s(dve.tensor_copy(tile_f[e, :], loc_i[e, :]))
                s(dve.tensor_scalar(self_f[e, :], self_f[e, :], -64.0, 64.0, ALU.mult, ALU.add))
                s(dve.tensor_tensor(self_f[e, :], self_f[e, :], tile_f[e, :], ALU.add))
                s(dve.memset(counts[:, :], 0.0))
                with dve.Fori(0, NT) as r:
                    dve.tensor_scalar(mask[e, :], tile_f[e, :], iota[e, ds(r, 1)], 0.0, ALU.is_equal,
                                      ALU.add, accum_out=counts[e, ds(r, 1)]).then_inc(counted, 1)
                    dve.wait_ge(counted, r + 1)
                dve.wait_ge(sums, 1)
                s(dve.tensor_copy(small[:, 0, :], bank[0][:, NT:2 * NT]))
                s(dve.tensor_scalar(small[:, 1, :], small[:, 0, :], float(P - 1), None, ALU.add))
                s(dve.tensor_copy(small_i[:, :], small[:, 1, :]))
                s(dve.tensor_scalar(small_i[:, :], small_i[:, :], 7, None, ALU.arith_shift_right))
                s(dve.tensor_copy(small[:, 2, :], small_i[:, :]))
                s(dve.tensor_tensor_scan(small[:, 3, :], ones[:, 0:NT], small[:, 2, :], 0.0, ALU.mult, ALU.add))
                s(dve.tensor_tensor(small[:, 4, :], small[:, 3, :], small[:, 2, :], ALU.subtract))
                dve.sem_inc(firsts, 1)
                s(dve.tensor_scalar(base[:, :], small[:, 4, :], float(P), -1.0, ALU.mult, ALU.add))
                s(dve.tensor_tensor(base[:, :], base[:, :], bank[0][:, 0:NT], ALU.add))
                dve.wait_ge(sums, 2)
                s(dve.tensor_copy(first_t[:, :], bank[1][0:NT, 0:1]))
                s(dve.tensor_scalar(tab_ind[:, :], iota[0:NT, :], first_t[:, 0:1], None, ALU.is_ge))
                dve.sem_inc(inds, 1)
                dve.wait_ge(sums, 3)
                for k in range(2):
                    s(dve.tensor_scalar(chunk_tile[0:1, k * H:(k + 1) * H], bank[2 + k][0:1, 0:H], -1.0, None, ALU.add))
                dve.wait_ge(counted, NT)
                with dve.Fori(0, NT) as r:
                    dve.tensor_scalar(mask[e, :], tile_f[e, :], iota[e, ds(r, 1)], None, ALU.is_equal).then_inc(scanned, 1)
                    dve.wait_ge(scanned, r * 3 + 1)
                    dve.tensor_tensor_scan(running[e, :], ones_e[e, :], mask[e, :], base[e, ds(r, 1)], ALU.mult,
                                           ALU.add).then_inc(scanned, 1)
                    dve.wait_ge(scanned, r * 3 + 2)
                    dve.sem_inc(scan_turn, 1)
                    dve.copy_predicated(pos_f[e, :], mask[e, :].bitcast(U16), running[e, :]).then_inc(scanned, 1)
                    dve.wait_ge(scanned, r * 3 + 3)
                s(dve.tensor_copy(loc_i[e, :], pos_f[e, :]))
                s(dve.tensor_scalar(dst_i[e, :], loc_i[e, :], P - 1, None, ALU.bitwise_and))
                s(dve.tensor_scalar(loc_i[e, :], loc_i[e, :], 7, None, ALU.arith_shift_right))
                s(dve.tensor_copy(src_f[e, :], dst_i[e, :]))
                s(dve.tensor_copy(dst_f[e, :], loc_i[e, :]))
                s(dve.scalar_tensor_tensor(addr[e, :], src_f[e, :], float(NCH), dst_f[e, :], ALU.mult, ALU.add))

            @block.tensor
            def _(pe):
                pe.wait_ge(consts_ready, 8)
                pe.wait_ge(counted, NT)
                pe.matmul(bank[0][:, 0:NT], before[:, :], counts[:, :], start=True, stop=True)
                pe.matmul(bank[0][:, NT:2 * NT], ones[:, :], counts[:, :], start=True, stop=True).then_inc(sums, 1)
                pe.wait_ge(firsts, 1)
                pe.transpose(bank[1][0:NT, 0:P], small[:, 4, :], ident[:, :]).then_inc(sums, 1)
                pe.wait_ge(inds, 1)
                for k in range(2):
                    ins = pe.matmul(bank[2 + k][0:1, 0:H], ones[0:NT, 0:1], tab_ind[:, k * H:(k + 1) * H],
                                    start=True, stop=True)
                ins.then_inc(sums, 1)


def wait_past(eng, sem, value):
    if not isinstance(value, int) or value > 0:
        eng.wait_ge(sem, value)


def pairs(eng, body, n=NT):
    body([0, 1])
    with eng.Fori(1, n // 2) as it:
        body([it * 2, it * 2 + 1])
    if n % 2:
        body([n - 1])


def norm_stats(dve, s, stats, mean, var, rstd, ready, rooted):
    s(dve.tensor_tensor(mean, stats[:, :, 1], stats[:, :, 4], ALU.add))
    s(dve.tensor_scalar(mean, mean, 0.5, None, ALU.mult))
    s(dve.tensor_tensor(rstd, stats[:, :, 1], stats[:, :, 4], ALU.subtract))
    s(dve.tensor_tensor(rstd, rstd, rstd, ALU.mult))
    s(dve.tensor_scalar(rstd, rstd, 0.25, LN_EPS, ALU.mult, ALU.add))
    s(dve.tensor_tensor(var, stats[:, :, 2], stats[:, :, 5], ALU.add))
    s(dve.scalar_tensor_tensor(var, var, 1.0 / C, rstd, ALU.mult, ALU.add))
    dve.sem_inc(ready, 1)
    dve.wait_ge(rooted, 1)
    s(dve.reciprocal(rstd, var))


def mix_block(nc, outer, alloc, v):
    iota, ones, ident, word, addr, tile_f, self_f, loc_f, degs, dinv, half, diag, ndinv, valid, rows_a, rows_b, bank = (
        v[k] for k in ("iota", "ones", "ident", "word", "addr", "tile_f", "self_f", "loc_f", "degs", "dinv", "half",
                       "diag", "ndinv", "valid", "rows_a", "rows_b", "bank"))
    base_d, base2_d, u_d, edge_list = v["base_d"], v["base2_d"], v["u_d"], v["edge_list"]
    xt_d = nc.dram_tensor("xt_rows", (NP, C), F32).ap()
    with ExitStack() as ctx:
        sb, sem = alloc(ctx, "mix_")
        ring_addr = sb("ring_addr", [P, 2, RING], I32)
        ring_word = sb("ring_word", [P, 2, RING], I32)
        hot_loc = sb("hot_loc", [P, 2, GB, P], BF16)
        hot_tile = sb("hot_tile", [P, 2, GB, 2, NT], BF16)
        zeros = sb("zeros", [P, P])
        wkv = sb("wkv", [P, CK, 2 * C])
        wq = sb("wq", [P, CK, C])
        wm = sb("wm", [P, CK, C])
        wg = sb("wg", [P, CK, C])
        w1 = sb("w1", [P, 2 * CK, F2])
        w2 = sb("w2", [P, FK, C])
        bias = sb("bias", [1, 2, C])
        g1c, b1c = sb("g1c", [P, CK]), sb("b1c", [P, CK])
        g2b = sb("g2b", [P, C])
        stats = sb("stats", [P, NT, 6])
        mean, var, rstd = sb("mean", [P, NT]), sb("var", [P, NT]), sb("rstd", [P, NT])
        kv_bd = sb("kv_bd", [P, CK, P + HH])
        t_row = sb("t_row", [P, 2, C])
        t_col = sb("t_col", [P, 2, CK, P])
        t_exp = sb("t_exp", [P, 2, C])
        t_k = sb("t_k", [P, 2, C])
        t_v = sb("t_v", [P, 2, CK, P + 1])
        t_out = sb("t_out", [P, 2, C])
        t_hid = sb("t_hid", [P, 2, FK, P])
        t_mt = sb("t_mt", [P, 2, CK, P])
        t_den = sb("t_den", [P, 2, 2, HEADS])
        names = ("scatter_turn scatter_copied word0 word1 x_in wts_in zeroed dsteps var_ready var_rooted "
                 "act_turn dve_turn hot_made hot_used deg_done root_in root_done").split()
        S = {n: sem("m_" + n) for n in names}
        e = slice(0, EP)
        loopsem = lambda n: sem("m_" + n)
        L1 = {n: loopsem("l1_" + n) for n in "norm xt xtc kv kmin kexp kdone vdone sum base stored0 stored1 out0 out1 moved fold".split()}
        L2 = {n: loopsem("l2_" + n) for n in "in0 in1 q qmin qexp qdone att den z msg mt mtc m stat kept".split()}
        L3 = {n: loopsem("l3_" + n) for n in "in0 in1 norm nt ntc h hc o stat kept".split()}
        L4 = {n: loopsem("l4_" + n) for n in "in0 in1 a b c u u0 u1 out0 out1".split()}
        R1 = {n: loopsem("r1_" + n) for n in "ready rooted".split()}
        R2 = {n: loopsem("r2_" + n) for n in "ready rooted".split()}
        bcol = lambda ap: ap.rearrange("(k p) -> p k", p=P)
        rowtile = lambda d, t: d.rearrange("(t p) c -> t p c", p=P)[ds(t, 1)].rearrange("a p c -> (a p) c")
        flat_a = lambda t: flat(rows_a[:, ds(t, 1), :])
        flat_b = lambda t: flat(rows_b[:, ds(t, 1), :])
        col = lambda ap, t: ap[:, ds(t, 1)]

        with nc.Block() as block:
            @block.sync
            def _(sp):
                xin = v["x"]
                sp.dma_start(rows_a[:, 0:NT - 1, :], xin[0:(NT - 1) * P, :].rearrange("(t p) c -> p t c", p=P)).then_inc(S["x_in"], 16)
                sp.wait_ge(S["zeroed"], 1)
                sp.dma_start(rows_a[0:TAIL, NT - 1, :], xin[(NT - 1) * P:N, :]).then_inc(S["x_in"], 16)
                w = S["wts_in"]
                kpc = lambda a: a.rearrange("(k p) n -> p k n", p=P)
                sp.dma_start(wkv[:, :, 0:C], kpc(v["wk"])).then_inc(w, 16)
                sp.dma_start(wkv[:, :, C:2 * C], kpc(v["wv"])).then_inc(w, 16)
                sp.dma_start(wq[:, :, :], kpc(v["wq"])).then_inc(w, 16)
                sp.dma_start(wm[:, :, :], kpc(v["wm"])).then_inc(w, 16)
                sp.dma_start(wg[:, :, :], kpc(v["gnn_w"][0])).then_inc(w, 16)
                sp.dma_start(w1[:, :, :], kpc(v["w1"])).then_inc(w, 16)
                sp.dma_start(w2[:, :, :], kpc(v["w2"])).then_inc(w, 16)
                sp.dma_start(bias[:, 0, :], v["gnn_b"].rearrange("(a n) -> a n", a=1)).then_inc(w, 16)
                sp.dma_start(bias[:, 1, :], v["b2"].rearrange("(a n) -> a n", a=1)).then_inc(w, 16)
                sp.dma_start(g2b[:, :], v["g2"].rearrange("(a n) -> a n", a=1).to_broadcast([P, C])).then_inc(w, 16)
                with nc.allow_non_contiguous_dma(reason="256 values, once"):
                    sp.dma_start(g1c[:, :], bcol(v["g1"])).then_inc(w, 16)
                    sp.dma_start(b1c[:, :], bcol(v["b1"])).then_inc(w, 16)

                def l1(ts):
                    for j, t in enumerate(ts):
                        sp.wait_ge(L1["xtc"], t + 1)
                        sp.dma_start(rowtile(xt_d, t), t_col[:, j, :, :].rearrange("p k n -> p (k n)")).then_inc(L1[f"stored{j}"], 16)
                        sp.wait_ge(L1["base"], t + 1)
                        sp.dma_start(rowtile(base_d, t), t_out[:, j, :]).then_inc(L1[f"out{j}"], 16)
                pairs(sp, l1)
                for j in range(2):
                    sp.wait_ge(L1[f"stored{j}"], 16 * (NT // 2 + 1 - j))
                    sp.wait_ge(L1[f"out{j}"], 16 * (NT // 2 + 1 - j))

                def load_xt(L, used, k):
                    def body(ts):
                        for j, t in enumerate(ts):
                            sp.wait_ge(used, (t + 1) * k)
                            sp.dma_start(t_col[:, j, :, :].rearrange("p k n -> p (k n)"), rowtile(xt_d, t)).then_inc(L[f"in{j}"], 16)
                    pairs(sp, body)
                sp.wait_ge(L1["kv"], NT)
                sp.sem_inc(L2["q"], 2)
                load_xt(L2, L2["q"], 1)
                sp.wait_ge(L2["q"], NT + 2)
                sp.sem_inc(L3["h"], 2)
                load_xt(L3, L3["h"], 1)

                def l4_in(ts):
                    for j, t in enumerate(ts):
                        wait_past(sp, L4[f"out{j}"], (t - j) * 8)
                        sp.dma_start(t_out[:, j, :], rowtile(base_d, t)).then_inc(L4[f"in{j}"], 16)
                    for j, t in enumerate(ts):
                        sp.wait_ge(L4["c"], t + 1)
                        sp.dma_start(rowtile(base2_d, t), t_out[:, j, :]).then_inc(L4[f"out{j}"], 16)
                        sp.wait_ge(L4["u"], t + 1)
                        sp.dma_start(rowtile(u_d[0], t), t_row[:, j, :]).then_inc(L4[f"u{j}"], 16)
                pairs(sp, l4_in)
                for j in range(2):
                    sp.wait_ge(L4[f"out{j}"], 16 * (NT // 2 + 1 - j))
                    sp.wait_ge(L4[f"u{j}"], 16 * (NT // 2 + 1 - j))

            @block.gpsimd
            def _(pool):
                pool.memset(rows_a[:, NT - 1, :], 0.0).then_inc(S["zeroed"], 1)
                list_rows = edge_list.rearrange("(n a) -> n a", a=1)
                half_turn = [S["word0"], S["word1"]]

                def scatter(it):
                    for h in range(2):
                        c = it * (2 * RING) + h * RING
                        wait_past(pool, half_turn[h], it * (16 * RING))
                        pool.sem_inc(S["scatter_turn"], 1)
                        pool.tensor_copy(ring_addr[e, h, :], addr[e, ds(c, RING)]).then_inc(S["scatter_copied"], 1)
                        pool.tensor_copy(ring_word[e, h, :], word[e, ds(c, RING)]).then_inc(S["scatter_copied"], 1)
                        pool.wait_ge(S["scatter_copied"], it * 4 + h * 2 + 2)
                        pool.sem_inc(S["scatter_turn"], 1)
                        for i in range(RING):
                            pool.indirect_dma_start(
                                list_rows, bass.IndirectOffsetOnAxis(ap=ring_addr[e, h, i:i + 1].bitcast(U32), axis=0),
                                ring_word[e, h, i:i + 1], None).then_inc(half_turn[h], 16)
                scatter(0)
                with pool.Fori(1, TURNS // 2) as it:
                    scatter(it)
                for h in range(2):
                    pool.wait_ge(half_turn[h], 16 * RING * (TURNS // 2))

            @block.scalar
            def _(act):
                def root(R):
                    act.wait_ge(R["ready"], 1)
                    act.activation(var[:, :], var[:, :], ACT.Sqrt).then_inc(R["rooted"], 1)

                root({"ready": S["var_ready"], "rooted": S["var_rooted"]})
                act.sem_inc(L1["moved"], 2)

                def l1(ts):
                    for j, t in enumerate(ts):
                        act.wait_ge(L1["xt"], t + 1)
                        wait_past(act, L1[f"stored{j}"], (t - j) * 8)
                        act.copy(t_col[:, j, :, :].rearrange("p k n -> p (k n)"), bank[j][:, 0:C]).then_inc(L1["xtc"], 1)
                    for j, t in enumerate(ts):
                        act.wait_ge(L1["kmin"], t + 1)
                        act.activation(t_exp[:, j, :], t_exp[:, j, :], ACT.Exp).then_inc(L1["kexp"], 1)
                    for j, t in enumerate(ts):
                        act.wait_ge(L1["sum"], t + 1)
                        act.copy(t_v[:, j, :, 0:P], bank[j][:, 0:C].rearrange("p (k n) -> p k n", k=CK)).then_inc(L1["vdone"], 1)
                    for j, t in enumerate(ts):
                        act.wait_ge(L1["base"], t + 1)
                        act.sem_inc(S["act_turn"], 1)
                        act.copy(flat_a(t), t_row[:, j, :]).then_inc(L1["moved"], 1)
                pairs(act, l1)

                def l2(ts):
                    for j, t in enumerate(ts):
                        act.wait_ge(L2["qmin"], t + 1)
                        act.activation(t_exp[:, j, :], t_exp[:, j, :], ACT.Exp).then_inc(L2["qexp"], 1)
                    for j, t in enumerate(ts):
                        act.wait_ge(L2["mt"], t + 1)
                        act.copy(t_mt[:, j, :, :].rearrange("p k n -> p (k n)"), bank[4 + j][:, 0:C]).then_inc(L2["mtc"], 1)
                    for j, t in enumerate(ts):
                        act.wait_ge(L2["m"], t + 1)
                        act.sem_inc(S["act_turn"], 1)
                        act.copy(flat_b(t), bank[6 + j][:, 0:C]).then_inc(L2["kept"], 1)
                pairs(act, l2)
                root(R1)

                def l3(ts):
                    for j, t in enumerate(ts):
                        act.wait_ge(L3["nt"], t + 1)
                        for k in range(CK):
                            act.activation(t_mt[:, j, k, :], bank[j][:, k * P:(k + 1) * P], ACT.Identity,
                                           scale=g1c[:, k:k + 1], bias=b1c[:, k:k + 1]).then_inc(L3["ntc"], 1)
                    for j, t in enumerate(ts):
                        act.wait_ge(L3["h"], t + 3)
                        act.activation(t_hid[:, j, :, :].rearrange("p k n -> p (k n)"), bank[2 + j][:, :], ACT.Relu).then_inc(L3["hc"], 1)
                    for j, t in enumerate(ts):
                        act.wait_ge(L3["o"], t + 1)
                        act.sem_inc(S["act_turn"], 1)
                        act.copy(flat_b(t), bank[4 + j][:, 0:C]).then_inc(L3["kept"], 1)
                pairs(act, l3)
                root(R2)
                act.wait_ge(S["root_in"], 1)
                act.activation(half[:, :], half[:, :], ACT.Sqrt).then_inc(S["root_done"], 1)

            @block.vector
            def _(dve):
                ch = Chain(dve, S["dsteps"])
                s = ch.step
                s(dve.memset(zeros[:, :], 0.0))
                s(dve.memset(kv_bd[:, :, :], 0.0))
                dve.wait_ge(S["x_in"], 32)
                with dve.Fori(0, NT) as t:
                    dve.bn_stats(stats[:, ds(t, 1), :].rearrange("p a n -> p (a n)"), flat_a(t)).then_inc(L1["norm"], 1)
                dve.wait_ge(L1["norm"], NT)
                norm_stats(dve, s, stats, mean[:, :], var[:, :], rstd[:, :], S["var_ready"], S["var_rooted"])
                dve.wait_ge(S["wts_in"], 16 * 12)
                s(dve.tensor_tensor(wg[:, 0, 0:P], wg[:, 0, 0:P], ident[:, :], ALU.add))
                s(dve.tensor_tensor(wg[:, 1, P:C], wg[:, 1, P:C], ident[:, :], ALU.add))
                s(dve.tensor_tensor(bias[:, 0, :], bias[:, 0, :], bias[:, 1, :], ALU.add))
                dve.sem_inc(L1["fold"], 1)

                def l1(ts):
                    for j, t in enumerate(ts):
                        dve.wait_ge(L1["moved"], t + 1)
                        dve.tensor_scalar(t_row[:, j, :], flat_a(t), col(mean, t), col(rstd, t), ALU.subtract,
                                          ALU.mult).then_inc(L1["norm"], 1)
                    for j, t in enumerate(ts):
                        dve.wait_ge(L1["kv"], t + 1)
                        dve.tensor_scalar(t_exp[:, j, :], bank[2 + j][:, 0:C], 0.0, None, ALU.min).then_inc(L1["kmin"], 1)
                    for j, t in enumerate(ts):
                        dve.wait_ge(L1["sum"], t + 1)
                        dve.tensor_scalar(t_v[:, j, :, P:P + 1], valid[:, ds(t, 1)].unsqueeze(1).to_broadcast([P, CK, 1]), 1.0, None,
                                          ALU.mult).then_inc(L1["kdone"], 1)
                        dve.wait_ge(L1["kexp"], t + 1)
                        dve.scalar_tensor_tensor(t_k[:, j, :], bank[2 + j][:, 0:C], 0.0, t_exp[:, j, :], ALU.max,
                                                 ALU.add).then_inc(L1["kdone"], 1)
                        wait_past(dve, L1[f"out{j}"], (t - j) * 8)
                        dve.tensor_tensor(t_out[:, j, :], flat_a(t), bank[4 + j][:, 0:C], ALU.add).then_inc(L1["base"], 1)
                pairs(dve, l1)

                dve.wait_ge(L1["sum"], NT + 3)
                for m in range(CK):
                    for h in range(HH):
                        r = slice(h * HD, (h + 1) * HD)
                        o = m * (P + 1)
                        s(dve.tensor_copy(kv_bd[r, m, r], bank[6][r, o + h * HD:o + (h + 1) * HD]))
                        s(dve.tensor_copy(kv_bd[r, m, P + h:P + h + 1], bank[6][r, o + P:o + P + 1]))
                dve.sem_inc(L2["den"], 1)

                def l2(ts):
                    for j, t in enumerate(ts):
                        dve.wait_ge(L2["q"], t + 3)
                        dve.tensor_scalar(t_exp[:, j, :], bank[j][:, 0:C], 0.0, None, ALU.min).then_inc(L2["qmin"], 1)
                    for j, t in enumerate(ts):
                        dve.wait_ge(L2["qexp"], t + 1)
                        dve.scalar_tensor_tensor(t_k[:, j, :], bank[j][:, 0:C], 0.0, t_exp[:, j, :], ALU.max,
                                                 ALU.add).then_inc(L2["qdone"], 1)
                    for j, t in enumerate(ts):
                        dve.wait_ge(L2["att"], t + 1)
                        att = bank[2 + j][:, 0:CK * (P + HH)].rearrange("p (k n) -> p k n", k=CK)
                        den = t_den[:, j, 0, :].rearrange("p (k h) -> p k h", k=CK)
                        z = t_den[:, j, 1, :]
                        dve.tensor_scalar(den, att[:, :, P:P + HH], ATT_EPS, None, ALU.add).then_inc(L2["z"], 1)
                        dve.wait_ge(L2["z"], t * 2 + 1)
                        dve.reciprocal(z, t_den[:, j, 0, :]).then_inc(L2["z"], 1)
                        dve.wait_ge(L2["z"], t * 2 + 2)
                        for k in range(CK):
                            zb = t_den[:, j, 1, k * HH:(k + 1) * HH].unsqueeze(2).to_broadcast([P, HH, HD])
                            dve.tensor_tensor(t_row[:, j, k * P:(k + 1) * P].rearrange("p (h d) -> p h d", d=HD),
                                              att[:, k, 0:P].rearrange("p (h d) -> p h d", d=HD), zb, ALU.mult).then_inc(L2["msg"], 1)
                    for j, t in enumerate(ts):
                        dve.wait_ge(L2["kept"], t + 1)
                        dve.sem_inc(S["dve_turn"], 1)
                        dve.bn_stats(flat(stats[:, ds(t, 1), :]), flat_b(t)).then_inc(L2["stat"], 1)
                pairs(dve, l2)
                dve.wait_ge(L2["stat"], NT)
                norm_stats(dve, s, stats, mean[:, :], var[:, :], rstd[:, :], R1["ready"], R1["rooted"])
                dve.wait_ge(L2["kept"], NT)

                def l3(ts):
                    for j, t in enumerate(ts):
                        dve.wait_ge(L3["hc"], t + 1)
                        dve.tensor_scalar(t_row[:, j, :], flat_b(t), col(mean, t), col(rstd, t), ALU.subtract,
                                          ALU.mult).then_inc(L3["norm"], 1)
                    for j, t in enumerate(ts):
                        dve.wait_ge(L3["kept"], t + 1)
                        dve.sem_inc(S["dve_turn"], 1)
                        dve.bn_stats(flat(stats[:, ds(t, 1), :]), flat_b(t)).then_inc(L3["stat"], 1)
                dve.sem_inc(L3["hc"], 2)
                pairs(dve, l3)
                dve.wait_ge(L3["stat"], NT)
                norm_stats(dve, s, stats, mean[:, :], var[:, :], rstd[:, :], R2["ready"], R2["rooted"])
                dve.wait_ge(L3["kept"], NT)

                dve.sem_inc(S["hot_used"], 2)
                with dve.Fori(0, EC // (2 * GB)) as it:
                    for h in range(2):
                        c = it * (2 * GB) + h * GB
                        dve.wait_ge(S["hot_used"], it * 2 + (h + 1))
                        dve.tensor_tensor(hot_loc[e, h, :, :], loc_f[e, ds(c, GB)].unsqueeze(2).to_broadcast([EP, GB, P]),
                                          iota[e, 0:P].unsqueeze(1).to_broadcast([EP, GB, P]), ALU.is_equal).then_inc(S["hot_made"], 1)
                        for a, key in enumerate((tile_f, self_f)):
                            dve.tensor_tensor(hot_tile[e, h, :, a, :], key[e, ds(c, GB)].unsqueeze(2).to_broadcast([EP, GB, NT]),
                                              iota[e, 0:NT].unsqueeze(1).to_broadcast([EP, GB, NT]), ALU.is_equal).then_inc(S["hot_made"], 1)
                dve.wait_ge(S["deg_done"], 1)
                s(dve.tensor_copy(degs[:, :, :], bank[0][:, 0:2 * NT].rearrange("p (a b) -> p a b", a=2)))
                s(dve.tensor_scalar(half[:, :], degs[:, 0, :], 1.0, None, ALU.add))
                dve.sem_inc(S["root_in"], 1)
                dve.wait_ge(S["root_done"], 1)
                s(dve.reciprocal(dinv[:, :], half[:, :]))
                s(dve.tensor_scalar(half[:, :], half[:, :], 0.5, None, ALU.mult))
                s(dve.tensor_tensor(diag[:, :], dinv[:, :], dinv[:, :], ALU.mult))
                s(dve.tensor_tensor(diag[:, :], degs[:, 1, :], diag[:, :], ALU.subtract))
                s(dve.tensor_scalar(diag[:, :], diag[:, :], 1.0, None, ALU.add))
                s(dve.tensor_scalar(ndinv[:, 0, :], dinv[:, :], -1.0, None, ALU.mult))
                s(dve.tensor_scalar(ndinv[:, 1, :], dinv[:, :], -2.0, None, ALU.mult))

                def l4(ts):
                    for j, t in enumerate(ts):
                        wait_past(dve, L4[f"u{j}"], (t - j) * 8)
                        dve.tensor_scalar(t_row[:, j, :], flat_a(t), col(dinv, t), None, ALU.mult).then_inc(L4["u"], 1)
                        dve.tensor_scalar(t_exp[:, j, :], flat_b(t), col(mean, t), col(rstd, t), ALU.subtract,
                                          ALU.mult).then_inc(L4["a"], 1)
                        dve.wait_ge(L4["a"], t + 1)
                        dve.tensor_tensor(t_k[:, j, :], t_exp[:, j, :], g2b[:, :], ALU.mult).then_inc(L4["b"], 1)
                        dve.wait_ge(L4["b"], t + 1)
                        dve.wait_ge(L4[f"in{j}"], (t - j) * 8 + 16)
                        dve.tensor_tensor(t_out[:, j, :], t_out[:, j, :], t_k[:, j, :], ALU.add).then_inc(L4["c"], 1)
                pairs(dve, l4)

            @block.tensor
            def _(pe):
                pe.wait_ge(L1["fold"], 1)
                kv = bank[6][:, 0:CK * (P + 1)]
                pe.matmul(kv, zeros[:, :], wkv[:, 0, 0:CK * (P + 1)], start=True, stop=False)
                pe.sem_inc(L1["sum"], 2)

                def turn(src, dst, j):
                    for k in range(CK):
                        ins = pe.transpose(dst[:, k * P:(k + 1) * P], src[:, j, k * P:(k + 1) * P], ident[:, :])
                    return ins

                def times(out, lhs, rhs, n, start=True, stop=True):
                    for k in range(n):
                        ins = pe.matmul(out, lhs(k), rhs(k), start=start and k == 0, stop=stop and k == n - 1)
                    return ins

                def l1(ts):
                    for j, t in enumerate(ts):
                        pe.wait_ge(L1["norm"], t + NT + 1)
                        turn(t_row, bank[j], j).then_inc(L1["xt"], 1)
                    for j, t in enumerate(ts):
                        pe.wait_ge(L1["xtc"], t + 1)
                        times(bank[2 + j][:, 0:C], lambda k: t_col[:, j, k, :], lambda k: wkv[:, k, 0:C], CK)
                        times(bank[j][:, 0:C], lambda k: t_col[:, j, k, :], lambda k: wkv[:, k, C:2 * C], CK)
                        times(bank[4 + j][:, 0:C], lambda k: t_col[:, j, k, :], lambda k: wg[:, k, :], CK, stop=False)
                        pe.matmul(bank[4 + j][:, 0:C], ones[0:1, :], bias[:, 0, :], start=False, stop=True).then_inc(L1["kv"], 1)
                    for j, t in enumerate(ts):
                        pe.wait_ge(L1["kdone"], t * 2 + 2)
                        pe.wait_ge(L1["vdone"], t + 1)
                        for m in range(CK):
                            ins = pe.matmul(kv[:, m * (P + 1):(m + 1) * (P + 1)], t_k[:, j, m * P:(m + 1) * P], t_v[:, j, m, :],
                                            start=False, stop=False, skip_group_check=True)
                        ins.then_inc(L1["sum"], 1)
                pairs(pe, l1)
                pe.matmul(kv, zeros[:, :], wkv[:, 0, 0:CK * (P + 1)], start=False, stop=True).then_inc(L1["sum"], 1)
                pe.wait_ge(L2["den"], 1)

                def l2(ts):
                    for j, t in enumerate(ts):
                        pe.wait_ge(L2[f"in{j}"], (t - j) * 8 + 16)
                        for m in range(CK):
                            ins = times(bank[j][:, m * P:(m + 1) * P], lambda k: wq[:, k, m * P:(m + 1) * P],
                                        lambda k: t_col[:, j, k, :], CK)
                        ins.then_inc(L2["q"], 1)
                    for j, t in enumerate(ts):
                        pe.wait_ge(L2["qdone"], t + 1)
                        for m in range(CK):
                            ins = pe.matmul(bank[2 + j][:, m * (P + HH):(m + 1) * (P + HH)], t_k[:, j, m * P:(m + 1) * P],
                                            kv_bd[:, m, :], start=True, stop=True)
                        ins.then_inc(L2["att"], 1)
                    for j, t in enumerate(ts):
                        pe.wait_ge(L2["msg"], t * 2 + 2)
                        turn(t_row, bank[4 + j], j).then_inc(L2["mt"], 1)
                    for j, t in enumerate(ts):
                        pe.wait_ge(L2["mtc"], t + 1)
                        times(bank[6 + j][:, 0:C], lambda k: t_mt[:, j, k, :], lambda k: wm[:, k, :], CK).then_inc(L2["m"], 1)
                pairs(pe, l2)

                def l3(ts):
                    for j, t in enumerate(ts):
                        pe.wait_ge(L3["norm"], t + 1)
                        turn(t_row, bank[j], j).then_inc(L3["nt"], 1)
                    for j, t in enumerate(ts):
                        pe.wait_ge(L3[f"in{j}"], (t - j) * 8 + 16)
                        pe.wait_ge(L3["ntc"], t * 2 + 2)
                        for m in range(FK):
                            ins = times(bank[2 + j][:, m * P:(m + 1) * P], lambda k: w1[:, k, m * P:(m + 1) * P],
                                        lambda k: t_col[:, j, k, :] if k < CK else t_mt[:, j, k - CK, :], 2 * CK)
                        ins.then_inc(L3["h"], 1)
                    for j, t in enumerate(ts):
                        pe.wait_ge(L3["hc"], t + 3)
                        times(bank[4 + j][:, 0:C], lambda k: t_hid[:, j, k, :], lambda k: w2[:, k, :], FK).then_inc(L3["o"], 1)
                pairs(pe, l3)
                pe.wait_ge(L3["kept"], NT)
                d = bank[0][:, 0:2 * NT]
                pe.matmul(d, zeros[:, :], ones[:, 0:2 * NT], start=True, stop=False)
                with pe.Fori(0, EC // (2 * GB)) as it:
                    for h in range(2):
                        pe.wait_ge(S["hot_made"], it * 6 + (h + 1) * 3)
                        for i in range(GB):
                            ins = pe.matmul(d, hot_loc[e, h, i, :], hot_tile[e, h, i, :, :].rearrange("p a b -> p (a b)"),
                                            start=False, stop=False, skip_group_check=True)
                        ins.then_inc(S["hot_used"], 1)
                pe.matmul(d, zeros[:, :], ones[:, 0:2 * NT], start=False, stop=True).then_inc(S["deg_done"], 1)


def cheb_block(nc, outer, alloc, v, k):
    iota, ident, cols, locs, chunk_tile, dinv, half, diag, ndinv, rows_a, rows_b, bank, edge_list, u_d = (
        v[n] for n in ("iota", "ident", "cols", "locs", "chunk_tile", "dinv", "half", "diag", "ndinv", "rows_a",
                       "rows_b", "bank", "edge_list", "u_d"))
    cur, acc = (rows_a, rows_b) if k % 2 == 0 else (rows_b, rows_a)
    base_in, base_out = (v["base2_d"], v["base_d"]) if k == 1 else (v["base_d"], v["base2_d"])
    G = 8
    HALVES = NCH // G
    with ExitStack() as ctx:
        sb, sem_ = alloc(ctx, f"cheb{k}_")
        sem = lambda n: sem_(f"c{k}_{n}")
        list_i = sb("list_i", [P, NCH], I32) if k == 0 else None
        part_i = sb("part_i", [P, NCH], I32) if k == 0 else None
        ring_idx = sb("ring_idx", [P, 2, G], U32)
        rows = sb("rows", [P, 2, G, C])
        hot = sb("hot", [P, 2, G, P])
        wt = sb("wt", [P, CK, C])
        t_row = sb("t_row", [P, C])
        t_col = sb("t_col", [P, CK, P])
        t_base = sb("t_base", [P, 2, C])
        t_u = sb("t_u", [P, 2, C])
        S = {n: sem(n) for n in ("listed clear ready gathered0 gathered1 copied pool_turn hot_made scattered added "
                                 "copied_row turned turned_col times base_in base_made base_out w_in act_turn r a b u "
                                 "out0 out1 steps").split()}
        rowtile = lambda d, t: d.rearrange("(t p) c -> t p c", p=P)[ds(t, 1)].rearrange("a p c -> (a p) c")
        tile_of = lambda rows_, t: flat(rows_[:, ds(t, 1), :])
        tiles = NT if k else 0

        def turns(eng, body):
            if tiles:
                with eng.Fori(0, tiles) as it:
                    body(it, True)
            with eng.Fori(tiles, HALVES // 2) as it:
                body(it, False)

        with nc.Block() as block:
            @block.sync
            def _(sp):
                if k == 0:
                    sp.dma_start(list_i[:, :], edge_list.rearrange("(p c) -> p c", p=P)).then_inc(S["listed"], 16)
                if tiles:
                    sp.dma_start(wt[:, :, :], v["gnn_w"][k].rearrange("(k p) n -> p k n", p=P)).then_inc(S["w_in"], 16)
                    sp.dma_start(t_base[:, 0, :], rowtile(base_in, 0)).then_inc(S["base_in"], 16)

                    def store_sum(t):
                        sp.wait_ge(S["base_made"], t + 2)
                        sp.dma_start(rowtile(base_out, t), t_base[:, 1, :]).then_inc(S["base_out"], 16)
                        sp.wait_ge(S["base_out"], t * 16 + 16)
                    with sp.Fori(0, tiles - 1) as t:
                        store_sum(t)
                        sp.dma_start(t_base[:, 0, :], rowtile(base_in, t + 1)).then_inc(S["base_in"], 16)
                    store_sum(tiles - 1)
                if k < 2:
                    def store(ts):
                        for j, t in enumerate(ts):
                            sp.wait_ge(S["u"], t + 1)
                            sp.dma_start(rowtile(u_d[k + 1], t), t_u[:, j, :]).then_inc(S[f"out{j}"], 16)
                    pairs(sp, store)
                    for j in range(2):
                        sp.wait_ge(S[f"out{j}"], 16 * (NT // 2 + 1 - j))

            @block.gpsimd
            def _(pool):
                pool.wait_ge(S["ready"], 1)
                pool.sem_inc(S["scattered"], 2 * G)

                def turn(it, _):
                    for h in range(2):
                        n = it * 2 + h
                        pool.wait_ge(S["scattered"], (n + 1) * G)
                        pool.sem_inc(S["pool_turn"], 1)
                        pool.tensor_copy(ring_idx[:, h, :], cols[:, ds(n * G, G)]).then_inc(S["copied"], 1)
                        pool.wait_ge(S["copied"], n + 1)
                        pool.sem_inc(S["pool_turn"], 1)
                        for i in range(G):
                            pool.indirect_dma_start(rows[:, h, i, :], None, u_d[k],
                                                    bass.IndirectOffsetOnAxis(ap=ring_idx[:, h, i:i + 1], axis=0)
                                                    ).then_inc(S[f"gathered{h}"], 16)
                turns(pool, turn)

            @block.scalar
            def _(act):
                if tiles:
                    act.wait_ge(S["ready"], 1)
                    with act.Fori(0, tiles) as t:
                        act.wait_ge(S["turned"], t + 1)
                        act.sem_inc(S["act_turn"], 1)
                        act.copy(t_row[:, :], tile_of(cur, t)).then_inc(S["copied_row"], 1)
                        act.wait_ge(S["turned"], t + 2)
                        act.copy(t_col[:, :, :].rearrange("p k n -> p (k n)"), bank[4][:, 0:C]).then_inc(S["turned_col"], 1)

            @block.vector
            def _(dve):
                s = Chain(dve, S["steps"]).step
                if k == 0:
                    for q in range(7):
                        s(dve.memset(acc[:, q * 7:(q + 1) * 7, :], 0.0))
                    dve.wait_ge(S["listed"], 16)
                    s(dve.tensor_scalar(part_i[:, :], list_i[:, :], (1 << LOC_SHIFT) - 1, None, ALU.bitwise_and))
                    s(dve.tensor_copy(cols[:, :], part_i[:, :]))
                    s(dve.tensor_scalar(part_i[:, :], list_i[:, :], LOC_SHIFT, None, ALU.arith_shift_right))
                    s(dve.tensor_copy(locs[:, :], part_i[:, :]))
                dve.sem_inc(S["ready"], 1)
                def turn(it, with_tile):
                    for h in range(2):
                        n = it * 2 + h
                        dve.wait_ge(S["scattered"], (n + 1) * G)
                        dve.tensor_tensor(hot[:, h, :, :], locs[:, ds(n * G, G)].unsqueeze(2).to_broadcast([P, G, P]),
                                          iota[:, 0:P].unsqueeze(1).to_broadcast([P, G, P]), ALU.is_equal).then_inc(S["hot_made"], 1)
                    if with_tile:
                        dve.wait_ge(S["base_in"], it * 16 + 16)
                        dve.wait_ge(S["times"], it + 1)
                        dve.tensor_tensor(t_base[:, 1, :], t_base[:, 0, :], bank[5][:, 0:C], ALU.add).then_inc(S["base_made"], 1)
                    for h in range(2):
                        n = it * 2 + h
                        _, regs = nc.values_load_multi_w_load_instructions(
                            chunk_tile[0:1, ds(n * G, G)], engines=[mybir.EngineType.DVE], min_val=0, max_val=NT - 1)
                        for i in range(G):
                            if i % 2 == 0:
                                dve.wait_ge(S["scattered"], n * G + 2 * G + i + 2)
                            dve.wait_ge(S["added"], n * G + 8 + i)
                            a = tile_of(acc, regs[i])
                            dve.tensor_tensor(a, a, bank[i // 2][:, (i % 2) * C:(i % 2 + 1) * C], ALU.add).then_inc(S["added"], 1)
                turns(dve, turn)
                dve.wait_ge(S["added"], NCH + 8)
                al = 0 if k == 0 else 1
                if tiles:
                    dve.wait_ge(S["times"], NT)
                if k == 1:
                    s(dve.tensor_scalar(diag[:, :], diag[:, :], 2.0, None, ALU.mult))

                def recur(ts):
                    for j, t in enumerate(ts):
                        old = tile_of(cur, t)
                        dve.wait_ge(S["a"], t + 1)
                        dve.tensor_scalar(rows[:, 0, j, :], old, diag[:, ds(t, 1)], None, ALU.mult).then_inc(S["r"], 1)
                    for j, t in enumerate(ts):
                        new, old = tile_of(acc, t), tile_of(cur, t)
                        dve.wait_ge(S["r"], t + 1)
                        dve.scalar_tensor_tensor(new, new, ndinv[:, al, ds(t, 1)], rows[:, 0, j, :], ALU.mult,
                                                 ALU.add).then_inc(S["a"], 1)
                        if k < 2:
                            dve.tensor_scalar(old, old, half[:, ds(t, 1)], None, ALU.mult).then_inc(S["b"], 1)
                    for j, t in enumerate(ts):
                        if k < 2:
                            dve.wait_ge(S["a"], t + 3)
                            wait_past(dve, S[f"out{j}"], (t - j) * 8)
                            dve.tensor_scalar(t_u[:, j, :], tile_of(acc, t), dinv[:, ds(t, 1)], None, ALU.mult).then_inc(S["u"], 1)
                dve.sem_inc(S["a"], 2)
                pairs(dve, recur)

            @block.tensor
            def _(pe):
                pe.sem_inc(S["added"], 8)
                if tiles:
                    pe.wait_ge(S["w_in"], 16)
                    pe.sem_inc(S["turned"], 1)
                    pe.sem_inc(S["base_made"], 1)

                def turn(it, with_tile):
                    if with_tile:
                        pe.wait_ge(S["copied_row"], it + 1)
                        for c in range(CK):
                            ins = pe.transpose(bank[4][:, c * P:(c + 1) * P], t_row[:, c * P:(c + 1) * P], ident[:, :])
                        ins.then_inc(S["turned"], 1)
                        pe.wait_ge(S["turned_col"], it + 1)
                        pe.wait_ge(S["base_made"], it + 1)
                        for c in range(CK):
                            ins = pe.matmul(bank[5][:, 0:C], t_col[:, c, :], wt[:, c, :], start=c == 0, stop=c == CK - 1)
                        ins.then_inc(S["times"], 1)
                    for h in range(2):
                        n = it * 2 + h
                        pe.wait_ge(S["hot_made"], n + 1)
                        pe.wait_ge(S[f"gathered{h}"], it * (16 * G) + 16 * G)
                        for i in range(G):
                            if i % 2 == 0:
                                pe.wait_ge(S["added"], n * G + i + 2)
                            pe.matmul(bank[i // 2][:, (i % 2) * C:(i % 2 + 1) * C], hot[:, h, i, :], rows[:, h, i, :],
                                      start=True, stop=True).then_inc(S["scattered"], 1)
                turns(pe, turn)


def gate_block(nc, outer, alloc, v):
    iota, ones, ident, before, valid, rows_a, rows_b, bank = (
        v[n] for n in ("iota", "ones", "ident", "before", "valid", "rows_a", "rows_b", "bank"))
    slot_i, gate_w2, tile_expert = v["slot_i"], v["gate_w2"], v["tile_expert"]
    t3, x1 = rows_b, rows_a
    with ExitStack() as ctx:
        sb, sem_ = alloc(ctx, "gate_")
        sem = lambda n: sem_("g_" + n)
        wt = sb("g_wt", [P, CK, C])
        wgate = sb("g_wgate", [P, CK, NE])
        bgate = sb("g_bgate", [1, NE])
        eb2 = sb("g_eb2", [NE, C])
        stats = sb("g_stats", [P, NT, 6])
        mean, var, rstd = sb("g_mean", [P, NT]), sb("g_var", [P, NT]), sb("g_rstd", [P, NT])
        t_row = sb("g_row", [P, 2, C])
        t_col = sb("g_col", [P, 2, CK, P])
        t_base = sb("g_base", [P, 2, C])
        t_out = sb("g_out", [P, 2, C])
        logit = sb("g_logit", [P, 2, NE])
        top = sb("g_top", [P, 2, 8])
        top_i = sb("g_top_i", [P, 2, 8], U32)
        top_f = sb("g_top_f", [P, 2, 2])
        best = sb("g_best", [P, 2, NT])
        pick = sb("g_pick", [P, 2, NT, NE])
        both = sb("g_both", [P, NT, NE])
        place = sb("g_place", [P, NT, NE])
        tot = sb("g_tot", [P, NT, NE])
        upto = sb("g_upto", [P, NE, NT])
        small = sb("g_small", [P, 5, NE])
        small_i = sb("g_small_i", [P, NE], I32)
        first_t = sb("g_first_t", [NE, 1])
        tab = sb("g_tab", [NE, MT])
        dump_i = sb("g_dump_i", [P, 1], I32)
        dump = sb("g_dump", [P, 1])
        inval = sb("g_inval", [P, NT])
        slot = sb("g_slot", [P, 2, NT])
        tmp = sb("g_tmp", [P, NT, NE])
        w_row = sb("g_wrow", [P, 2, NE])
        w_col = sb("g_wcol", [NE, 2, P])
        ring = sb("g_ring", [P, 2, C])
        ring_i = sb("g_ring_i", [P, 2, 2], I32)
        S = {n: sem(n) for n in (
            "wts base_in0 base_in1 copied turned turned_col times x1 stat steps var_ready rooted act_turn dve_turn "
            "normed nt ntc lg lgc mx mi mf pk best x1_out all ready exp_in exp_done wsum placed slots_ready pool_turn "
            "pool_copied scattered0 scattered1 wr wt wtc b2 out0 out1 outm dump kept first ind tabs x1loop").split()}
        rowtile = lambda d, t: d.rearrange("(t p) c -> t p c", p=P)[ds(t, 1)].rearrange("a p c -> (a p) c")
        tile_of = lambda rows_, t: flat(rows_[:, ds(t, 1), :])
        E2 = NT * NE // 2

        with nc.Block() as block:
            @block.sync
            def _(sp):
                kpc = lambda a: a.rearrange("(k p) n -> p k n", p=P)
                sp.dma_start(wt[:, :, :], kpc(v["gnn_w"][3])).then_inc(S["wts"], 16)
                sp.dma_start(wgate[:, :, :], kpc(v["gate_w"])).then_inc(S["wts"], 16)
                sp.dma_start(bgate[:, :], v["gate_b"].rearrange("(a n) -> a n", a=1)).then_inc(S["wts"], 16)
                sp.dma_start(eb2[:, :], v["eb2"]).then_inc(S["wts"], 16)
                sp.sem_inc(S["x1"], 2)

                def g1(ts):
                    for j, t in enumerate(ts):
                        sp.wait_ge(S["x1"], t + 1)
                        sp.dma_start(t_base[:, j, :], rowtile(v["base2_d"], t)).then_inc(S[f"base_in{j}"], 16)
                pairs(sp, g1)
                sp.wait_ge(S["x1"], NT + 2)
                sp.dma_start(v["x1_d"].rearrange("(t p) c -> p t c", p=P), x1[:, :, :]).then_inc(S["x1_out"], 16)

                def g3(ts):
                    for j, t in enumerate(ts):
                        sp.wait_ge(S["outm"], t + 1)
                        sp.dma_start(rowtile(v["xg_d"], t), t_out[:, j, :]).then_inc(S[f"out{j}"], 16)
                pairs(sp, g3)
                for j in range(2):
                    sp.wait_ge(S[f"out{j}"], 16 * (NT // 2 + 1 - j))
                sp.wait_ge(S["x1_out"], 16)

            @block.gpsimd
            def _(pool):
                pool.iota(dump_i[:, :], pattern=[[0, 1]], base=MT * P, channel_multiplier=1).then_inc(S["dump"], 1)
                pool.wait_ge(S["slots_ready"], 1)
                slots = v["slots_in"]

                def scatter(ts):
                    for j, t in enumerate(ts):
                        wait_past(pool, S[f"scattered{j}"], (t - j) * 16)
                        pool.sem_inc(S["pool_turn"], 1)
                        pool.tensor_copy(ring[:, j, :], tile_of(rows_b, t)).then_inc(S["pool_copied"], 1)
                        for a in range(2):
                            pool.tensor_copy(ring_i[:, j, a:a + 1], slot_i[:, a, ds(t, 1)]).then_inc(S["pool_copied"], 1)
                    for j, t in enumerate(ts):
                        pool.wait_ge(S["pool_copied"], t * 3 + 3)
                        pool.sem_inc(S["pool_turn"], 1)
                        for a in range(2):
                            pool.indirect_dma_start(
                                slots, bass.IndirectOffsetOnAxis(ap=ring_i[:, j, a:a + 1].bitcast(U32), axis=0),
                                ring[:, j, :], None).then_inc(S[f"scattered{j}"], 16)
                pairs(pool, scatter)
                for j in range(2):
                    pool.wait_ge(S[f"scattered{j}"], 32 * (NT // 2 + 1 - j))

            @block.scalar
            def _(act):
                def g1(ts):
                    for j, t in enumerate(ts):
                        act.wait_ge(S["turned"], t + 1)
                        act.sem_inc(S["act_turn"], 1)
                        act.copy(t_row[:, j, :], tile_of(t3, t)).then_inc(S["copied"], 1)
                    for j, t in enumerate(ts):
                        act.wait_ge(S["turned"], t + 3)
                        act.copy(t_col[:, j, :, :].rearrange("p k n -> p (k n)"), bank[j][:, 0:C]).then_inc(S["turned_col"], 1)
                pairs(act, g1)
                act.wait_ge(S["var_ready"], 1)
                act.activation(var[:, :], var[:, :], ACT.Sqrt).then_inc(S["rooted"], 1)

                def g2(ts):
                    for j, t in enumerate(ts):
                        act.wait_ge(S["nt"], t + 1)
                        act.copy(t_col[:, j, :, :].rearrange("p k n -> p (k n)"), bank[j][:, 0:C]).then_inc(S["ntc"], 1)
                        act.wait_ge(S["normed"], t + 1)
                        act.sem_inc(S["act_turn"], 1)
                        act.copy(tile_of(rows_b, t), t_row[:, j, :]).then_inc(S["kept"], 1)
                pairs(act, g2)
                act.wait_ge(S["exp_in"], 1)
                act.activation(best[:, 1, :], best[:, 1, :], ACT.Exp).then_inc(S["exp_done"], 1)

                def g3(ts):
                    for j, t in enumerate(ts):
                        act.wait_ge(S["wt"], t + 1)
                        act.copy(w_col[:, j, :], bank[j][0:NE, 0:P]).then_inc(S["wtc"], 1)
                pairs(act, g3)

            @block.vector
            def _(dve):
                s = Chain(dve, S["steps"]).step

                def g1(ts):
                    for j, t in enumerate(ts):
                        dve.wait_ge(S[f"base_in{j}"], (t - j) * 8 + 16)
                        dve.wait_ge(S["times"], t + 1)
                        dve.tensor_tensor(tile_of(x1, t), t_base[:, j, :], bank[2 + j][:, 0:C], ALU.add).then_inc(S["x1"], 1)
                    for j, t in enumerate(ts):
                        dve.wait_ge(S["x1"], t + 3)
                        dve.sem_inc(S["dve_turn"], 1)
                        dve.bn_stats(flat(stats[:, ds(t, 1), :]), tile_of(x1, t)).then_inc(S["stat"], 1)
                pairs(dve, g1)
                dve.wait_ge(S["stat"], NT)
                norm_stats(dve, s, stats, mean[:, :], var[:, :], rstd[:, :], S["var_ready"], S["rooted"])
                dve.wait_ge(S["turned_col"], NT)
                dve.sem_inc(S["kept"], 2)

                def g2(ts):
                    for j, t in enumerate(ts):
                        dve.wait_ge(S["kept"], t + 1)
                        dve.tensor_scalar(t_row[:, j, :], tile_of(x1, t), mean[:, ds(t, 1)], rstd[:, ds(t, 1)], ALU.subtract,
                                          ALU.mult).then_inc(S["normed"], 1)
                    for j, t in enumerate(ts):
                        dve.wait_ge(S["lg"], t + 1)
                        dve.tensor_copy(logit[:, j, :], bank[2 + j][:, 0:NE]).then_inc(S["lgc"], 1)
                    for j, t in enumerate(ts):
                        dve.wait_ge(S["lgc"], t + 1)
                        dve.sem_inc(S["dve_turn"], 1)
                        dve.max(top[:, j, :], logit[:, j, :]).then_inc(S["mx"], 1)
                    for j, t in enumerate(ts):
                        dve.wait_ge(S["mx"], t + 1)
                        dve.sem_inc(S["dve_turn"], 1)
                        dve.max_index(top_i[:, j, :], top[:, j, :], logit[:, j, :]).then_inc(S["mi"], 1)
                        dve.tensor_scalar(best[:, :, ds(t, 1)], top[:, j, 0:2].unsqueeze(2), 1.0, None, ALU.mult).then_inc(S["best"], 1)
                    for j, t in enumerate(ts):
                        dve.wait_ge(S["mi"], t + 1)
                        dve.tensor_copy(top_f[:, j, :], top_i[:, j, 0:2]).then_inc(S["mf"], 1)
                    for j, t in enumerate(ts):
                        dve.wait_ge(S["mf"], t + 1)
                        for a in range(2):
                            dve.tensor_scalar(flat(pick[:, a, ds(t, 1), :]), iota[:, 0:NE], top_f[:, j, a:a + 1], None,
                                              ALU.is_equal).then_inc(S["pk"], 1)
                pairs(dve, g2)
                dve.wait_ge(S["pk"], 2 * NT)
                dve.wait_ge(S["best"], NT)
                dve.wait_ge(S["kept"], NT + 2)
                vb = valid[:, :].unsqueeze(2).to_broadcast([P, NT, NE])
                s(dve.tensor_tensor(both[:, :, :], pick[:, 0, :, :], pick[:, 1, :, :], ALU.add))
                s(dve.tensor_tensor(both[:, :, :], both[:, :, :], vb, ALU.mult))
                dve.sem_inc(S["all"], 1)
                s(dve.tensor_tensor(best[:, 1, :], best[:, 1, :], best[:, 0, :], ALU.subtract))
                dve.sem_inc(S["exp_in"], 1)
                dve.wait_ge(S["exp_done"], 1)
                s(dve.tensor_scalar(best[:, 0, :], best[:, 1, :], 1.0, None, ALU.add))
                s(dve.reciprocal(gate_w2[:, 0, :], best[:, 0, :]))
                s(dve.tensor_tensor(gate_w2[:, 1, :], gate_w2[:, 0, :], best[:, 1, :], ALU.mult))
                dve.wait_ge(S["ready"], 1)
                fl = lambda a: a[:, :, :].rearrange("p t e -> p (t e)")
                for i in range(2):
                    s(dve.tensor_copy(fl(place)[:, i * E2:(i + 1) * E2], bank[i][:, 0:E2]))
                    s(dve.tensor_copy(fl(tot)[:, i * E2:(i + 1) * E2], bank[2 + i][:, 0:E2]))
                for x in range(NE):
                    s(dve.tensor_tensor_scan(upto[:, x, :], ones[:, 0:NT], tot[:, :, x], 0.0, ALU.mult, ALU.add))
                s(dve.tensor_tensor(place[:, :, :], place[:, :, :], upto[:, :, :].rearrange("p e t -> p t e"), ALU.add))
                s(dve.tensor_tensor(place[:, :, :], place[:, :, :], tot[:, :, :], ALU.subtract))
                s(dve.tensor_scalar(small[:, 0, :], upto[:, :, NT - 1], float(P - 1), None, ALU.add))
                s(dve.tensor_copy(small_i[:, :], small[:, 0, :]))
                s(dve.tensor_scalar(small_i[:, :], small_i[:, :], 7, None, ALU.arith_shift_right))
                s(dve.tensor_copy(small[:, 1, :], small_i[:, :]))
                s(dve.tensor_tensor_scan(small[:, 2, :], ones[:, 0:NE], small[:, 1, :], 0.0, ALU.mult, ALU.add))
                s(dve.tensor_tensor(small[:, 3, :], small[:, 2, :], small[:, 1, :], ALU.subtract))
                dve.sem_inc(S["first"], 1)
                s(dve.tensor_scalar(small[:, 4, :], small[:, 3, :], float(P), None, ALU.mult))
                s(dve.tensor_tensor(place[:, :, :], place[:, :, :], small[:, 4, :].unsqueeze(1).to_broadcast([P, NT, NE]), ALU.add))
                dve.wait_ge(S["tabs"], 1)
                s(dve.tensor_copy(first_t[:, :], bank[4][0:NE, 0:1]))
                s(dve.tensor_scalar(tab[:, :], iota[0:NE, 0:MT], first_t[:, 0:1], None, ALU.is_ge))
                dve.sem_inc(S["ind"], 1)
                dve.wait_ge(S["tabs"], 2)
                s(dve.tensor_scalar(tile_expert[0:1, :], bank[5][0:1, 0:MT], -1.0, None, ALU.add))
                dve.wait_ge(S["dump"], 1)
                s(dve.tensor_copy(dump[:, :], dump_i[:, :]))
                s(dve.tensor_scalar(inval[:, :], valid[:, :], -1.0, 1.0, ALU.mult, ALU.add))
                for a in range(2):
                    s(dve.tensor_tensor(tmp[:, :, :], pick[:, a, :, :], place[:, :, :], ALU.mult))
                    s(dve.tensor_reduce(slot[:, a, :], tmp[:, :, :], AX_X, ALU.add))
                    s(dve.tensor_tensor(slot[:, a, :], slot[:, a, :], valid[:, :], ALU.mult))
                    s(dve.scalar_tensor_tensor(slot[:, a, :], inval[:, :], dump[:, 0:1], slot[:, a, :], ALU.mult, ALU.add))
                    s(dve.tensor_scalar(dump[:, :], dump[:, :], -64.0, None, ALU.add))
                    s(dve.tensor_copy(slot_i[:, a, :], slot[:, a, :]))
                dve.sem_inc(S["slots_ready"], 1)
                for a in range(2):
                    s(dve.tensor_tensor(pick[:, a, :, :], pick[:, a, :, :], gate_w2[:, a, :].unsqueeze(2).to_broadcast([P, NT, NE]), ALU.mult))
                s(dve.tensor_tensor(both[:, :, :], pick[:, 0, :, :], pick[:, 1, :, :], ALU.add))

                def g3(ts):
                    for j, t in enumerate(ts):
                        dve.wait_ge(S["wtc"], t + 1)
                        dve.tensor_scalar(w_row[:, j, :], flat(both[:, ds(t, 1), :]), 1.0, None, ALU.mult).then_inc(S["wr"], 1)
                    for j, t in enumerate(ts):
                        dve.wait_ge(S["b2"], t + 1)
                        wait_past(dve, S[f"out{j}"], (t - j) * 8)
                        dve.tensor_tensor(t_out[:, j, :], tile_of(rows_b, t), bank[2 + j][:, 0:C], ALU.add).then_inc(S["outm"], 1)
                dve.sem_inc(S["wtc"], 2)
                pairs(dve, g3)

            @block.tensor
            def _(pe):
                pe.wait_ge(S["wts"], 64)
                pe.sem_inc(S["turned"], 2)

                def turn(dst, j):
                    for k in range(CK):
                        ins = pe.transpose(dst[:, k * P:(k + 1) * P], t_row[:, j, k * P:(k + 1) * P], ident[:, :])
                    return ins

                def g1(ts):
                    for j, t in enumerate(ts):
                        pe.wait_ge(S["copied"], t + 1)
                        turn(bank[j], j).then_inc(S["turned"], 1)
                    for j, t in enumerate(ts):
                        pe.wait_ge(S["turned_col"], t + 1)
                        pe.wait_ge(S["x1"], t + 1)
                        for k in range(CK):
                            ins = pe.matmul(bank[2 + j][:, 0:C], t_col[:, j, k, :], wt[:, k, :], start=k == 0, stop=k == CK - 1)
                        ins.then_inc(S["times"], 1)
                pairs(pe, g1)

                def g2(ts):
                    for j, t in enumerate(ts):
                        pe.wait_ge(S["normed"], t + 1)
                        turn(bank[j], j).then_inc(S["nt"], 1)
                    for j, t in enumerate(ts):
                        pe.wait_ge(S["ntc"], t + 1)
                        for k in range(CK):
                            pe.matmul(bank[2 + j][:, 0:NE], t_col[:, j, k, :], wgate[:, k, :], start=k == 0, stop=False)
                        pe.matmul(bank[2 + j][:, 0:NE], ones[0:1, :], bgate[:, :], start=False, stop=True).then_inc(S["lg"], 1)
                pairs(pe, g2)
                pe.wait_ge(S["all"], 1)
                fl = both[:, :, :].rearrange("p t e -> p (t e)")
                for i in range(2):
                    pe.matmul(bank[i][:, 0:E2], before[:, :], fl[:, i * E2:(i + 1) * E2], start=True, stop=True)
                    ins = pe.matmul(bank[2 + i][:, 0:E2], ones[:, :], fl[:, i * E2:(i + 1) * E2], start=True, stop=True)
                ins.then_inc(S["ready"], 1)
                pe.wait_ge(S["first"], 1)
                pe.transpose(bank[4][0:NE, 0:P], small[:, 3, :], ident[:, :]).then_inc(S["tabs"], 1)
                pe.wait_ge(S["ind"], 1)
                pe.matmul(bank[5][0:1, 0:MT], ones[0:NE, 0:1], tab[:, :], start=True, stop=True).then_inc(S["tabs"], 1)

                def g3(ts):
                    for j, t in enumerate(ts):
                        pe.wait_ge(S["wr"], t + 1)
                        pe.transpose(bank[j][0:NE, 0:P], w_row[:, j, :], ident[:, :]).then_inc(S["wt"], 1)
                    for j, t in enumerate(ts):
                        pe.wait_ge(S["wtc"], t + 3)
                        pe.matmul(bank[2 + j][:, 0:C], w_col[:, j, :], eb2[:, :], start=True, stop=True).then_inc(S["b2"], 1)
                pairs(pe, g3)


def expert_block(nc, alloc, v):
    ident, bank, slot_i, gate_w2, tile_expert = (v[n] for n in ("ident", "bank", "slot_i", "gate_w2", "tile_expert"))
    with ExitStack() as ctx:
        sb, sem_ = alloc(ctx, "expert_")
        sem = lambda n: sem_("e_" + n)
        w1 = sb("e_w1", [P, NE, CK, FE])
        w2 = sb("e_w2", [P, NE, EK, C])
        b1 = sb("e_b1", [P, NE, EK])
        xin = sb("e_xin", [P, 2, C])
        col = sb("e_col", [P, 2, CK, P])
        hid = sb("e_hid", [P, 2, FE])
        hid_t = sb("e_hid_t", [P, 2, EK, P])
        res = sb("e_res", [P, 2, C])
        S = {n: sem(n) for n in ("w b in0 in1 xt xtc h hc ht htc y yc out0 out1 act_turn zero zout".split())}
        rowtile = lambda d, t: d.rearrange("(t p) c -> t p c", p=P)[ds(t, 1)].rearrange("a p c -> (a p) c")

        with nc.Block() as block:
            @block.sync
            def _(sp):
                with nc.allow_non_contiguous_dma(reason="8192 biases, once"):
                    for x in range(NE):
                        sp.dma_start(b1[:, x, :], v["eb1"][x].rearrange("(k p) -> p k", p=P)).then_inc(S["b"], 16)
                for x in range(NE):
                    sp.dma_start(w1[:, x, :, :], v["ew1"][x].rearrange("(k p) f -> p k f", p=P)).then_inc(S["w"], 16)
                    sp.dma_start(w2[:, x, :, :], v["ew2"][x].rearrange("(k p) c -> p k c", p=P)).then_inc(S["w"], 16)
                sp.wait_ge(S["w"], 16 * 2 * NE)
                sp.sem_inc(S["xt"], 2)

                def body(ts):
                    for j, t in enumerate(ts):
                        sp.wait_ge(S["xt"], t + 1)
                        sp.dma_start(xin[:, j, :], rowtile(v["slots_in"], t)).then_inc(S[f"in{j}"], 16)
                    for j, t in enumerate(ts):
                        sp.wait_ge(S["yc"], t + 1)
                        sp.dma_start(rowtile(v["slots_out"], t), res[:, j, :]).then_inc(S[f"out{j}"], 16)
                pairs(sp, body, MT)
                for j in range(2):
                    sp.wait_ge(S[f"out{j}"], 16 * (MT // 2))

            @block.scalar
            def _(act):
                act.wait_ge(S["b"], 16 * NE)

                def body(ts):
                    for j, t in enumerate(ts):
                        act.wait_ge(S["xt"], t + 3)
                        act.copy(col[:, j, :, :].rearrange("p k n -> p (k n)"), bank[j][:, 0:C]).then_inc(S["xtc"], 1)
                    for j, t in enumerate(ts):
                        (_, (x,)) = nc.values_load_multi_w_load_instructions(
                            tile_expert[0:1, ds(t, 1)], engines=[mybir.EngineType.Activation], min_val=0, max_val=NE - 1)
                        act.wait_ge(S["ht"], t + 1)
                        act.sem_inc(S["act_turn"], 1)
                        for k in range(EK):
                            act.activation(hid_t[:, j, k, :], bank[4 + j][:, k * P:(k + 1) * P], ACT.Relu,
                                           bias=b1[:, ds(x, 1), k:k + 1].rearrange("p a b -> p (a b)")).then_inc(S["htc"], 1)
                pairs(act, body, MT)

            @block.vector
            def _(dve):

                def body(ts):
                    for j, t in enumerate(ts):
                        dve.wait_ge(S["h"], t + 1)
                        dve.tensor_copy(hid[:, j, :], bank[2 + j][:, :]).then_inc(S["hc"], 1)
                    for j, t in enumerate(ts):
                        dve.wait_ge(S["y"], t + 1)
                        wait_past(dve, S[f"out{j}"], (t - j) * 8)
                        dve.tensor_copy(res[:, j, :], bank[6 + j][:, 0:C]).then_inc(S["yc"], 1)
                pairs(dve, body, MT)

            @block.tensor
            def _(pe):
                pe.wait_ge(S["w"], 16 * 2 * NE)

                def body(ts):
                    for j, t in enumerate(ts):
                        pe.wait_ge(S[f"in{j}"], (t - j) * 8 + 16)
                        for k in range(CK):
                            ins = pe.transpose(bank[j][:, k * P:(k + 1) * P], xin[:, j, k * P:(k + 1) * P], ident[:, :])
                        ins.then_inc(S["xt"], 1)
                    expert = []
                    for j, t in enumerate(ts):
                        (_, (x,)) = nc.values_load_multi_w_load_instructions(
                            tile_expert[0:1, ds(t, 1)], engines=[mybir.EngineType.PE], min_val=0, max_val=NE - 1)
                        expert.append(x)
                    for j, t in enumerate(ts):
                        pe.wait_ge(S["xtc"], t + 1)
                        for k in range(CK):
                            ins = pe.matmul(bank[2 + j][:, :], col[:, j, k, :], w1[:, ds(expert[j], 1), k, :].rearrange("p a f -> p (a f)"),
                                            start=k == 0, stop=k == CK - 1)
                        ins.then_inc(S["h"], 1)
                    for j, t in enumerate(ts):
                        pe.wait_ge(S["hc"], t + 1)
                        for k in range(EK):
                            ins = pe.transpose(bank[4 + j][:, k * P:(k + 1) * P], hid[:, j, k * P:(k + 1) * P], ident[:, :])
                        ins.then_inc(S["ht"], 1)
                    for j, t in enumerate(ts):
                        pe.wait_ge(S["htc"], t * EK + EK)
                        for k in range(EK):
                            ins = pe.matmul(bank[6 + j][:, 0:C], hid_t[:, j, k, :], w2[:, ds(expert[j], 1), k, :].rearrange("p a f -> p (a f)"),
                                            start=k == 0, stop=k == EK - 1)
                        ins.then_inc(S["y"], 1)
                pairs(pe, body, MT)


def combine_block(nc, alloc, v):
    slot_i, gate_w2 = v["slot_i"], v["gate_w2"]
    with ExitStack() as ctx:
        sb, sem_ = alloc(ctx, "combine_")
        sem = lambda n: sem_("f_" + n)
        y = sb("f_y", [P, NT, C])
        o = sb("f_o", [P, NT, C])
        got = sb("f_got", [P, 2, 2, C])
        idx = sb("f_idx", [P, 2, 2], I32)
        gam, bet = sb("f_gam", [P, C]), sb("f_bet", [P, C])
        stats = sb("f_stats", [P, NT, 6])
        mean, var, rstd = sb("f_mean", [P, NT]), sb("f_var", [P, NT]), sb("f_rstd", [P, NT])
        t1, t2 = sb("f_t1", [P, 2, C]), sb("f_t2", [P, 2, C])
        S = {n: sem(n) for n in "in y0 y1 stat copied pool_turn got0 got1 ready rooted steps dve_turn a b c d out".split()}
        tile_of = lambda rows_, t: flat(rows_[:, ds(t, 1), :])
        CUT = [0, 16, 32, NT]

        with nc.Block() as block:
            @block.sync
            def _(sp):
                sp.dma_start(y[:, :, :], v["xg_d"].rearrange("(t p) c -> p t c", p=P)).then_inc(S["in"], 16)
                sp.dma_start(o[:, :, :], v["x1_d"].rearrange("(t p) c -> p t c", p=P)).then_inc(S["in"], 16)
                for s_, d in ((v["gamma"], gam), (v["beta"], bet)):
                    sp.dma_start(d[:, :], s_.rearrange("(a n) -> a n", a=1).to_broadcast([P, C])).then_inc(S["in"], 16)
                full = v["out"][0:(NT - 1) * P, :].rearrange("(t p) c -> p t c", p=P)
                for a, b in ((0, 16), (16, 32), (32, NT - 1)):
                    sp.wait_ge(S["d"], b)
                    sp.dma_start(full[:, a:b, :], o[:, a:b, :]).then_inc(S["out"], 16)
                sp.wait_ge(S["d"], NT)
                sp.dma_start(v["out"][(NT - 1) * P:N, :], o[0:TAIL, NT - 1, :]).then_inc(S["out"], 16)
                sp.wait_ge(S["out"], 64)

            @block.gpsimd
            def _(pool):
                pool.sem_inc(S["y1"], 2)

                def body(ts):
                    for j, t in enumerate(ts):
                        pool.wait_ge(S["y1"], t + 1)
                        pool.sem_inc(S["pool_turn"], 1)
                        for a in range(2):
                            pool.tensor_copy(idx[:, j, a:a + 1], slot_i[:, a, ds(t, 1)]).then_inc(S["copied"], 1)
                    for j, t in enumerate(ts):
                        pool.wait_ge(S["copied"], t * 2 + 2)
                        pool.sem_inc(S["pool_turn"], 1)
                        for a in range(2):
                            pool.indirect_dma_start(got[:, j, a, :], None, v["slots_out"],
                                                    bass.IndirectOffsetOnAxis(ap=idx[:, j, a:a + 1].bitcast(U32), axis=0)
                                                    ).then_inc(S[f"got{j}"], 16)
                pairs(pool, body)

            @block.scalar
            def _(act):
                act.wait_ge(S["ready"], 1)
                act.activation(var[:, :], var[:, :], ACT.Sqrt).then_inc(S["rooted"], 1)

            @block.vector
            def _(dve):
                s = Chain(dve, S["steps"]).step
                dve.wait_ge(S["in"], 64)

                def body(ts):
                    for j, t in enumerate(ts):
                        dve.wait_ge(S[f"got{j}"], (t - j) * 16 + 32)
                        yt = tile_of(y, t)
                        dve.scalar_tensor_tensor(yt, got[:, j, 0, :], gate_w2[:, 0, ds(t, 1)], yt, ALU.mult, ALU.add).then_inc(S["y0"], 1)
                    for j, t in enumerate(ts):
                        yt = tile_of(y, t)
                        dve.wait_ge(S["y0"], t + 1)
                        dve.scalar_tensor_tensor(yt, got[:, j, 1, :], gate_w2[:, 1, ds(t, 1)], yt, ALU.mult, ALU.add).then_inc(S["y1"], 1)
                    for j, t in enumerate(ts):
                        dve.wait_ge(S["y1"], t + 3)
                        dve.sem_inc(S["dve_turn"], 1)
                        dve.bn_stats(flat(stats[:, ds(t, 1), :]), tile_of(y, t)).then_inc(S["stat"], 1)
                pairs(dve, body)
                dve.wait_ge(S["stat"], NT)
                norm_stats(dve, s, stats, mean[:, :], var[:, :], rstd[:, :], S["ready"], S["rooted"])

                def last(ts):
                    for j, t in enumerate(ts):
                        dve.tensor_scalar(t1[:, j, :], tile_of(y, t), mean[:, ds(t, 1)], rstd[:, ds(t, 1)], ALU.subtract,
                                          ALU.mult).then_inc(S["a"], 1)
                    for j, t in enumerate(ts):
                        dve.wait_ge(S["a"], t + 1)
                        dve.tensor_tensor(t2[:, j, :], t1[:, j, :], gam[:, :], ALU.mult).then_inc(S["b"], 1)
                        dve.tensor_tensor(tile_of(o, t), tile_of(o, t), bet[:, :], ALU.add).then_inc(S["c"], 1)
                    for j, t in enumerate(ts):
                        dve.wait_ge(S["b"], t + 1)
                        dve.wait_ge(S["c"], t + 1)
                        dve.tensor_tensor(tile_of(o, t), tile_of(o, t), t2[:, j, :], ALU.add).then_inc(S["d"], 1)
                pairs(dve, last)


_NAMES = ["x", "src", "dst", "L0_gnn_weight", "L0_gnn_bias", "L0_mix_Wq", "L0_mix_Wk", "L0_mix_Wv", "L0_mix_Wm", "L0_mix_W1",
          "L0_mix_W2", "L0_mix_g1", "L0_mix_b1", "L0_mix_g2", "L0_mix_b2", "L0_ffn_gate_w", "L0_ffn_gate_b", "L0_ffn_w1",
          "L0_ffn_b1", "L0_ffn_w2", "L0_ffn_b2", "L0_ffn_gamma", "L0_ffn_beta"]


def kernel(**inputs):
    import numpy as np
    import concourse.bacc as bacc
    from concourse.bass_utils import run_bass_kernel_spmd as run

    nc = bacc.Bacc("TRN2", target_bir_lowering=False, num_devices=1)
    arrays, args = {}, []
    for name in _NAMES:
        a = np.ascontiguousarray(inputs[name])
        arrays["in_" + name] = a
        args.append(nc.dram_tensor("in_" + name, a.shape, mybir.dt.from_np(a.dtype), kind="ExternalInput").ap())
    result = nc.dram_tensor("result", (N, C), F32, kind="ExternalOutput").ap()
    build(nc, *args, result)
    r = run(nc, [arrays], core_ids=[0])
    return r.results[0]["result"]
```

```python
from contextlib import ExitStack

import concourse.bass as bass
from concourse import mybir

F32 = mybir.dt.float32
BF16 = mybir.dt.bfloat16
I32 = mybir.dt.int32
U32 = mybir.dt.uint32
U16 = mybir.dt.uint16
ALU = mybir.AluOpType
ACT = mybir.ActivationFunctionType
AX_X = mybir.AxisListType.X
ds = bass.ds

P = 128
N, C = 6250, 256
CK = C // P
NT = -(-N // P)
NP = NT * P
TAIL = N - (NT - 1) * P
E = 100000
EP = 125
EC = E // EP
RING = 16
TURNS = EC // RING
NCH = -(-(E // P + NT) // RING) * RING
LOC_SHIFT = 13
NO_ROW = 255
LN_EPS, ATT_EPS = 1e-5, 1e-6
HEADS, HD = 8, 32
HH = P // HD
F2 = 512
FK = F2 // P
NE, FE = 16, 512
EK = FE // P
MT = 114
assert MT * P >= 2 * N + NE * (P - 1) and MT % 2 == 0
GB = 8
assert EC == (NT + 1) * 2 * GB


def flat(ap):
    return ap.rearrange("p a n -> p (a n)")


class Chain:

    def __init__(self, eng, sem, first=0):
        self.eng, self.sem, self.first, self.n = eng, sem, first, 0

    def __call__(self, ins):
        ins.then_inc(self.sem, 1)
        self.n += 1

    def wait(self):
        self.eng.wait_ge(self.sem, self.first + self.n)

    def step(self, ins):
        self(ins)
        self.wait()


def build(nc, x, src, dst, gnn_w, gnn_b, wq, wk, wv, wm, w1, w2, g1, b1, g2, b2,
          gate_w, gate_b, ew1, eb1, ew2, eb2, gamma, beta, out):
    def dram(name, shape, dt=F32):
        return nc.dram_tensor(name, shape, dt).ap()

    edge_list = dram("edge_list", (P * NCH,), I32)
    u_d = [dram(f"u{k}_rows", (NP, C)) for k in range(3)]
    base_d = dram("base_rows", (NP, C))
    base2_d = dram("base2_rows", (NP, C))
    h2_d = dram("h2_rows", (NP, C))
    xg_d = dram("xg_rows", (NP, C))
    x1_d = dram("x1_rows", (NP, C))
    slots_in = dram("slots_in", ((MT + 1) * P, C))
    slots_out = dram("slots_out", ((MT + 1) * P, C))

    with ExitStack() as outer:
        def alloc(ctx, label=""):
            sems = []

            def sem(name):
                sems.append(nc.alloc_semaphore(name=name))
                return sems[-1]

            def clear():
                if sems:
                    nc.clear_and_free_semaphores(sems)
                    nc.all_engine_barrier()

            ctx.callback(clear)
            return (lambda name, shape, dt=F32: ctx.enter_context(nc.sbuf_tensor(label + name, shape, dt)),
                    sem)

        sb, sem = alloc(outer)
        bank = [outer.enter_context(nc.psum_tensor(f"bank{i}", [P, 512], F32)) for i in range(8)]
        iota = sb("iota", [P, NCH])
        ones = sb("ones", [P, P])
        ident = sb("ident", [P, P])
        before = sb("before", [P, P])
        valid = sb("valid", [P, NT])
        slot_i = sb("slot_i", [P, 2, NT], I32)
        gate_w2 = sb("gate_w2", [P, 2, NT])
        tile_expert = sb("tile_expert", [1, MT], I32)
        with ExitStack() as graph:
            sb, _ = alloc(graph)
            cols = sb("cols", [P, NCH], U32)
            locs = sb("locs", [P, NCH])
            chunk_tile = sb("chunk_tile", [1, NCH], I32)
            degs = sb("degs", [P, 2, NT])
            dinv = sb("dinv", [P, NT])
            half = sb("half", [P, NT])
            diag = sb("diag", [P, NT])
            own = sb("own", [P, NT])
            ndinv = sb("ndinv", [P, 2, NT])
            udinv = sb("udinv", [P, 2, NT])
            mean, var, rstd = sb("mean", [P, NT]), sb("var", [P, NT]), sb("rstd", [P, NT])
            rows_a = sb("rows_a", [P, NT, C])
            rows_b = sb("rows_b", [P, NT, C])
            with ExitStack() as edges:
                sb, _ = alloc(edges)
                word = sb("word", [P, EC], I32)
                addr = sb("addr", [P, EC], I32)
                tile_f = sb("tile_f", [P, EC])
                self_f = sb("self_f", [P, EC])
                loc_f = sb("loc_f", [P, EC])
                sort_block(nc, outer, alloc, locals())
                mix_block(nc, outer, alloc, locals())
            for k in range(3):
                cheb_block(nc, outer, alloc, locals(), k)
            gate_block(nc, outer, alloc, locals())
        expert_block(nc, alloc, locals())
        combine_block(nc, alloc, locals())


def sort_block(nc, outer, alloc, v):
    iota, ones, ident, before = v["iota"], v["ones"], v["ident"], v["before"]
    word, addr, tile_f, self_f, loc_f, chunk_tile, bank, edge_list = (
        v[k] for k in ("word", "addr", "tile_f", "self_f", "loc_f", "chunk_tile", "bank", "edge_list"))
    slots_in, rows_a = v["slots_in"], v["rows_a"]
    with ExitStack() as ctx:
        sb, sem = alloc(ctx, "sort_")
        iota_i = sb("iota_i", [P, NCH], I32)
        src_i = sb("src_i", [P, EC], I32)
        dst_i = sb("dst_i", [P, EC], I32)
        src_f = sb("src_f", [P, EC])
        dst_f = sb("dst_f", [P, EC])
        loc_i = sb("loc_i", [P, EC], I32)
        mask = sb("mask", [P, EC], BF16)
        ones_e = sb("ones_e", [P, EC], BF16)
        running = sb("running", [P, EC])
        pos_f = sb("pos_f", [P, EC])
        counts = sb("counts", [P, NT])
        small = sb("small", [P, 5, NT])
        small_i = sb("small_i", [P, NT], I32)
        base = sb("base", [P, NT])
        tab_ind = sb("tab_ind", [NT, NCH])
        first_t = sb("first_t", [NT, 1])
        fill = sb("fill", [P, NCH], I32)
        zero = sb("zero", [P, 1024])
        consts_ready, made, loaded, steps = sem("consts_ready"), sem("made"), sem("edges_loaded"), sem("sort_steps")
        stored, counted, sums, firsts, inds = sem("fill_stored"), sem("tiles_counted"), sem("sums"), sem("firsts"), sem("inds")
        scanned, scan_turn = sem("scanned"), sem("scan_turn")
        e = slice(0, EP)
        H = NCH // 2

        with nc.Block() as block:
            @block.sync
            def _(sp):
                sp.dma_start(src_i[e, :], v["src"].rearrange("(p c) -> p c", p=EP)).then_inc(loaded, 16)
                sp.dma_start(dst_i[e, :], v["dst"].rearrange("(p c) -> p c", p=EP)).then_inc(loaded, 16)
                xin = v["x"]
                sp.dma_start(rows_a[:, 0:NT - 1, :], xin[0:(NT - 1) * P, :].rearrange("(t p) c -> p t c", p=P)).then_inc(stored, 16)
                sp.wait_ge(consts_ready, 9)
                sp.dma_start(rows_a[0:TAIL, NT - 1, :], xin[(NT - 1) * P:N, :]).then_inc(stored, 16)
                sp.dma_start(edge_list.rearrange("(p c) -> p c", p=P), fill[:, :]).then_inc(stored, 16)
                tiles = slots_in.rearrange("(t p) c -> p t c", p=P)
                z = zero[:, :].rearrange("p (t c) -> p t c", c=C)
                n = 3
                for t in range(0, MT, 4):
                    k = min(4, MT - t)
                    sp.dma_start(tiles[:, t:t + k, :], z[:, 0:k, :]).then_inc(stored, 16)
                    n += 1
                sp.dma_start(v["slots_out"][MT * P:(MT + 1) * P, :], zero[:, 0:C]).then_inc(stored, 16)
                sp.wait_ge(stored, 16 * (n + 1))

            @block.gpsimd
            def _(pool):
                pool.memset(rows_a[:, NT - 1, :], 0.0).then_inc(consts_ready, 1)
                pool.iota(iota_i[:, :], pattern=[[1, NCH]], base=0, channel_multiplier=0).then_inc(consts_ready, 1)
                pool.memset(ones[:, :], 1.0).then_inc(consts_ready, 1)
                pool.memset(ones_e[:, :], 1.0).then_inc(consts_ready, 1)
                pool.memset(fill[:, :], NO_ROW << LOC_SHIFT).then_inc(consts_ready, 1)
                pool.memset(zero[:, :], 0.0).then_inc(consts_ready, 1)
                pool.memset(ident[:, :], 0.0).then_inc(made, 1)
                pool.memset(before[:, :], 1.0).then_inc(made, 1)
                pool.memset(v["valid"][:, :], 1.0).then_inc(made, 1)
                pool.wait_ge(made, 3)
                pool.affine_select(out=ident[:, :], in_=ident[:, :], compare_op=ALU.not_equal, fill=1.0, base=0,
                                   pattern=[[-1, P]], channel_multiplier=1).then_inc(consts_ready, 1)
                pool.affine_select(out=before[:, :], in_=before[:, :], compare_op=ALU.is_gt, fill=0.0, base=0,
                                   pattern=[[1, P]], channel_multiplier=-1).then_inc(consts_ready, 1)
                pool.affine_select(out=v["valid"][:, :], in_=v["valid"][:, :], compare_op=ALU.is_gt, fill=0.0, base=N,
                                   pattern=[[-P, NT]], channel_multiplier=-1).then_inc(consts_ready, 1)

            @block.vector
            def _(dve):
                s = Chain(dve, steps).step
                dve.wait_ge(consts_ready, 9)
                s(dve.tensor_copy(iota[:, :], iota_i[:, :]))
                dve.wait_ge(loaded, 32)
                s(dve.tensor_copy(src_f[e, :], src_i[e, :]))
                s(dve.tensor_copy(dst_f[e, :], dst_i[e, :]))
                s(dve.tensor_tensor(self_f[e, :], src_f[e, :], dst_f[e, :], ALU.is_equal))
                s(dve.tensor_scalar(loc_i[e, :], src_i[e, :], P - 1, None, ALU.bitwise_and))
                s(dve.tensor_copy(loc_f[e, :], loc_i[e, :]))
                s(dve.tensor_scalar(word[e, :], loc_i[e, :], LOC_SHIFT, None, ALU.logical_shift_left))
                s(dve.tensor_tensor(word[e, :], word[e, :], dst_i[e, :], ALU.bitwise_or))
                s(dve.tensor_scalar(loc_i[e, :], src_i[e, :], 7, None, ALU.arith_shift_right))
                s(dve.tensor_copy(tile_f[e, :], loc_i[e, :]))
                s(dve.tensor_scalar(self_f[e, :], self_f[e, :], -64.0, 64.0, ALU.mult, ALU.add))
                s(dve.tensor_tensor(self_f[e, :], self_f[e, :], tile_f[e, :], ALU.add))
                s(dve.memset(counts[:, :], 0.0))
                with dve.Fori(0, NT) as r:
                    dve.tensor_scalar(mask[e, :], tile_f[e, :], iota[e, ds(r, 1)], 0.0, ALU.is_equal,
                                      ALU.add, accum_out=counts[e, ds(r, 1)]).then_inc(counted, 1)
                    dve.wait_ge(counted, r + 1)
                dve.wait_ge(sums, 1)
                s(dve.tensor_copy(small[:, 0, :], bank[0][:, NT:2 * NT]))
                s(dve.tensor_scalar(small[:, 1, :], small[:, 0, :], float(P - 1), None, ALU.add))
                s(dve.tensor_copy(small_i[:, :], small[:, 1, :]))
                s(dve.tensor_scalar(small_i[:, :], small_i[:, :], 7, None, ALU.arith_shift_right))
                s(dve.tensor_copy(small[:, 2, :], small_i[:, :]))
                s(dve.tensor_tensor_scan(small[:, 3, :], ones[:, 0:NT], small[:, 2, :], 0.0, ALU.mult, ALU.add))
                s(dve.tensor_tensor(small[:, 4, :], small[:, 3, :], small[:, 2, :], ALU.subtract))
                dve.sem_inc(firsts, 1)
                s(dve.tensor_scalar(base[:, :], small[:, 4, :], float(P), -1.0, ALU.mult, ALU.add))
                s(dve.tensor_tensor(base[:, :], base[:, :], bank[0][:, 0:NT], ALU.add))
                dve.wait_ge(sums, 2)
                s(dve.tensor_copy(first_t[:, :], bank[1][0:NT, 0:1]))
                s(dve.tensor_scalar(tab_ind[:, :], iota[0:NT, :], first_t[:, 0:1], None, ALU.is_ge))
                dve.sem_inc(inds, 1)
                dve.wait_ge(sums, 3)
                for k in range(2):
                    s(dve.tensor_scalar(chunk_tile[0:1, k * H:(k + 1) * H], bank[2 + k][0:1, 0:H], -1.0, None, ALU.add))
                dve.wait_ge(counted, NT)
                with dve.Fori(0, NT) as r:
                    dve.tensor_scalar(mask[e, :], tile_f[e, :], iota[e, ds(r, 1)], None, ALU.is_equal).then_inc(scanned, 1)
                    dve.wait_ge(scanned, r * 3 + 1)
                    dve.tensor_tensor_scan(running[e, :], ones_e[e, :], mask[e, :], base[e, ds(r, 1)], ALU.mult,
                                           ALU.add).then_inc(scanned, 1)
                    dve.wait_ge(scanned, r * 3 + 2)
                    dve.sem_inc(scan_turn, 1)
                    dve.copy_predicated(pos_f[e, :], mask[e, :].bitcast(U16), running[e, :]).then_inc(scanned, 1)
                    dve.wait_ge(scanned, r * 3 + 3)
                s(dve.tensor_copy(loc_i[e, :], pos_f[e, :]))
                s(dve.tensor_scalar(dst_i[e, :], loc_i[e, :], P - 1, None, ALU.bitwise_and))
                s(dve.tensor_scalar(loc_i[e, :], loc_i[e, :], 7, None, ALU.arith_shift_right))
                s(dve.tensor_copy(src_f[e, :], dst_i[e, :]))
                s(dve.tensor_copy(dst_f[e, :], loc_i[e, :]))
                s(dve.scalar_tensor_tensor(addr[e, :], src_f[e, :], float(NCH), dst_f[e, :], ALU.mult, ALU.add))

            @block.tensor
            def _(pe):
                pe.wait_ge(consts_ready, 9)
                pe.wait_ge(counted, NT)
                pe.matmul(bank[0][:, 0:NT], before[:, :], counts[:, :], start=True, stop=True)
                pe.matmul(bank[0][:, NT:2 * NT], ones[:, :], counts[:, :], start=True, stop=True).then_inc(sums, 1)
                pe.wait_ge(firsts, 1)
                pe.transpose(bank[1][0:NT, 0:P], small[:, 4, :], ident[:, :]).then_inc(sums, 1)
                pe.wait_ge(inds, 1)
                for k in range(2):
                    ins = pe.matmul(bank[2 + k][0:1, 0:H], ones[0:NT, 0:1], tab_ind[:, k * H:(k + 1) * H],
                                    start=True, stop=True)
                ins.then_inc(sums, 1)


def wait_past(eng, sem, value):
    if not isinstance(value, int) or value > 0:
        eng.wait_ge(sem, value)


def pairs(eng, body, n=NT):
    body([0, 1])
    with eng.Fori(1, n // 2) as it:
        body([it * 2, it * 2 + 1])
    if n % 2:
        body([n - 1])


def ahead(eng, first, body, n=NT):
    m = n // 2
    odd = [n - 1] if n % 2 else []
    first([0, 1])
    body([0, 1], [2, 3])
    with eng.Fori(1, m - 1) as it:
        body([it * 2, it * 2 + 1], [it * 2 + 2, it * 2 + 3])
    body([2 * m - 2, 2 * m - 1], odd)
    if odd:
        body(odd, [])


def pair_before(ts):
    if isinstance(ts[0], int) and ts[0] == 0:
        return []
    return [ts[0] - 2, ts[0] - 1]


def norm_stats(dve, s, stats, mean, var, rstd, ready, rooted):
    s(dve.tensor_tensor(mean, stats[:, :, 1], stats[:, :, 4], ALU.add))
    s(dve.tensor_scalar(mean, mean, 0.5, None, ALU.mult))
    s(dve.tensor_tensor(rstd, stats[:, :, 1], stats[:, :, 4], ALU.subtract))
    s(dve.tensor_tensor(rstd, rstd, rstd, ALU.mult))
    s(dve.tensor_scalar(rstd, rstd, 0.25, LN_EPS, ALU.mult, ALU.add))
    s(dve.tensor_tensor(var, stats[:, :, 2], stats[:, :, 5], ALU.add))
    s(dve.scalar_tensor_tensor(var, var, 1.0 / C, rstd, ALU.mult, ALU.add))
    dve.sem_inc(ready, 1)
    dve.wait_ge(rooted, 1)
    s(dve.reciprocal(rstd, var))


def mix_block(nc, outer, alloc, v):
    iota, ones, ident, word, addr, tile_f, self_f, loc_f, degs, dinv, half, diag, valid, rows_a, rows_b, bank = (
        v[k] for k in ("iota", "ones", "ident", "word", "addr", "tile_f", "self_f", "loc_f", "degs", "dinv", "half",
                       "diag", "valid", "rows_a", "rows_b", "bank"))
    own, ndinv, udinv, mean, var, rstd = (v[k] for k in ("own", "ndinv", "udinv", "mean", "var", "rstd"))
    base_d, h2_d, edge_list = v["base_d"], v["h2_d"], v["edge_list"]
    xt_d = nc.dram_tensor("xt_rows", (NP, C), F32).ap()
    with ExitStack() as ctx:
        sb, sem = alloc(ctx, "mix_")
        ring_addr = sb("ring_addr", [P, 2, RING], I32)
        ring_word = sb("ring_word", [P, 2, RING], I32)
        hot_loc = sb("hot_loc", [P, 2, GB, P], BF16)
        hot_tile = sb("hot_tile", [P, 2, GB, 2, NT], BF16)
        zeros = sb("zeros", [P, P])
        wkg = sb("wkg", [P, CK, 2 * C])
        wv = sb("wv", [P, CK, C])
        wq = sb("wq", [P, CK, C])
        wm = sb("wm", [P, CK, C])
        w1 = sb("w1", [P, 2 * CK, F2])
        w2 = sb("w2", [P, FK, C])
        g1c, b1c = sb("g1c", [P, CK]), sb("b1c", [P, CK])
        stats = sb("stats", [P, NT, 6])
        kv_bd = sb("kv_bd", [P, CK, P + HH])
        t_row = sb("t_row", [P, 2, C])
        t_col = sb("t_col", [P, 2, CK, P])
        t_exp = sb("t_exp", [P, 2, C])
        t_k = sb("t_k", [P, 2, C])
        t_v = sb("t_v", [P, 2, CK, P + 1])
        t_out = sb("t_out", [P, 2, C])
        t_hid = sb("t_hid", [P, 2, FK, P])
        t_mt = sb("t_mt", [P, 2, CK, P])
        t_den = sb("t_den", [P, 2, 2, HEADS])
        names = ("scatter_turn scatter_copied word0 word1 wts_in dsteps var_ready var_rooted "
                 "act_turn dve_turn hot_made hot_used deg_done root_in root_done").split()
        S = {n: sem("m_" + n) for n in names}
        e = slice(0, EP)
        loopsem = lambda n: sem("m_" + n)
        L1 = {n: loopsem("l1_" + n) for n in "stat norm xt xtc kg v kmin kexp kdone vdone sum base kept stored0 stored1 out0 out1 fold".split()}
        L2 = {n: loopsem("l2_" + n) for n in "in0 in1 q qmin qexp qdone att den z msg mt mtc m stat kept".split()}
        L3 = {n: loopsem("l3_" + n) for n in "in0 in1 norm nt ntc h hc o stat kept out0 out1".split()}
        R1 = {n: loopsem("r1_" + n) for n in "ready rooted".split()}
        R2 = {n: loopsem("r2_" + n) for n in "ready rooted".split()}
        bcol = lambda ap: ap.rearrange("(k p) -> p k", p=P)
        rowtile = lambda d, t: d.rearrange("(t p) c -> t p c", p=P)[ds(t, 1)].rearrange("a p c -> (a p) c")
        flat_a = lambda t: flat(rows_a[:, ds(t, 1), :])
        flat_b = lambda t: flat(rows_b[:, ds(t, 1), :])
        col = lambda ap, t: ap[:, ds(t, 1)]

        with nc.Block() as block:
            @block.sync
            def _(sp):
                w = S["wts_in"]
                kpc = lambda a: a.rearrange("(k p) n -> p k n", p=P)
                sp.dma_start(wkg[:, :, 0:C], kpc(v["wk"])).then_inc(w, 16)
                sp.dma_start(wkg[:, :, C:2 * C], kpc(v["gnn_w"][0])).then_inc(w, 16)
                sp.dma_start(wv[:, :, :], kpc(v["wv"])).then_inc(w, 16)
                sp.dma_start(wq[:, :, :], kpc(v["wq"])).then_inc(w, 16)
                sp.dma_start(wm[:, :, :], kpc(v["wm"])).then_inc(w, 16)
                sp.dma_start(w1[:, :, :], kpc(v["w1"])).then_inc(w, 16)
                sp.dma_start(w2[:, :, :], kpc(v["w2"])).then_inc(w, 16)
                with nc.allow_non_contiguous_dma(reason="256 values, once"):
                    sp.dma_start(g1c[:, :], bcol(v["g1"])).then_inc(w, 16)
                    sp.dma_start(b1c[:, :], bcol(v["b1"])).then_inc(w, 16)

                def l1(ts):
                    for j, t in enumerate(ts):
                        sp.wait_ge(L1["xtc"], t + 1)
                        sp.dma_start(rowtile(xt_d, t), t_col[:, j, :, :].rearrange("p k n -> p (k n)")).then_inc(L1[f"stored{j}"], 16)
                    for j, t in enumerate(ts):
                        sp.wait_ge(L1["base"], t + 3)
                        sp.dma_start(rowtile(base_d, t), t_out[:, j, :]).then_inc(L1[f"out{j}"], 16)
                pairs(sp, l1)
                for j in range(2):
                    sp.wait_ge(L1[f"stored{j}"], 16 * (NT // 2 + 1 - j))
                    sp.wait_ge(L1[f"out{j}"], 16 * (NT // 2 + 1 - j))

                def load_xt(L, ts):
                    for j, t in enumerate(ts):
                        sp.dma_start(t_col[:, j, :, :].rearrange("p k n -> p (k n)"), rowtile(xt_d, t)).then_inc(L[f"in{j}"], 16)
                sp.wait_ge(L1["sum"], NT + 2)
                load_xt(L2, [0, 1])

                def l2(ts, later):
                    for j, t in enumerate(later):
                        sp.wait_ge(L2["q"], t - 1)
                        sp.dma_start(t_col[:, j, :, :].rearrange("p k n -> p (k n)"), rowtile(xt_d, t)).then_inc(L2[f"in{j}"], 16)
                ahead(sp, lambda ts: None, l2)
                sp.wait_ge(L2["q"], NT)
                load_xt(L3, [0, 1])

                def store_h2(ts):
                    for j, t in enumerate(ts):
                        sp.wait_ge(L3["kept"], t + 1)
                        sp.dma_start(rowtile(h2_d, t), t_out[:, j, :]).then_inc(L3[f"out{j}"], 16)

                def l3(ts, later):
                    for j, t in enumerate(later):
                        sp.wait_ge(L3["h"], t - 1)
                        sp.dma_start(t_col[:, j, :, :].rearrange("p k n -> p (k n)"), rowtile(xt_d, t)).then_inc(L3[f"in{j}"], 16)
                    store_h2(ts)
                ahead(sp, lambda ts: None, l3)
                for j in range(2):
                    sp.wait_ge(L3[f"out{j}"], 16 * (NT // 2 + 1 - j))

            @block.gpsimd
            def _(pool):
                list_rows = edge_list.rearrange("(n a) -> n a", a=1)
                half_turn = [S["word0"], S["word1"]]

                def scatter(it):
                    for h in range(2):
                        c = it * (2 * RING) + h * RING
                        wait_past(pool, half_turn[h], it * (16 * RING))
                        pool.sem_inc(S["scatter_turn"], 1)
                        pool.tensor_copy(ring_addr[e, h, :], addr[e, ds(c, RING)]).then_inc(S["scatter_copied"], 1)
                        pool.tensor_copy(ring_word[e, h, :], word[e, ds(c, RING)]).then_inc(S["scatter_copied"], 1)
                        pool.wait_ge(S["scatter_copied"], it * 4 + h * 2 + 2)
                        pool.sem_inc(S["scatter_turn"], 1)
                        for i in range(RING):
                            pool.indirect_dma_start(
                                list_rows, bass.IndirectOffsetOnAxis(ap=ring_addr[e, h, i:i + 1].bitcast(U32), axis=0),
                                ring_word[e, h, i:i + 1], None).then_inc(half_turn[h], 16)
                scatter(0)
                with pool.Fori(1, TURNS // 2) as it:
                    scatter(it)
                for h in range(2):
                    pool.wait_ge(half_turn[h], 16 * RING * (TURNS // 2))

            @block.scalar
            def _(act):
                def root(R):
                    act.wait_ge(R["ready"], 1)
                    act.activation(var[:, :], var[:, :], ACT.Sqrt).then_inc(R["rooted"], 1)

                root({"ready": S["var_ready"], "rooted": S["var_rooted"]})
                act.sem_inc(L1["vdone"], 2)

                def l1_turned(ts):
                    for j, t in enumerate(ts):
                        act.wait_ge(L1["xt"], t + 1)
                        wait_past(act, L1[f"stored{j}"], (t - j) * 8)
                        act.copy(t_col[:, j, :, :].rearrange("p k n -> p (k n)"), bank[j][:, 0:C]).then_inc(L1["xtc"], 1)

                def l1(ts, later):
                    for j, t in enumerate(ts):
                        act.wait_ge(L1["kmin"], t + 1)
                        act.activation(t_exp[:, j, :], t_exp[:, j, :], ACT.Exp).then_inc(L1["kexp"], 1)
                        act.wait_ge(L1["v"], t + 1)
                        act.wait_ge(L1["sum"], t + 1)
                        act.copy(t_v[:, j, :, 0:P], bank[4 + j][:, 0:C].rearrange("p (k n) -> p k n", k=CK)).then_inc(L1["vdone"], 1)
                    l1_turned(later)
                ahead(act, l1_turned, l1)

                def l2_exp(ts):
                    for j, t in enumerate(ts):
                        act.wait_ge(L2["qmin"], t + 1)
                        act.activation(t_exp[:, j, :], t_exp[:, j, :], ACT.Exp).then_inc(L2["qexp"], 1)

                def l2(ts, later):
                    l2_exp(later)
                    for j, t in enumerate(ts):
                        act.wait_ge(L2["mt"], t + 1)
                        act.copy(t_mt[:, j, :, :].rearrange("p k n -> p (k n)"), bank[4 + j][:, 0:C]).then_inc(L2["mtc"], 1)
                    for j, t in enumerate(ts):
                        act.wait_ge(L2["m"], t + 1)
                        act.sem_inc(S["act_turn"], 1)
                        act.copy(flat_b(t), bank[4 + j][:, C:2 * C]).then_inc(L2["kept"], 1)
                act.sem_inc(L2["kept"], 2)
                ahead(act, l2_exp, l2)
                root(R1)

                def l3_normed(ts):
                    for j, t in enumerate(ts):
                        act.wait_ge(L3["nt"], t + 1)
                        for k in range(CK):
                            act.activation(t_mt[:, j, k, :], bank[j][:, k * P:(k + 1) * P], ACT.Identity,
                                           scale=g1c[:, k:k + 1], bias=b1c[:, k:k + 1]).then_inc(L3["ntc"], 1)

                def l3(ts, later):
                    for j, t in enumerate(ts):
                        act.wait_ge(L3["h"], t + 1)
                        act.activation(t_hid[:, j, :, :].rearrange("p k n -> p (k n)"), bank[2 + j][:, :], ACT.Relu).then_inc(L3["hc"], 1)
                    l3_normed(later)
                    for j, t in enumerate(ts):
                        act.wait_ge(L3["o"], t + 1)
                        act.wait_ge(L3["stat"], t + 1)
                        wait_past(act, L3[f"out{j}"], (t - j) * 8)
                        act.copy(t_out[:, j, :], bank[4 + j][:, 0:C]).then_inc(L3["kept"], 1)
                ahead(act, l3_normed, l3)
                root(R2)
                act.wait_ge(S["root_in"], 1)
                act.activation(half[:, :], half[:, :], ACT.Sqrt).then_inc(S["root_done"], 1)

            @block.vector
            def _(dve):
                ch = Chain(dve, S["dsteps"])
                s = ch.step
                s(dve.memset(zeros[:, :], 0.0))
                s(dve.memset(kv_bd[:, :, :], 0.0))
                with dve.Fori(0, NT) as t:
                    dve.bn_stats(stats[:, ds(t, 1), :].rearrange("p a n -> p (a n)"), flat_a(t)).then_inc(L1["stat"], 1)
                dve.wait_ge(L1["stat"], NT)
                norm_stats(dve, s, stats, mean[:, :], var[:, :], rstd[:, :], S["var_ready"], S["var_rooted"])
                dve.wait_ge(S["wts_in"], 16 * 9)
                for k in range(CK):
                    r = slice(C + k * P, C + (k + 1) * P)
                    s(dve.tensor_tensor(wkg[:, k, r], wkg[:, k, r], ident[:, :], ALU.add))
                dve.sem_inc(L1["fold"], 1)
                dve.sem_inc(L1["base"], 2)

                def l1_norm(ts):
                    for j, t in enumerate(ts):
                        wait_past(dve, L1["xt"], t - 1)
                        dve.tensor_scalar(t_row[:, j, :], flat_a(t), col(mean, t), col(rstd, t), ALU.subtract,
                                          ALU.mult).then_inc(L1["norm"], 1)

                def l1(ts, later):
                    l1_norm(later)
                    for j, t in enumerate(ts):
                        dve.wait_ge(L1["kg"], t + 1)
                        dve.tensor_scalar(t_exp[:, j, :], bank[2 + j][:, 0:C], 0.0, None, ALU.min).then_inc(L1["kmin"], 1)
                        wait_past(dve, L1[f"out{j}"], (t - j) * 8)
                        dve.tensor_tensor(t_out[:, j, :], flat_a(t), bank[2 + j][:, C:2 * C], ALU.add).then_inc(L1["base"], 1)
                        dve.wait_ge(L1["sum"], t + 1)
                        dve.tensor_scalar(t_v[:, j, :, P:P + 1], valid[:, ds(t, 1)].unsqueeze(1).to_broadcast([P, CK, 1]), 1.0, None,
                                          ALU.mult).then_inc(L1["kdone"], 1)
                        dve.wait_ge(L1["kexp"], t + 1)
                        dve.scalar_tensor_tensor(t_k[:, j, :], bank[2 + j][:, 0:C], 0.0, t_exp[:, j, :], ALU.max,
                                                 ALU.add).then_inc(L1["kdone"], 1)
                    for j, t in enumerate(ts):
                        dve.wait_ge(L1["base"], t + 3)
                        dve.tensor_scalar(flat_a(t), flat_a(t), col(mean, t), col(rstd, t), ALU.subtract,
                                          ALU.mult).then_inc(L1["kept"], 1)
                ahead(dve, l1_norm, l1)
                dve.wait_ge(L1["kept"], NT)

                dve.wait_ge(L1["sum"], NT + 3)
                for m in range(CK):
                    for h in range(HH):
                        r = slice(h * HD, (h + 1) * HD)
                        o = m * (P + 1)
                        s(dve.tensor_copy(kv_bd[r, m, r], bank[6][r, o + h * HD:o + (h + 1) * HD]))
                        s(dve.tensor_copy(kv_bd[r, m, P + h:P + h + 1], bank[6][r, o + P:o + P + 1]))
                dve.sem_inc(L2["den"], 1)

                def l2_q(ts):
                    for j, t in enumerate(ts):
                        dve.wait_ge(L2["q"], t + 1)
                        dve.tensor_scalar(t_exp[:, j, :], bank[j][:, 0:C], 0.0, None, ALU.min).then_inc(L2["qmin"], 1)
                    for j, t in enumerate(ts):
                        dve.wait_ge(L2["qexp"], t + 1)
                        dve.scalar_tensor_tensor(t_k[:, j, :], bank[j][:, 0:C], 0.0, t_exp[:, j, :], ALU.max,
                                                 ALU.add).then_inc(L2["qdone"], 1)

                def l2(ts, later):
                    for j, t in enumerate(ts):
                        dve.wait_ge(L2["att"], t + 1)
                        att = bank[2 + j][:, 0:CK * (P + HH)].rearrange("p (k n) -> p k n", k=CK)
                        den = t_den[:, j, 0, :].rearrange("p (k h) -> p k h", k=CK)
                        z = t_den[:, j, 1, :]
                        dve.tensor_scalar(den, att[:, :, P:P + HH], ATT_EPS, None, ALU.add).then_inc(L2["z"], 1)
                        dve.wait_ge(L2["z"], t * 2 + 1)
                        dve.reciprocal(z, t_den[:, j, 0, :]).then_inc(L2["z"], 1)
                        dve.wait_ge(L2["z"], t * 2 + 2)
                        for k in range(CK):
                            zb = t_den[:, j, 1, k * HH:(k + 1) * HH].unsqueeze(2).to_broadcast([P, HH, HD])
                            dve.tensor_tensor(t_row[:, j, k * P:(k + 1) * P].rearrange("p (h d) -> p h d", d=HD),
                                              att[:, k, 0:P].rearrange("p (h d) -> p h d", d=HD), zb, ALU.mult).then_inc(L2["msg"], 1)
                    l2_q(later)
                    for j, t in enumerate(ts):
                        dve.wait_ge(L2["kept"], t + 3)
                        dve.sem_inc(S["dve_turn"], 1)
                        dve.bn_stats(flat(stats[:, ds(t, 1), :]), flat_b(t)).then_inc(L2["stat"], 1)
                ahead(dve, l2_q, l2)
                dve.wait_ge(L2["stat"], NT)
                norm_stats(dve, s, stats, mean[:, :], var[:, :], rstd[:, :], R1["ready"], R1["rooted"])
                dve.wait_ge(L2["m"], NT)

                def l3_norm(ts):
                    for j, t in enumerate(ts):
                        wait_past(dve, L3["nt"], t - 1)
                        dve.tensor_scalar(t_row[:, j, :], flat_b(t), col(mean, t), col(rstd, t), ALU.subtract,
                                          ALU.mult).then_inc(L3["norm"], 1)

                def hot(t):
                    for h in range(2):
                        c = t * (2 * GB) + h * GB
                        dve.wait_ge(S["hot_used"], t * 2 + (h + 1))
                        dve.tensor_tensor(hot_loc[e, h, :, :], loc_f[e, ds(c, GB)].unsqueeze(2).to_broadcast([EP, GB, P]),
                                          iota[e, 0:P].unsqueeze(1).to_broadcast([EP, GB, P]), ALU.is_equal).then_inc(S["hot_made"], 1)
                        for a, key in enumerate((tile_f, self_f)):
                            dve.tensor_tensor(hot_tile[e, h, :, a, :], key[e, ds(c, GB)].unsqueeze(2).to_broadcast([EP, GB, NT]),
                                              iota[e, 0:NT].unsqueeze(1).to_broadcast([EP, GB, NT]), ALU.is_equal).then_inc(S["hot_made"], 1)

                def l3_stats(ts):
                    for j, t in enumerate(ts):
                        dve.wait_ge(L3["kept"], t + 1)
                        dve.sem_inc(S["dve_turn"], 1)
                        dve.bn_stats(flat(stats[:, ds(t, 1), :]), t_out[:, j, :]).then_inc(L3["stat"], 1)

                def l3(ts, later):
                    l3_norm(later)
                    for t in ts:
                        hot(t)
                    l3_stats(pair_before(ts))
                dve.sem_inc(L3["stat"], 2)
                dve.sem_inc(S["hot_used"], 2)
                ahead(dve, l3_norm, l3)
                l3_stats([NT - 1])
                hot(NT)
                dve.wait_ge(L3["stat"], NT + 2)
                norm_stats(dve, s, stats, mean[:, :], var[:, :], rstd[:, :], R2["ready"], R2["rooted"])
                dve.wait_ge(S["deg_done"], 1)
                s(dve.tensor_copy(degs[:, :, :], bank[7][:, 0:2 * NT].rearrange("p (a b) -> p a b", a=2)))
                s(dve.tensor_scalar(half[:, :], degs[:, 0, :], 1.0, None, ALU.add))
                dve.sem_inc(S["root_in"], 1)
                dve.wait_ge(S["root_done"], 1)
                s(dve.reciprocal(dinv[:, :], half[:, :]))
                s(dve.tensor_scalar(half[:, :], half[:, :], 0.5, None, ALU.mult))
                s(dve.tensor_tensor(diag[:, :], dinv[:, :], dinv[:, :], ALU.mult))
                s(dve.tensor_tensor(diag[:, :], degs[:, 1, :], diag[:, :], ALU.subtract))
                s(dve.tensor_scalar(diag[:, :], diag[:, :], 1.0, None, ALU.add))
                s(dve.scalar_tensor_tensor(own[:, :], half[:, :], -2.0, diag[:, :], ALU.mult, ALU.mult))
                s(dve.tensor_scalar(ndinv[:, 0, :], dinv[:, :], -1.0, None, ALU.mult))
                s(dve.tensor_scalar(ndinv[:, 1, :], dinv[:, :], -2.0, None, ALU.mult))
                for i in range(2):
                    s(dve.tensor_tensor(udinv[:, i, :], ndinv[:, i, :], dinv[:, :], ALU.mult))

            @block.tensor
            def _(pe):
                pe.wait_ge(L1["fold"], 1)
                kv = bank[6][:, 0:CK * (P + 1)]
                pe.matmul(kv, zeros[:, :], wkg[:, 0, 0:CK * (P + 1)], start=True, stop=False)
                pe.sem_inc(L1["sum"], 2)

                def turn(src, dst, j):
                    for k in range(CK):
                        ins = pe.transpose(dst[:, k * P:(k + 1) * P], src[:, j, k * P:(k + 1) * P], ident[:, :])
                    return ins

                def times(out, lhs, rhs, n, start=True, stop=True):
                    for k in range(n):
                        ins = pe.matmul(out, lhs(k), rhs(k), start=start and k == 0, stop=stop and k == n - 1)
                    return ins

                def l1_turn(ts):
                    for j, t in enumerate(ts):
                        pe.wait_ge(L1["norm"], t + 1)
                        turn(t_row, bank[j], j).then_inc(L1["xt"], 1)

                def l1(ts, later):
                    for j, t in enumerate(ts):
                        pe.wait_ge(L1["xtc"], t + 1)
                        pe.wait_ge(L1["base"], t + 1)
                        pe.wait_ge(L1["kdone"], t * 2 + 2)
                        times(bank[2 + j][:, :], lambda k: t_col[:, j, k, :], lambda k: wkg[:, k, :], CK).then_inc(L1["kg"], 1)
                        pe.wait_ge(L1["vdone"], t + 1)
                        times(bank[4 + j][:, 0:C], lambda k: t_col[:, j, k, :], lambda k: wv[:, k, :], CK).then_inc(L1["v"], 1)
                    l1_turn(later)
                    for j, t in enumerate(ts):
                        pe.wait_ge(L1["kdone"], t * 2 + 4)
                        pe.wait_ge(L1["vdone"], t + 3)
                        for m in range(CK):
                            ins = pe.matmul(kv[:, m * (P + 1):(m + 1) * (P + 1)], t_k[:, j, m * P:(m + 1) * P], t_v[:, j, m, :],
                                            start=False, stop=False, skip_group_check=True)
                        ins.then_inc(L1["sum"], 1)
                pe.sem_inc(L1["kdone"], 2)
                ahead(pe, l1_turn, l1)
                pe.matmul(kv, zeros[:, :], wkg[:, 0, 0:CK * (P + 1)], start=False, stop=True).then_inc(L1["sum"], 1)
                pe.wait_ge(L2["den"], 1)

                def l2_q(ts):
                    for j, t in enumerate(ts):
                        pe.wait_ge(L2[f"in{j}"], (t - j) * 8 + 16)
                        for m in range(CK):
                            ins = times(bank[j][:, m * P:(m + 1) * P], lambda k: wq[:, k, m * P:(m + 1) * P],
                                        lambda k: t_col[:, j, k, :], CK)
                        ins.then_inc(L2["q"], 1)

                def l2(ts, later):
                    for j, t in enumerate(ts):
                        pe.wait_ge(L2["qdone"], t + 1)
                        for m in range(CK):
                            ins = pe.matmul(bank[2 + j][:, m * (P + HH):(m + 1) * (P + HH)], t_k[:, j, m * P:(m + 1) * P],
                                            kv_bd[:, m, :], start=True, stop=True)
                        ins.then_inc(L2["att"], 1)
                    l2_q(later)
                    for j, t in enumerate(ts):
                        pe.wait_ge(L2["kept"], t + 1)
                        pe.wait_ge(L2["msg"], t * 2 + 2)
                        turn(t_row, bank[4 + j], j).then_inc(L2["mt"], 1)
                    for j, t in enumerate(ts):
                        pe.wait_ge(L2["mtc"], t + 1)
                        times(bank[4 + j][:, C:2 * C], lambda k: t_mt[:, j, k, :], lambda k: wm[:, k, :], CK).then_inc(L2["m"], 1)
                ahead(pe, l2_q, l2)

                d = bank[7][:, 0:2 * NT]
                pe.matmul(d, zeros[:, :], ones[:, 0:2 * NT], start=True, stop=False)

                def degrees(t):
                    for h in range(2):
                        pe.wait_ge(S["hot_made"], t * 6 + (h + 1) * 3)
                        for i in range(GB):
                            ins = pe.matmul(d, hot_loc[e, h, i, :], hot_tile[e, h, i, :, :].rearrange("p a b -> p (a b)"),
                                            start=False, stop=False, skip_group_check=True)
                        ins.then_inc(S["hot_used"], 1)

                def l3_turn(ts):
                    for j, t in enumerate(ts):
                        pe.wait_ge(L3["norm"], t + 1)
                        turn(t_row, bank[j], j).then_inc(L3["nt"], 1)

                def l3(ts, later):
                    for j, t in enumerate(ts):
                        pe.wait_ge(L3[f"in{j}"], (t - j) * 8 + 16)
                        pe.wait_ge(L3["ntc"], t * 2 + 2)
                        for m in range(FK):
                            ins = times(bank[2 + j][:, m * P:(m + 1) * P], lambda k: w1[:, k, m * P:(m + 1) * P],
                                        lambda k: t_col[:, j, k, :] if k < CK else t_mt[:, j, k - CK, :], 2 * CK)
                        ins.then_inc(L3["h"], 1)
                        if j == 0:
                            degrees(t)
                    l3_turn(later)
                    for j, t in enumerate(ts):
                        pe.wait_ge(L3["hc"], t + 1)
                        wait_past(pe, L3["kept"], t - 1)
                        times(bank[4 + j][:, 0:C], lambda k: t_hid[:, j, k, :], lambda k: w2[:, k, :], FK).then_inc(L3["o"], 1)
                        if j == 0 and len(ts) > 1:
                            degrees(ts[1])
                ahead(pe, l3_turn, l3)
                degrees(NT)
                pe.matmul(d, zeros[:, :], ones[:, 0:2 * NT], start=False, stop=True).then_inc(S["deg_done"], 1)


def cheb_block(nc, outer, alloc, v, k):
    iota, ident, cols, locs, chunk_tile, dinv, half, own, ndinv, udinv, rows_a, rows_b, bank, edge_list, u_d = (
        v[n] for n in ("iota", "ident", "cols", "locs", "chunk_tile", "dinv", "half", "own", "ndinv", "udinv", "rows_a",
                       "rows_b", "bank", "edge_list", "u_d"))
    mean, rstd, h2_d = v["mean"], v["rstd"], v["h2_d"]
    cur, acc = (rows_a, rows_b) if k % 2 == 0 else (rows_b, rows_a)
    base_in, base_out = (v["base2_d"], v["base_d"]) if k == 1 else (v["base_d"], v["base2_d"])
    G = 8
    HALVES = NCH // G
    with ExitStack() as ctx:
        sb, sem_ = alloc(ctx, f"cheb{k}_")
        sem = lambda n: sem_(f"c{k}_{n}")
        list_i = sb("list_i", [P, NCH], I32) if k == 0 else None
        part_i = sb("part_i", [P, NCH], I32) if k == 0 else None
        ring_idx = sb("ring_idx", [P, 2, G], U32)
        rows = sb("rows", [P, 2, G, C])
        hot = sb("hot", [P, 2, G, P])
        wt = sb("wt", [P, CK, C])
        t_row = sb("t_row", [P, C])
        t_col = sb("t_col", [P, CK, P])
        t_base = sb("t_base", [P, 2, C])
        t_h2 = sb("t_h2", [P, C]) if k == 0 else None
        t_n = sb("t_n", [P, 2, C]) if k == 0 else None
        gain = sb("gain", [P, C]) if k == 0 else None
        bias = sb("bias", [P, 2, C]) if k == 0 else None
        S = {n: sem(n) for n in ("listed ready gathered0 gathered1 copied pool_turn hot_made scattered added "
                                 "copied_row turned turned_col times base_in base_made base_out w_in act_turn "
                                 "u_made u_out0 u_out1 halved scaled begun n0 n1 n2 n3 steps").split()}
        rowtile = lambda d, t: d.rearrange("(t p) c -> t p c", p=P)[ds(t, 1)].rearrange("a p c -> (a p) c")
        tile_of = lambda rows_, t: flat(rows_[:, ds(t, 1), :])
        tiles = NT
        al = 0 if k == 1 else 1
        GU = 7
        assert NT % GU == 0 and GU <= G

        def turns(eng, body):
            with eng.Fori(0, tiles) as it:
                body(it, True)
            with eng.Fori(tiles, HALVES // 2) as it:
                body(it, False)

        with nc.Block() as block:
            @block.sync
            def _(sp):
                if k == 0:
                    sp.dma_start(list_i[:, :], edge_list.rearrange("(p c) -> p c", p=P)).then_inc(S["listed"], 16)
                    w = S["w_in"]
                    sp.dma_start(gain[:, :], v["g2"].rearrange("(a n) -> a n", a=1).to_broadcast([P, C])).then_inc(w, 16)
                    sp.dma_start(bias[:, 0, :], v["gnn_b"].rearrange("(a n) -> a n", a=1).to_broadcast([P, C])).then_inc(w, 16)
                    sp.dma_start(bias[:, 1, :], v["b2"].rearrange("(a n) -> a n", a=1).to_broadcast([P, C])).then_inc(w, 16)
                else:
                    sp.dma_start(wt[:, :, :], v["gnn_w"][k].rearrange("(k p) n -> p k n", p=P)).then_inc(S["w_in"], 16)

                def store_u(gs):
                    for j, g in enumerate(gs):
                        sp.wait_ge(S["u_made"], g * GU + GU)
                        dst = u_d[k].rearrange("(g t p) c -> p g t c", p=P, t=GU)[:, ds(g, 1)].rearrange("p a t c -> p (a t) c")
                        sp.dma_start(dst, rows[:, j, 0:GU, :]).then_inc(S[f"u_out{j}"], 16)
                pairs(sp, store_u, NT // GU)

                def load(t):
                    sp.dma_start(t_base[:, 0, :], rowtile(base_in, t)).then_inc(S["base_in"], 16)
                    if k == 0:
                        sp.dma_start(t_h2[:, :], rowtile(h2_d, t)).then_inc(S["base_in"], 16)
                load(0)

                def store_sum(t):
                    sp.wait_ge(S["base_made"], t + 2)
                    sp.dma_start(rowtile(base_out, t), t_base[:, 1, :]).then_inc(S["base_out"], 16)
                    sp.wait_ge(S["base_out"], t * 16 + 16)
                with sp.Fori(0, tiles - 1) as t:
                    store_sum(t)
                    load(t + 1)
                store_sum(tiles - 1)

            @block.gpsimd
            def _(pool):
                for j in range(2):
                    pool.wait_ge(S[f"u_out{j}"], 16 * (NT // GU // 2 + 1 - j))
                pool.wait_ge(S["ready"], 1)
                pool.sem_inc(S["scattered"], 2 * G)

                def turn(it, _):
                    for h in range(2):
                        n = it * 2 + h
                        pool.wait_ge(S["scattered"], (n + 1) * G)
                        pool.sem_inc(S["pool_turn"], 1)
                        pool.tensor_copy(ring_idx[:, h, :], cols[:, ds(n * G, G)]).then_inc(S["copied"], 1)
                        pool.wait_ge(S["copied"], n + 1)
                        pool.sem_inc(S["pool_turn"], 1)
                        for i in range(G):
                            pool.indirect_dma_start(rows[:, h, i, :], None, u_d[k],
                                                    bass.IndirectOffsetOnAxis(ap=ring_idx[:, h, i:i + 1], axis=0)
                                                    ).then_inc(S[f"gathered{h}"], 16)
                turns(pool, turn)

            @block.scalar
            def _(act):
                def make_u(gs):
                    for j, g in enumerate(gs):
                        wait_past(act, S[f"u_out{j}"], (g - j) * 8)
                        act.sem_inc(S["act_turn"], 1)
                        for i in range(GU):
                            t = g * GU + i
                            f = dinv[:, ds(t, 1)] if k == 0 else udinv[:, al, ds(t, 1)]
                            act.activation(rows[:, j, i, :], tile_of(cur, t), ACT.Copy, scale=f).then_inc(S["u_made"], 1)
                pairs(act, make_u, NT // GU)
                if k:
                    act.wait_ge(S["begun"], NT)
                    with act.Fori(0, tiles) as t:
                        act.wait_ge(S["turned"], t + 1)
                        act.sem_inc(S["act_turn"], 1)
                        act.copy(t_row[:, :], tile_of(cur, t)).then_inc(S["copied_row"], 1)
                        act.wait_ge(S["turned"], t + 2)
                        act.copy(t_col[:, :, :].rearrange("p k n -> p (k n)"), bank[4][:, 0:C]).then_inc(S["turned_col"], 1)

            @block.vector
            def _(dve):
                s = Chain(dve, S["steps"]).step
                if k == 0:
                    dve.wait_ge(S["listed"], 16)
                    s(dve.tensor_scalar(part_i[:, :], list_i[:, :], (1 << LOC_SHIFT) - 1, None, ALU.bitwise_and))
                    s(dve.tensor_copy(cols[:, :], part_i[:, :]))
                    s(dve.tensor_scalar(part_i[:, :], list_i[:, :], LOC_SHIFT, None, ALU.arith_shift_right))
                    s(dve.tensor_copy(locs[:, :], part_i[:, :]))
                dve.sem_inc(S["ready"], 1)
                if k == 0:
                    dve.wait_ge(S["w_in"], 48)
                    s(dve.tensor_tensor(bias[:, 0, :], bias[:, 0, :], bias[:, 1, :], ALU.add))

                def begin(ts):
                    for j, t in enumerate(ts):
                        if k:
                            dve.tensor_scalar(tile_of(acc, t), tile_of(acc, t), half[:, ds(t, 1)], None, ALU.mult).then_inc(S["halved"], 1)
                            dve.wait_ge(S["u_made"], t + 1)
                            dve.tensor_scalar(tile_of(cur, t), tile_of(cur, t), ndinv[:, al, ds(t, 1)], None, ALU.mult).then_inc(S["scaled"], 1)
                    for j, t in enumerate(ts):
                        own_t = own[:, ds(t, 1)]
                        if k:
                            dve.wait_ge(S["halved"], t + 1)
                            dve.wait_ge(S["scaled"], t + 1)
                            dve.scalar_tensor_tensor(tile_of(acc, t), tile_of(cur, t), own_t, tile_of(acc, t), ALU.mult,
                                                     ALU.add).then_inc(S["begun"], 1)
                        else:
                            dve.tensor_scalar(tile_of(acc, t), tile_of(cur, t), own_t, None, ALU.mult).then_inc(S["begun"], 1)
                pairs(dve, begin)
                dve.wait_ge(S["begun"], NT)

                def tile_sum(t):
                    if k:
                        dve.wait_ge(S["base_in"], t * 16 + 16)
                        dve.wait_ge(S["times"], t + 1)
                        dve.tensor_tensor(t_base[:, 1, :], t_base[:, 0, :], bank[5][:, 0:C], ALU.add).then_inc(S["base_made"], 1)
                        return
                    dve.wait_ge(S["base_in"], t * 32 + 32)
                    dve.tensor_scalar(t_n[:, 0, :], t_h2[:, :], mean[:, ds(t, 1)], rstd[:, ds(t, 1)], ALU.subtract,
                                      ALU.mult).then_inc(S["n0"], 1)
                    dve.tensor_tensor(t_base[:, 0, :], t_base[:, 0, :], bias[:, 0, :], ALU.add).then_inc(S["n1"], 1)
                    dve.wait_ge(S["n0"], t + 1)
                    dve.tensor_tensor(t_n[:, 1, :], t_n[:, 0, :], gain[:, :], ALU.mult).then_inc(S["n2"], 1)
                    dve.wait_ge(S["n1"], t + 1)
                    dve.wait_ge(S["n2"], t + 1)
                    dve.tensor_tensor(t_base[:, 1, :], t_base[:, 0, :], t_n[:, 1, :], ALU.add).then_inc(S["base_made"], 1)
                    dve.wait_ge(S["base_made"], t + 2)

                def turn(it, with_tile):
                    for h in range(2):
                        n = it * 2 + h
                        dve.wait_ge(S["scattered"], (n + 1) * G)
                        dve.tensor_tensor(hot[:, h, :, :], locs[:, ds(n * G, G)].unsqueeze(2).to_broadcast([P, G, P]),
                                          iota[:, 0:P].unsqueeze(1).to_broadcast([P, G, P]), ALU.is_equal).then_inc(S["hot_made"], 1)
                    if with_tile:
                        tile_sum(it)
                    for h in range(2):
                        n = it * 2 + h
                        _, regs = nc.values_load_multi_w_load_instructions(
                            chunk_tile[0:1, ds(n * G, G)], engines=[mybir.EngineType.DVE], min_val=0, max_val=NT - 1)
                        for i in range(G):
                            if i % 2 == 0:
                                dve.wait_ge(S["scattered"], n * G + 2 * G + i + 2)
                            dve.wait_ge(S["added"], n * G + 8 + i)
                            a = tile_of(acc, regs[i])
                            dve.tensor_tensor(a, a, bank[i // 2][:, (i % 2) * C:(i % 2 + 1) * C], ALU.add).then_inc(S["added"], 1)
                turns(dve, turn)
                dve.wait_ge(S["added"], NCH + 8)

            @block.tensor
            def _(pe):
                pe.sem_inc(S["added"], 8)
                pe.sem_inc(S["base_made"], 1)
                if k:
                    pe.wait_ge(S["w_in"], 16)
                    pe.sem_inc(S["turned"], 1)

                def turn(it, with_tile):
                    if with_tile and k:
                        pe.wait_ge(S["copied_row"], it + 1)
                        for c in range(CK):
                            ins = pe.transpose(bank[4][:, c * P:(c + 1) * P], t_row[:, c * P:(c + 1) * P], ident[:, :])
                        ins.then_inc(S["turned"], 1)
                        pe.wait_ge(S["turned_col"], it + 1)
                        pe.wait_ge(S["base_made"], it + 1)
                        for c in range(CK):
                            ins = pe.matmul(bank[5][:, 0:C], t_col[:, c, :], wt[:, c, :], start=c == 0, stop=c == CK - 1)
                        ins.then_inc(S["times"], 1)
                    for h in range(2):
                        n = it * 2 + h
                        pe.wait_ge(S["hot_made"], n + 1)
                        pe.wait_ge(S[f"gathered{h}"], it * (16 * G) + 16 * G)
                        for i in range(G):
                            if i % 2 == 0:
                                pe.wait_ge(S["added"], n * G + i + 2)
                            pe.matmul(bank[i // 2][:, (i % 2) * C:(i % 2 + 1) * C], hot[:, h, i, :], rows[:, h, i, :],
                                      start=True, stop=True).then_inc(S["scattered"], 1)
                turns(pe, turn)


def gate_block(nc, outer, alloc, v):
    iota, ones, ident, before, valid, rows_a, rows_b, bank = (
        v[n] for n in ("iota", "ones", "ident", "before", "valid", "rows_a", "rows_b", "bank"))
    slot_i, gate_w2, tile_expert = v["slot_i"], v["gate_w2"], v["tile_expert"]
    t3, x1 = rows_b, rows_a
    with ExitStack() as ctx:
        sb, sem_ = alloc(ctx, "gate_")
        sem = lambda n: sem_("g_" + n)
        wt = sb("g_wt", [P, CK, C])
        wgate = sb("g_wgate", [P, CK, NE])
        bgate = sb("g_bgate", [1, NE])
        eb2 = sb("g_eb2", [NE, C])
        stats = sb("g_stats", [P, NT, 6])
        mean, var, rstd = v["mean"], v["var"], v["rstd"]
        t_row = sb("g_row", [P, 2, C])
        t_col = sb("g_col", [P, 2, CK, P])
        t_base = sb("g_base", [P, 2, C])
        t_out = sb("g_out", [P, 2, C])
        logit = sb("g_logit", [P, 2, NE])
        top = sb("g_top", [P, 2, 8])
        top_i = sb("g_top_i", [P, 2, 8], U32)
        top_f = sb("g_top_f", [P, 2, 2])
        best = sb("g_best", [P, 2, NT])
        pick = sb("g_pick", [P, 2, NT, NE])
        both = sb("g_both", [P, NT, NE])
        place = sb("g_place", [P, NT, NE])
        tot = sb("g_tot", [P, NT, NE])
        upto = sb("g_upto", [P, NE, NT])
        small = sb("g_small", [P, 5, NE])
        small_i = sb("g_small_i", [P, NE], I32)
        first_t = sb("g_first_t", [NE, 1])
        tab = sb("g_tab", [NE, MT])
        dump_i = sb("g_dump_i", [P, 1], I32)
        dump = sb("g_dump", [P, 1])
        inval = sb("g_inval", [P, NT])
        slot = sb("g_slot", [P, 2, NT])
        tmp = sb("g_tmp", [P, NT, NE])
        w_row = sb("g_wrow", [P, 2, NE])
        w_col = sb("g_wcol", [NE, 2, P])
        ring = sb("g_ring", [P, 2, C])
        ring_i = sb("g_ring_i", [P, 2, 2], I32)
        S = {n: sem(n) for n in (
            "wts base_in0 base_in1 copied turned turned_col times x1 stat steps var_ready rooted act_turn dve_turn "
            "normed nt ntc lg lgc mx mi mf pk best x1_out all ready exp_in exp_done wsum placed slots_ready pool_turn "
            "pool_copied scattered0 scattered1 wr wt wtc b2 out0 out1 outm dump kept first ind tabs x1loop").split()}
        rowtile = lambda d, t: d.rearrange("(t p) c -> t p c", p=P)[ds(t, 1)].rearrange("a p c -> (a p) c")
        tile_of = lambda rows_, t: flat(rows_[:, ds(t, 1), :])
        E2 = NT * NE // 2

        with nc.Block() as block:
            @block.sync
            def _(sp):
                kpc = lambda a: a.rearrange("(k p) n -> p k n", p=P)
                sp.dma_start(wt[:, :, :], kpc(v["gnn_w"][3])).then_inc(S["wts"], 16)
                sp.dma_start(wgate[:, :, :], kpc(v["gate_w"])).then_inc(S["wts"], 16)
                sp.dma_start(bgate[:, :], v["gate_b"].rearrange("(a n) -> a n", a=1)).then_inc(S["wts"], 16)
                sp.dma_start(eb2[:, :], v["eb2"]).then_inc(S["wts"], 16)
                sp.sem_inc(S["x1"], 2)

                def g1(ts):
                    for j, t in enumerate(ts):
                        sp.wait_ge(S["x1"], t + 1)
                        sp.dma_start(t_base[:, j, :], rowtile(v["base2_d"], t)).then_inc(S[f"base_in{j}"], 16)
                pairs(sp, g1)
                sp.wait_ge(S["x1"], NT + 2)
                sp.dma_start(v["x1_d"].rearrange("(t p) c -> p t c", p=P), x1[:, :, :]).then_inc(S["x1_out"], 16)

                def g3(ts):
                    for j, t in enumerate(ts):
                        sp.wait_ge(S["outm"], t + 1)
                        sp.dma_start(rowtile(v["xg_d"], t), t_out[:, j, :]).then_inc(S[f"out{j}"], 16)
                pairs(sp, g3)
                for j in range(2):
                    sp.wait_ge(S[f"out{j}"], 16 * (NT // 2 + 1 - j))
                sp.wait_ge(S["x1_out"], 16)

            @block.gpsimd
            def _(pool):
                pool.iota(dump_i[:, :], pattern=[[0, 1]], base=MT * P, channel_multiplier=1).then_inc(S["dump"], 1)
                pool.wait_ge(S["slots_ready"], 1)
                slots = v["slots_in"]

                def scatter(ts):
                    for j, t in enumerate(ts):
                        wait_past(pool, S[f"scattered{j}"], (t - j) * 16)
                        pool.sem_inc(S["pool_turn"], 1)
                        pool.tensor_copy(ring[:, j, :], tile_of(rows_b, t)).then_inc(S["pool_copied"], 1)
                        for a in range(2):
                            pool.tensor_copy(ring_i[:, j, a:a + 1], slot_i[:, a, ds(t, 1)]).then_inc(S["pool_copied"], 1)
                    for j, t in enumerate(ts):
                        pool.wait_ge(S["pool_copied"], t * 3 + 3)
                        pool.sem_inc(S["pool_turn"], 1)
                        for a in range(2):
                            pool.indirect_dma_start(
                                slots, bass.IndirectOffsetOnAxis(ap=ring_i[:, j, a:a + 1].bitcast(U32), axis=0),
                                ring[:, j, :], None).then_inc(S[f"scattered{j}"], 16)
                pairs(pool, scatter)
                for j in range(2):
                    pool.wait_ge(S[f"scattered{j}"], 32 * (NT // 2 + 1 - j))

            @block.scalar
            def _(act):
                def g1(ts):
                    for j, t in enumerate(ts):
                        act.wait_ge(S["turned"], t + 1)
                        act.sem_inc(S["act_turn"], 1)
                        act.activation(t_row[:, j, :], tile_of(t3, t), ACT.Copy, scale=v["ndinv"][:, 1, ds(t, 1)]).then_inc(S["copied"], 1)
                    for j, t in enumerate(ts):
                        act.wait_ge(S["turned"], t + 3)
                        act.copy(t_col[:, j, :, :].rearrange("p k n -> p (k n)"), bank[j][:, 0:C]).then_inc(S["turned_col"], 1)
                pairs(act, g1)
                act.wait_ge(S["var_ready"], 1)
                act.activation(var[:, :], var[:, :], ACT.Sqrt).then_inc(S["rooted"], 1)

                def g2(ts):
                    for j, t in enumerate(ts):
                        act.wait_ge(S["nt"], t + 1)
                        act.copy(t_col[:, j, :, :].rearrange("p k n -> p (k n)"), bank[j][:, 0:C]).then_inc(S["ntc"], 1)
                        act.wait_ge(S["normed"], t + 1)
                        act.sem_inc(S["act_turn"], 1)
                        act.copy(tile_of(rows_b, t), t_row[:, j, :]).then_inc(S["kept"], 1)
                pairs(act, g2)
                act.wait_ge(S["exp_in"], 1)
                act.activation(best[:, 1, :], best[:, 1, :], ACT.Exp).then_inc(S["exp_done"], 1)

                def g3(ts):
                    for j, t in enumerate(ts):
                        act.wait_ge(S["wt"], t + 1)
                        act.copy(w_col[:, j, :], bank[j][0:NE, 0:P]).then_inc(S["wtc"], 1)
                pairs(act, g3)

            @block.vector
            def _(dve):
                s = Chain(dve, S["steps"]).step

                def g1(ts):
                    for j, t in enumerate(ts):
                        dve.wait_ge(S[f"base_in{j}"], (t - j) * 8 + 16)
                        dve.wait_ge(S["times"], t + 1)
                        dve.tensor_tensor(tile_of(x1, t), t_base[:, j, :], bank[2 + j][:, 0:C], ALU.add).then_inc(S["x1"], 1)
                    for j, t in enumerate(ts):
                        dve.wait_ge(S["x1"], t + 3)
                        dve.sem_inc(S["dve_turn"], 1)
                        dve.bn_stats(flat(stats[:, ds(t, 1), :]), tile_of(x1, t)).then_inc(S["stat"], 1)
                pairs(dve, g1)
                dve.wait_ge(S["stat"], NT)
                norm_stats(dve, s, stats, mean[:, :], var[:, :], rstd[:, :], S["var_ready"], S["rooted"])
                dve.wait_ge(S["turned_col"], NT)
                dve.sem_inc(S["kept"], 2)

                def g2(ts):
                    for j, t in enumerate(ts):
                        dve.wait_ge(S["kept"], t + 1)
                        dve.tensor_scalar(t_row[:, j, :], tile_of(x1, t), mean[:, ds(t, 1)], rstd[:, ds(t, 1)], ALU.subtract,
                                          ALU.mult).then_inc(S["normed"], 1)
                    for j, t in enumerate(ts):
                        dve.wait_ge(S["lg"], t + 1)
                        dve.tensor_copy(logit[:, j, :], bank[2 + j][:, 0:NE]).then_inc(S["lgc"], 1)
                    for j, t in enumerate(ts):
                        dve.wait_ge(S["lgc"], t + 1)
                        dve.sem_inc(S["dve_turn"], 1)
                        dve.max(top[:, j, :], logit[:, j, :]).then_inc(S["mx"], 1)
                    for j, t in enumerate(ts):
                        dve.wait_ge(S["mx"], t + 1)
                        dve.sem_inc(S["dve_turn"], 1)
                        dve.max_index(top_i[:, j, :], top[:, j, :], logit[:, j, :]).then_inc(S["mi"], 1)
                        dve.tensor_scalar(best[:, :, ds(t, 1)], top[:, j, 0:2].unsqueeze(2), 1.0, None, ALU.mult).then_inc(S["best"], 1)
                    for j, t in enumerate(ts):
                        dve.wait_ge(S["mi"], t + 1)
                        dve.tensor_copy(top_f[:, j, :], top_i[:, j, 0:2]).then_inc(S["mf"], 1)
                    for j, t in enumerate(ts):
                        dve.wait_ge(S["mf"], t + 1)
                        for a in range(2):
                            dve.tensor_scalar(flat(pick[:, a, ds(t, 1), :]), iota[:, 0:NE], top_f[:, j, a:a + 1], None,
                                              ALU.is_equal).then_inc(S["pk"], 1)
                pairs(dve, g2)
                dve.wait_ge(S["pk"], 2 * NT)
                dve.wait_ge(S["best"], NT)
                dve.wait_ge(S["kept"], NT + 2)
                vb = valid[:, :].unsqueeze(2).to_broadcast([P, NT, NE])
                s(dve.tensor_tensor(both[:, :, :], pick[:, 0, :, :], pick[:, 1, :, :], ALU.add))
                s(dve.tensor_tensor(both[:, :, :], both[:, :, :], vb, ALU.mult))
                dve.sem_inc(S["all"], 1)
                s(dve.tensor_tensor(best[:, 1, :], best[:, 1, :], best[:, 0, :], ALU.subtract))
                dve.sem_inc(S["exp_in"], 1)
                dve.wait_ge(S["exp_done"], 1)
                s(dve.tensor_scalar(best[:, 0, :], best[:, 1, :], 1.0, None, ALU.add))
                s(dve.reciprocal(gate_w2[:, 0, :], best[:, 0, :]))
                s(dve.tensor_tensor(gate_w2[:, 1, :], gate_w2[:, 0, :], best[:, 1, :], ALU.mult))
                dve.wait_ge(S["ready"], 1)
                fl = lambda a: a[:, :, :].rearrange("p t e -> p (t e)")
                for i in range(2):
                    s(dve.tensor_copy(fl(place)[:, i * E2:(i + 1) * E2], bank[i][:, 0:E2]))
                    s(dve.tensor_copy(fl(tot)[:, i * E2:(i + 1) * E2], bank[2 + i][:, 0:E2]))
                for x in range(NE):
                    s(dve.tensor_tensor_scan(upto[:, x, :], ones[:, 0:NT], tot[:, :, x], 0.0, ALU.mult, ALU.add))
                s(dve.tensor_tensor(place[:, :, :], place[:, :, :], upto[:, :, :].rearrange("p e t -> p t e"), ALU.add))
                s(dve.tensor_tensor(place[:, :, :], place[:, :, :], tot[:, :, :], ALU.subtract))
                s(dve.tensor_scalar(small[:, 0, :], upto[:, :, NT - 1], float(P - 1), None, ALU.add))
                s(dve.tensor_copy(small_i[:, :], small[:, 0, :]))
                s(dve.tensor_scalar(small_i[:, :], small_i[:, :], 7, None, ALU.arith_shift_right))
                s(dve.tensor_copy(small[:, 1, :], small_i[:, :]))
                s(dve.tensor_tensor_scan(small[:, 2, :], ones[:, 0:NE], small[:, 1, :], 0.0, ALU.mult, ALU.add))
                s(dve.tensor_tensor(small[:, 3, :], small[:, 2, :], small[:, 1, :], ALU.subtract))
                dve.sem_inc(S["first"], 1)
                s(dve.tensor_scalar(small[:, 4, :], small[:, 3, :], float(P), None, ALU.mult))
                s(dve.tensor_tensor(place[:, :, :], place[:, :, :], small[:, 4, :].unsqueeze(1).to_broadcast([P, NT, NE]), ALU.add))
                dve.wait_ge(S["tabs"], 1)
                s(dve.tensor_copy(first_t[:, :], bank[4][0:NE, 0:1]))
                s(dve.tensor_scalar(tab[:, :], iota[0:NE, 0:MT], first_t[:, 0:1], None, ALU.is_ge))
                dve.sem_inc(S["ind"], 1)
                dve.wait_ge(S["tabs"], 2)
                s(dve.tensor_scalar(tile_expert[0:1, :], bank[5][0:1, 0:MT], -1.0, None, ALU.add))
                dve.wait_ge(S["dump"], 1)
                s(dve.tensor_copy(dump[:, :], dump_i[:, :]))
                s(dve.tensor_scalar(inval[:, :], valid[:, :], -1.0, 1.0, ALU.mult, ALU.add))
                for a in range(2):
                    s(dve.tensor_tensor(tmp[:, :, :], pick[:, a, :, :], place[:, :, :], ALU.mult))
                    s(dve.tensor_reduce(slot[:, a, :], tmp[:, :, :], AX_X, ALU.add))
                    s(dve.tensor_tensor(slot[:, a, :], slot[:, a, :], valid[:, :], ALU.mult))
                    s(dve.scalar_tensor_tensor(slot[:, a, :], inval[:, :], dump[:, 0:1], slot[:, a, :], ALU.mult, ALU.add))
                    s(dve.tensor_scalar(dump[:, :], dump[:, :], -64.0, None, ALU.add))
                    s(dve.tensor_copy(slot_i[:, a, :], slot[:, a, :]))
                dve.sem_inc(S["slots_ready"], 1)
                for a in range(2):
                    s(dve.tensor_tensor(pick[:, a, :, :], pick[:, a, :, :], gate_w2[:, a, :].unsqueeze(2).to_broadcast([P, NT, NE]), ALU.mult))
                s(dve.tensor_tensor(both[:, :, :], pick[:, 0, :, :], pick[:, 1, :, :], ALU.add))

                def g3(ts):
                    for j, t in enumerate(ts):
                        dve.wait_ge(S["wtc"], t + 1)
                        dve.tensor_scalar(w_row[:, j, :], flat(both[:, ds(t, 1), :]), 1.0, None, ALU.mult).then_inc(S["wr"], 1)
                    for j, t in enumerate(ts):
                        dve.wait_ge(S["b2"], t + 1)
                        wait_past(dve, S[f"out{j}"], (t - j) * 8)
                        dve.tensor_tensor(t_out[:, j, :], tile_of(rows_b, t), bank[2 + j][:, 0:C], ALU.add).then_inc(S["outm"], 1)
                dve.sem_inc(S["wtc"], 2)
                pairs(dve, g3)

            @block.tensor
            def _(pe):
                pe.wait_ge(S["wts"], 64)
                pe.sem_inc(S["turned"], 2)

                def turn(dst, j):
                    for k in range(CK):
                        ins = pe.transpose(dst[:, k * P:(k + 1) * P], t_row[:, j, k * P:(k + 1) * P], ident[:, :])
                    return ins

                def g1(ts):
                    for j, t in enumerate(ts):
                        pe.wait_ge(S["copied"], t + 1)
                        turn(bank[j], j).then_inc(S["turned"], 1)
                    for j, t in enumerate(ts):
                        pe.wait_ge(S["turned_col"], t + 1)
                        pe.wait_ge(S["x1"], t + 1)
                        for k in range(CK):
                            ins = pe.matmul(bank[2 + j][:, 0:C], t_col[:, j, k, :], wt[:, k, :], start=k == 0, stop=k == CK - 1)
                        ins.then_inc(S["times"], 1)
                pairs(pe, g1)

                def g2(ts):
                    for j, t in enumerate(ts):
                        pe.wait_ge(S["normed"], t + 1)
                        turn(bank[j], j).then_inc(S["nt"], 1)
                    for j, t in enumerate(ts):
                        pe.wait_ge(S["ntc"], t + 1)
                        for k in range(CK):
                            pe.matmul(bank[2 + j][:, 0:NE], t_col[:, j, k, :], wgate[:, k, :], start=k == 0, stop=False)
                        pe.matmul(bank[2 + j][:, 0:NE], ones[0:1, :], bgate[:, :], start=False, stop=True).then_inc(S["lg"], 1)
                pairs(pe, g2)
                pe.wait_ge(S["all"], 1)
                fl = both[:, :, :].rearrange("p t e -> p (t e)")
                for i in range(2):
                    pe.matmul(bank[i][:, 0:E2], before[:, :], fl[:, i * E2:(i + 1) * E2], start=True, stop=True)
                    ins = pe.matmul(bank[2 + i][:, 0:E2], ones[:, :], fl[:, i * E2:(i + 1) * E2], start=True, stop=True)
                ins.then_inc(S["ready"], 1)
                pe.wait_ge(S["first"], 1)
                pe.transpose(bank[4][0:NE, 0:P], small[:, 3, :], ident[:, :]).then_inc(S["tabs"], 1)
                pe.wait_ge(S["ind"], 1)
                pe.matmul(bank[5][0:1, 0:MT], ones[0:NE, 0:1], tab[:, :], start=True, stop=True).then_inc(S["tabs"], 1)

                def g3(ts):
                    for j, t in enumerate(ts):
                        pe.wait_ge(S["wr"], t + 1)
                        pe.transpose(bank[j][0:NE, 0:P], w_row[:, j, :], ident[:, :]).then_inc(S["wt"], 1)
                    for j, t in enumerate(ts):
                        pe.wait_ge(S["wtc"], t + 3)
                        pe.matmul(bank[2 + j][:, 0:C], w_col[:, j, :], eb2[:, :], start=True, stop=True).then_inc(S["b2"], 1)
                pairs(pe, g3)


def expert_block(nc, alloc, v):
    ident, bank, tile_expert = (v[n] for n in ("ident", "bank", "tile_expert"))
    with ExitStack() as ctx:
        sb, sem_ = alloc(ctx, "expert_")
        sem = lambda n: sem_("e_" + n)
        w1 = sb("w1", [P, NE, CK, FE])
        w2 = sb("w2", [P, NE, EK, C])
        b1_row = sb("b1_row", [NE * EK, P])
        b1 = sb("b1", [P, NE, EK])
        xin = sb("xin", [P, 2, C])
        col = sb("col", [P, 2, CK, P])
        hid = sb("hid", [P, 2, FE])
        hid_t = sb("hid_t", [P, 2, EK, P])
        res = sb("res", [P, 2, C])
        S = {n: sem(n) for n in "w1 w2 b b_turned b_kept in0 in1 xt xtc h hc ht htc y yc out0 out1 act_turn".split()}
        rowtile = lambda d, t: d.rearrange("(t p) c -> t p c", p=P)[ds(t, 1)].rearrange("a p c -> (a p) c")

        with nc.Block() as block:
            @block.sync
            def _(sp):
                def load(ts):
                    for j, t in enumerate(ts):
                        sp.dma_start(xin[:, j, :], rowtile(v["slots_in"], t)).then_inc(S[f"in{j}"], 16)

                def body(ts, later):
                    for j, t in enumerate(later):
                        sp.wait_ge(S["xt"], t - 1)
                        sp.dma_start(xin[:, j, :], rowtile(v["slots_in"], t)).then_inc(S[f"in{j}"], 16)
                    store(pair_before(ts))

                def store(ts):
                    for j, t in enumerate(ts):
                        sp.wait_ge(S["yc"], t + 1)
                        sp.dma_start(rowtile(v["slots_out"], t), res[:, j, :]).then_inc(S[f"out{j}"], 16)

                sp.dma_start(b1_row[:, :], v["eb1"].rearrange("x (k p) -> (x k) p", p=P)).then_inc(S["b"], 16)
                load([0, 1])
                for x in range(NE):
                    sp.dma_start(w1[:, x, :, :], v["ew1"][x].rearrange("(k p) f -> p k f", p=P)).then_inc(S["w1"], 16)
                for x in range(NE):
                    sp.dma_start(w2[:, x, :, :], v["ew2"][x].rearrange("(k p) c -> p k c", p=P)).then_inc(S["w2"], 16)
                ahead(sp, lambda ts: None, body, MT)
                store([MT - 2, MT - 1])
                for j in range(2):
                    sp.wait_ge(S[f"out{j}"], 16 * (MT // 2))

            @block.scalar
            def _(act):
                act.wait_ge(S["b_turned"], 1)
                act.copy(b1[:, :, :].rearrange("p x k -> p (x k)"), bank[4][:, 0:NE * EK]).then_inc(S["b_kept"], 1)

                def keep_col(ts):
                    for j, t in enumerate(ts):
                        act.wait_ge(S["xt"], t + 1)
                        act.copy(col[:, j, :, :].rearrange("p k n -> p (k n)"), bank[j][:, 0:C]).then_inc(S["xtc"], 1)

                def body(ts, later):
                    keep_col(later)
                    for j, t in enumerate(ts):
                        (_, (x,)) = nc.values_load_multi_w_load_instructions(
                            tile_expert[0:1, ds(t, 1)], engines=[mybir.EngineType.Activation], min_val=0, max_val=NE - 1)
                        act.wait_ge(S["ht"], t + 1)
                        act.sem_inc(S["act_turn"], 1)
                        for k in range(EK):
                            act.activation(hid_t[:, j, k, :], bank[4 + j][:, k * P:(k + 1) * P], ACT.Relu,
                                           bias=b1[:, ds(x, 1), k:k + 1].rearrange("p a b -> p (a b)")).then_inc(S["htc"], 1)
                act.wait_ge(S["b_kept"], 1)
                ahead(act, keep_col, body, MT)

            @block.vector
            def _(dve):
                def body(ts):
                    for j, t in enumerate(ts):
                        dve.wait_ge(S["h"], t + 1)
                        dve.tensor_copy(hid[:, j, :], bank[2 + j][:, :]).then_inc(S["hc"], 1)
                    for j, t in enumerate(ts):
                        dve.wait_ge(S["y"], t + 1)
                        wait_past(dve, S[f"out{j}"], (t - j) * 8)
                        dve.tensor_copy(res[:, j, :], bank[6 + j][:, 0:C]).then_inc(S["yc"], 1)
                pairs(dve, body, MT)

            @block.tensor
            def _(pe):
                pe.wait_ge(S["b"], 16)
                pe.transpose(bank[4][:, 0:NE * EK], b1_row[:, :], ident[0:NE * EK, 0:NE * EK]).then_inc(S["b_turned"], 1)
                pe.wait_ge(S["b_kept"], 1)

                def turn(ts):
                    for j, t in enumerate(ts):
                        pe.wait_ge(S[f"in{j}"], (t - j) * 8 + 16)
                        for k in range(CK):
                            ins = pe.transpose(bank[j][:, k * P:(k + 1) * P], xin[:, j, k * P:(k + 1) * P], ident[:, :])
                        ins.then_inc(S["xt"], 1)

                def body(ts, later):
                    expert = []
                    for j, t in enumerate(ts):
                        (_, (x,)) = nc.values_load_multi_w_load_instructions(
                            tile_expert[0:1, ds(t, 1)], engines=[mybir.EngineType.PE], min_val=0, max_val=NE - 1)
                        expert.append(x)
                    for j, t in enumerate(ts):
                        pe.wait_ge(S["xtc"], t + 1)
                        for k in range(CK):
                            ins = pe.matmul(bank[2 + j][:, :], col[:, j, k, :], w1[:, ds(expert[j], 1), k, :].rearrange("p a f -> p (a f)"),
                                            start=k == 0, stop=k == CK - 1)
                        ins.then_inc(S["h"], 1)
                    turn(later)
                    for j, t in enumerate(ts):
                        pe.wait_ge(S["hc"], t + 1)
                        for k in range(EK):
                            ins = pe.transpose(bank[4 + j][:, k * P:(k + 1) * P], hid[:, j, k * P:(k + 1) * P], ident[:, :])
                        ins.then_inc(S["ht"], 1)
                    if isinstance(ts[0], int) and ts[0] == 0:
                        pe.wait_ge(S["w2"], 16 * NE)
                    for j, t in enumerate(ts):
                        pe.wait_ge(S["htc"], t * EK + EK)
                        for k in range(EK):
                            ins = pe.matmul(bank[6 + j][:, 0:C], hid_t[:, j, k, :], w2[:, ds(expert[j], 1), k, :].rearrange("p a f -> p (a f)"),
                                            start=k == 0, stop=k == EK - 1)
                        ins.then_inc(S["y"], 1)

                def first(ts):
                    turn(ts)
                    pe.wait_ge(S["w1"], 16 * NE)
                ahead(pe, first, body, MT)


def combine_block(nc, alloc, v):
    slot_i, gate_w2 = v["slot_i"], v["gate_w2"]
    with ExitStack() as ctx:
        sb, sem_ = alloc(ctx, "combine_")
        sem = lambda n: sem_("f_" + n)
        y = sb("f_y", [P, NT, C])
        o = sb("f_o", [P, NT, C])
        got = sb("f_got", [P, 2, 2, C])
        idx = sb("f_idx", [P, 2, 2], I32)
        gam, bet = sb("f_gam", [P, C]), sb("f_bet", [P, C])
        stats = sb("f_stats", [P, NT, 6])
        mean, var, rstd = sb("f_mean", [P, NT]), sb("f_var", [P, NT]), sb("f_rstd", [P, NT])
        t1, t2 = sb("f_t1", [P, 2, C]), sb("f_t2", [P, 2, C])
        S = {n: sem(n) for n in "in y0 y1 stat copied pool_turn got0 got1 ready rooted steps dve_turn a b c d out".split()}
        tile_of = lambda rows_, t: flat(rows_[:, ds(t, 1), :])
        CUT = [0, 16, 32, NT]

        with nc.Block() as block:
            @block.sync
            def _(sp):
                sp.dma_start(y[:, :, :], v["xg_d"].rearrange("(t p) c -> p t c", p=P)).then_inc(S["in"], 16)
                sp.dma_start(o[:, :, :], v["x1_d"].rearrange("(t p) c -> p t c", p=P)).then_inc(S["in"], 16)
                for s_, d in ((v["gamma"], gam), (v["beta"], bet)):
                    sp.dma_start(d[:, :], s_.rearrange("(a n) -> a n", a=1).to_broadcast([P, C])).then_inc(S["in"], 16)
                full = v["out"][0:(NT - 1) * P, :].rearrange("(t p) c -> p t c", p=P)
                for a, b in ((0, 16), (16, 32), (32, NT - 1)):
                    sp.wait_ge(S["d"], b)
                    sp.dma_start(full[:, a:b, :], o[:, a:b, :]).then_inc(S["out"], 16)
                sp.wait_ge(S["d"], NT)
                sp.dma_start(v["out"][(NT - 1) * P:N, :], o[0:TAIL, NT - 1, :]).then_inc(S["out"], 16)
                sp.wait_ge(S["out"], 64)

            @block.gpsimd
            def _(pool):
                pool.sem_inc(S["y1"], 2)

                def body(ts):
                    for j, t in enumerate(ts):
                        pool.wait_ge(S["y1"], t + 1)
                        pool.sem_inc(S["pool_turn"], 1)
                        for a in range(2):
                            pool.tensor_copy(idx[:, j, a:a + 1], slot_i[:, a, ds(t, 1)]).then_inc(S["copied"], 1)
                    for j, t in enumerate(ts):
                        pool.wait_ge(S["copied"], t * 2 + 2)
                        pool.sem_inc(S["pool_turn"], 1)
                        for a in range(2):
                            pool.indirect_dma_start(got[:, j, a, :], None, v["slots_out"],
                                                    bass.IndirectOffsetOnAxis(ap=idx[:, j, a:a + 1].bitcast(U32), axis=0)
                                                    ).then_inc(S[f"got{j}"], 16)
                pairs(pool, body)

            @block.scalar
            def _(act):
                act.wait_ge(S["ready"], 1)
                act.activation(var[:, :], var[:, :], ACT.Sqrt).then_inc(S["rooted"], 1)

            @block.vector
            def _(dve):
                s = Chain(dve, S["steps"]).step
                dve.wait_ge(S["in"], 64)

                def body(ts):
                    for j, t in enumerate(ts):
                        dve.wait_ge(S[f"got{j}"], (t - j) * 16 + 32)
                        yt = tile_of(y, t)
                        dve.scalar_tensor_tensor(yt, got[:, j, 0, :], gate_w2[:, 0, ds(t, 1)], yt, ALU.mult, ALU.add).then_inc(S["y0"], 1)
                    for j, t in enumerate(ts):
                        yt = tile_of(y, t)
                        dve.wait_ge(S["y0"], t + 1)
                        dve.scalar_tensor_tensor(yt, got[:, j, 1, :], gate_w2[:, 1, ds(t, 1)], yt, ALU.mult, ALU.add).then_inc(S["y1"], 1)
                    for j, t in enumerate(ts):
                        dve.wait_ge(S["y1"], t + 3)
                        dve.sem_inc(S["dve_turn"], 1)
                        dve.bn_stats(flat(stats[:, ds(t, 1), :]), tile_of(y, t)).then_inc(S["stat"], 1)
                pairs(dve, body)
                dve.wait_ge(S["stat"], NT)
                norm_stats(dve, s, stats, mean[:, :], var[:, :], rstd[:, :], S["ready"], S["rooted"])

                def last(ts):
                    for j, t in enumerate(ts):
                        dve.tensor_scalar(t1[:, j, :], tile_of(y, t), mean[:, ds(t, 1)], rstd[:, ds(t, 1)], ALU.subtract,
                                          ALU.mult).then_inc(S["a"], 1)
                    for j, t in enumerate(ts):
                        dve.wait_ge(S["a"], t + 1)
                        dve.tensor_tensor(t2[:, j, :], t1[:, j, :], gam[:, :], ALU.mult).then_inc(S["b"], 1)
                        dve.tensor_tensor(tile_of(o, t), tile_of(o, t), bet[:, :], ALU.add).then_inc(S["c"], 1)
                    for j, t in enumerate(ts):
                        dve.wait_ge(S["b"], t + 1)
                        dve.wait_ge(S["c"], t + 1)
                        dve.tensor_tensor(tile_of(o, t), tile_of(o, t), t2[:, j, :], ALU.add).then_inc(S["d"], 1)
                pairs(dve, last)


_NAMES = ["x", "src", "dst", "L0_gnn_weight", "L0_gnn_bias", "L0_mix_Wq", "L0_mix_Wk", "L0_mix_Wv", "L0_mix_Wm", "L0_mix_W1",
          "L0_mix_W2", "L0_mix_g1", "L0_mix_b1", "L0_mix_g2", "L0_mix_b2", "L0_ffn_gate_w", "L0_ffn_gate_b", "L0_ffn_w1",
          "L0_ffn_b1", "L0_ffn_w2", "L0_ffn_b2", "L0_ffn_gamma", "L0_ffn_beta"]


def kernel(**inputs):
    import numpy as np
    import concourse.bacc as bacc
    from concourse.bass_utils import run_bass_kernel_spmd as run

    nc = bacc.Bacc("TRN2", target_bir_lowering=False, num_devices=1)
    arrays, args = {}, []
    for name in _NAMES:
        a = np.ascontiguousarray(inputs[name])
        arrays["in_" + name] = a
        args.append(nc.dram_tensor("in_" + name, a.shape, mybir.dt.from_np(a.dtype), kind="ExternalInput").ap())
    result = nc.dram_tensor("result", (N, C), F32, kind="ExternalOutput").ap()
    build(nc, *args, result)
    r = run(nc, [arrays], core_ids=[0])
    return r.results[0]["result"]
```

```python
from contextlib import ExitStack

import concourse.bass as bass
from concourse import mybir

F32 = mybir.dt.float32
BF16 = mybir.dt.bfloat16
I32 = mybir.dt.int32
U32 = mybir.dt.uint32
U16 = mybir.dt.uint16
ALU = mybir.AluOpType
ACT = mybir.ActivationFunctionType
AX_X = mybir.AxisListType.X
ds = bass.ds

P = 128
N, C = 6250, 256
CK = C // P
NT = -(-N // P)
NP = NT * P
TAIL = N - (NT - 1) * P
E = 100000
EP = 125
EC = E // EP
RING = 25
G = 8
NCH = -(-(E // P + NT) // (2 * G)) * 2 * G
EARLY = 100
assert EARLY % (2 * RING) == 0 and EC % (2 * RING) == 0
LOC_SHIFT = 13
NO_ROW = 255
LN_EPS, ATT_EPS = 1e-5, 1e-6
HEADS, HD = 8, 32
HH = P // HD
F2 = 512
FK = F2 // P
NE, FE = 16, 512
EK = FE // P
MT = 114
assert MT * P >= 2 * N + NE * (P - 1) and MT % 2 == 0
GB = 8
CX = C + 2
GU = 7
NG = NT // GU
assert NT % GU == 0
assert EC == (NT + 1) * 2 * GB


def flat(ap):
    return ap.rearrange("p a n -> p (a n)")


class Chain:

    def __init__(self, eng, sem, first=0):
        self.eng, self.sem, self.first, self.n = eng, sem, first, 0

    def __call__(self, ins):
        ins.then_inc(self.sem, 1)
        self.n += 1

    def wait(self):
        self.eng.wait_ge(self.sem, self.first + self.n)

    def step(self, ins):
        self(ins)
        self.wait()


def build(nc, x, src, dst, gnn_w, gnn_b, wq, wk, wv, wm, w1, w2, g1, b1, g2, b2,
          gate_w, gate_b, ew1, eb1, ew2, eb2, gamma, beta, out):
    def dram(name, shape, dt=F32):
        return nc.dram_tensor(name, shape, dt).ap()

    edge_list = dram("edge_list", (P * NCH,), I32)
    u_d = [dram(f"u{k}_rows", (NP, C)) for k in range(3)]
    base_d = dram("base_rows", (NP, C))
    base2_d = dram("base2_rows", (NP, C))
    h2_d = dram("h2_rows", (NP, C))
    xg_d = dram("xg_rows", (NP + P, C))
    x1_d = dram("x1_rows", (NP, C))
    slots_in = dram("slots_in", ((MT + 1) * P, CX))

    with ExitStack() as outer:
        def alloc(ctx, label=""):
            sems = []

            def sem(name):
                sems.append(nc.alloc_semaphore(name=name))
                return sems[-1]

            def clear():
                if sems:
                    nc.clear_and_free_semaphores(sems)
                    nc.all_engine_barrier()

            ctx.callback(clear)
            return (lambda name, shape, dt=F32: ctx.enter_context(nc.sbuf_tensor(label + name, shape, dt)),
                    sem)

        sb, sem = alloc(outer)
        bank = [outer.enter_context(nc.psum_tensor(f"bank{i}", [P, 512], F32)) for i in range(8)]
        iota = sb("iota", [P, NCH])
        ones = sb("ones", [P, P])
        ident = sb("ident", [P, P])
        before = sb("before", [P, P])
        valid = sb("valid", [P, NT])
        slot_i = sb("slot_i", [P, 2, NT], I32)
        tile_expert = sb("tile_expert", [1, MT], I32)
        tiles_used = sb("tiles_used", [1, 1], I32)
        with ExitStack() as graph:
            sb, _ = alloc(graph)
            cols = sb("cols", [P, NCH], U32)
            locs = sb("locs", [P, NCH])
            chunk_tile = sb("chunk_tile", [1, NCH], I32)
            chunks = sb("chunks", [1, 1], I32)
            degs = sb("degs", [P, 2, NT])
            dinv = sb("dinv", [P, NT])
            half = sb("half", [P, NT])
            to_t = sb("to_t", [P, 3, NT])
            to_u = sb("to_u", [P, 3, NT])
            begin = sb("begin", [P, 3, NT])
            mean, var, rstd = sb("mean", [P, NT]), sb("var", [P, NT]), sb("rstd", [P, NT])
            rows_a = sb("rows_a", [P, NT, C])
            rows_b = sb("rows_b", [P, NT, C])
            with ExitStack() as edges:
                sb, _ = alloc(edges)
                word = sb("word", [P, EC], I32)
                addr = sb("addr", [P, EC], I32)
                tile_f = sb("tile_f", [P, EC])
                self_f = sb("self_f", [P, EC])
                loc_f = sb("loc_f", [P, EC])
                sort_block(nc, outer, alloc, locals())
                mix_block(nc, outer, alloc, locals())
            for k in range(3):
                cheb_block(nc, outer, alloc, locals(), k)
            gate_block(nc, outer, alloc, locals())
        expert_block(nc, alloc, locals())
        combine_block(nc, alloc, locals())


def scatter_columns(pool, ring, S, addr, word, list_rows, first, last):
    e = slice(0, EP)

    def turn(n):
        for h in range(2):
            half = S[f"words{h}"]
            wait_past(pool, half, n * (16 * RING))
            pool.sem_inc(S["scatter_turn"], 1)
            for i, src in enumerate((addr, word)):
                pool.tensor_copy(ring[e, h, i, :], src[e, ds(n * (2 * RING) + (first * 2 + h) * RING, RING)]
                                 ).then_inc(S["scatter_copied"], 1)
            pool.wait_ge(S["scatter_copied"], n * 4 + h * 2 + 2)
            pool.sem_inc(S["scatter_turn"], 1)
            for i in range(RING):
                pool.indirect_dma_start(
                    list_rows, bass.IndirectOffsetOnAxis(ap=ring[e, h, 0, i:i + 1].bitcast(U32), axis=0),
                    ring[e, h, 1, i:i + 1], None).then_inc(half, 16)
    turn(0)
    with pool.Fori(1, last - first) as n:
        turn(n)
    for h in range(2):
        pool.wait_ge(S[f"words{h}"], 16 * RING * (last - first))


def sort_block(nc, outer, alloc, v):
    iota, ones, ident, before = v["iota"], v["ones"], v["ident"], v["before"]
    word, addr, tile_f, self_f, loc_f, chunk_tile, bank, edge_list = (
        v[k] for k in ("word", "addr", "tile_f", "self_f", "loc_f", "chunk_tile", "bank", "edge_list"))
    slots_in, rows_a = v["slots_in"], v["rows_a"]
    with ExitStack() as ctx:
        sb, sem = alloc(ctx, "sort_")
        iota_i = sb("iota_i", [P, NCH], I32)
        src_i = sb("src_i", [P, EC], I32)
        dst_i = sb("dst_i", [P, EC], I32)
        src_f = sb("src_f", [P, EC])
        dst_f = sb("dst_f", [P, EC])
        loc_i = sb("loc_i", [P, EC], I32)
        low_i = sb("low_i", [P, EC], I32)
        tile_b = sb("tile_b", [P, EC], BF16)
        mask = sb("mask", [P, GU, EC], BF16)
        ones_e = sb("ones_e", [P, EC], BF16)
        running = sb("running", [P, GU, EC])
        ring = sb("ring", [P, 2, 2, RING], I32)
        pos_f = sb("pos_f", [P, EC])
        counts = sb("counts", [P, NT])
        small = sb("small", [P, 5, NT])
        small_i = sb("small_i", [P, NT], I32)
        base = sb("base", [P, 2, NT])
        tab_ind = sb("tab_ind", [NT, NCH])
        first_t = sb("first_t", [NT, 1])
        fill = sb("fill", [P, NCH], I32)
        zero = sb("zero", [P, 4, CX])
        spare_i = sb("spare_i", [P, 1], I32)
        consts_ready, made, loaded, steps = sem("consts_ready"), sem("made"), sem("edges_loaded"), sem("sort_steps")
        stored, counted, sums, firsts, inds = sem("fill_stored"), sem("tiles_counted"), sem("sums"), sem("firsts"), sem("inds")
        masked, scanned, picked, kept, scan_turn = (sem(n) for n in "masked scanned picked kept scan_turn".split())
        spared = sem("spared")
        filled, placed = sem("list_filled"), sem("early_placed")
        S = {n: sem("early_" + n) for n in "scatter_turn scatter_copied words0 words1".split()}
        e = slice(0, EP)
        H = NCH // 2

        with nc.Block() as block:
            @block.sync
            def _(sp):
                sp.dma_start(src_i[e, :], v["src"].rearrange("(p c) -> p c", p=EP)).then_inc(loaded, 16)
                sp.dma_start(dst_i[e, :], v["dst"].rearrange("(p c) -> p c", p=EP)).then_inc(loaded, 16)
                sp.wait_ge(consts_ready, 10)
                sp.dma_start(edge_list.rearrange("(p c) -> p c", p=P), fill[:, :]).then_inc(filled, 16)
                xin = v["x"]
                sp.dma_start(rows_a[:, 0:NT - 1, :], xin[0:(NT - 1) * P, :].rearrange("(t p) c -> p t c", p=P)).then_inc(stored, 16)
                sp.dma_start(rows_a[0:TAIL, NT - 1, :], xin[(NT - 1) * P:N, :]).then_inc(stored, 16)
                tiles = slots_in.rearrange("(t p) c -> p t c", p=P)
                sp.wait_ge(spared, 1)
                n = 1
                for t in range(0, MT, 4):
                    k = min(4, MT - t)
                    sp.dma_start(tiles[:, t:t + k, :], zero[:, 0:k, :]).then_inc(stored, 16)
                    n += 1
                sp.wait_ge(stored, 16 * (n + 1))

            @block.gpsimd
            def _(pool):
                pool.memset(rows_a[:, NT - 1, :], 0.0).then_inc(consts_ready, 1)
                pool.iota(iota_i[:, :], pattern=[[1, NCH]], base=0, channel_multiplier=0).then_inc(consts_ready, 1)
                pool.memset(ones[:, :], 1.0).then_inc(consts_ready, 1)
                pool.memset(ones_e[:, :], 1.0).then_inc(consts_ready, 1)
                pool.memset(fill[:, :], NO_ROW << LOC_SHIFT).then_inc(consts_ready, 1)
                pool.memset(zero[:, :, :], 0.0).then_inc(consts_ready, 1)
                pool.iota(spare_i[:, :], pattern=[[0, 1]], base=NP, channel_multiplier=1).then_inc(consts_ready, 1)
                pool.memset(ident[:, :], 0.0).then_inc(made, 1)
                pool.memset(before[:, :], 1.0).then_inc(made, 1)
                pool.memset(v["valid"][:, :], 1.0).then_inc(made, 1)
                pool.wait_ge(made, 3)
                pool.affine_select(out=ident[:, :], in_=ident[:, :], compare_op=ALU.not_equal, fill=1.0, base=0,
                                   pattern=[[-1, P]], channel_multiplier=1).then_inc(consts_ready, 1)
                pool.affine_select(out=before[:, :], in_=before[:, :], compare_op=ALU.is_gt, fill=0.0, base=0,
                                   pattern=[[1, P]], channel_multiplier=-1).then_inc(consts_ready, 1)
                pool.affine_select(out=v["valid"][:, :], in_=v["valid"][:, :], compare_op=ALU.is_gt, fill=0.0, base=N,
                                   pattern=[[-P, NT]], channel_multiplier=-1).then_inc(consts_ready, 1)
                pool.wait_ge(filled, 16)
                pool.wait_ge(placed, 1)
                scatter_columns(pool, ring, S, addr, word, edge_list.rearrange("(n a) -> n a", a=1), 0, EARLY // (2 * RING))

            @block.vector
            def _(dve):
                s = Chain(dve, steps).step
                dve.wait_ge(consts_ready, 10)
                s(dve.tensor_copy(iota[:, :], iota_i[:, :]))
                s(dve.tensor_copy(zero[:, :, C:C + 1], spare_i[:, :].unsqueeze(1).to_broadcast([P, 4, 1])))
                dve.sem_inc(spared, 1)
                dve.wait_ge(loaded, 32)
                s(dve.tensor_scalar(loc_i[e, :], src_i[e, :], 7, None, ALU.arith_shift_right))
                s(dve.tensor_copy(tile_b[e, :], loc_i[e, :]))
                s(dve.memset(counts[:, :], 0.0))
                with dve.Fori(0, NG) as g:
                    for i in range(GU):
                        t = g * GU + i
                        dve.tensor_scalar(mask[e, i, :], tile_b[e, :], iota[e, ds(t, 1)], 0.0, ALU.is_equal,
                                          ALU.add, accum_out=counts[e, ds(t, 1)]).then_inc(counted, 1)
                    dve.wait_ge(counted, g * GU + GU)
                dve.wait_ge(sums, 1)
                s(dve.tensor_copy(small[:, 0, :], bank[0][:, NT:2 * NT]))
                s(dve.tensor_scalar(small[:, 1, :], small[:, 0, :], float(P - 1), None, ALU.add))
                s(dve.tensor_copy(small_i[:, :], small[:, 1, :]))
                s(dve.tensor_scalar(small_i[:, :], small_i[:, :], 7, None, ALU.arith_shift_right))
                s(dve.tensor_copy(small[:, 2, :], small_i[:, :]))
                s(dve.tensor_tensor_scan(small[:, 3, :], ones[:, 0:NT], small[:, 2, :], 0.0, ALU.mult, ALU.add))
                s(dve.tensor_tensor(small[:, 4, :], small[:, 3, :], small[:, 2, :], ALU.subtract))
                dve.sem_inc(firsts, 1)
                s(dve.tensor_copy(v["chunks"][0:1, :], small[0:1, 3, NT - 1:NT]))
                s(dve.tensor_scalar(base[:, 0, :], small[:, 4, :], float(P), -1.0, ALU.mult, ALU.add))
                s(dve.tensor_tensor(base[:, 0, :], base[:, 0, :], bank[0][:, 0:NT], ALU.add))
                dve.wait_ge(sums, 2)
                s(dve.tensor_copy(first_t[:, :], bank[1][0:NT, 0:1]))
                s(dve.tensor_scalar(tab_ind[:, :], iota[0:NT, :], first_t[:, 0:1], None, ALU.is_ge))
                dve.sem_inc(inds, 1)
                dve.wait_ge(sums, 3)
                for k in range(2):
                    s(dve.tensor_scalar(chunk_tile[0:1, k * H:(k + 1) * H], bank[2 + k][0:1, 0:H], -1.0, None, ALU.add))
                dve.wait_ge(counted, NT)

                def place(part, cols):
                    o = part * NT
                    with dve.Fori(0, NG) as g:
                        for i in range(GU):
                            t = g * GU + i
                            dve.tensor_scalar(mask[e, i, cols], tile_b[e, cols], iota[e, ds(t, 1)], None, ALU.is_equal).then_inc(masked, 1)
                        for i in range(GU):
                            t = g * GU + i
                            dve.wait_ge(masked, g * GU + (o + i + 1))
                            dve.tensor_tensor_scan(running[e, i, cols], ones_e[e, cols], mask[e, i, cols], base[e, part, ds(t, 1)],
                                                   ALU.mult, ALU.add).then_inc(scanned, 1)
                        for i in range(GU):
                            t = g * GU + i
                            dve.wait_ge(scanned, g * GU + (o + i + 1))
                            if part == 0:
                                dve.tensor_scalar(base[e, 1, ds(t, 1)], running[e, i, cols.stop - 1:cols.stop], 0.0, None,
                                                  ALU.add).then_inc(kept, 1)
                            dve.sem_inc(scan_turn, 1)
                            dve.copy_predicated(pos_f[e, cols], mask[e, i, cols].bitcast(U16), running[e, i, cols]).then_inc(picked, 1)
                            dve.wait_ge(picked, g * GU + (o + i + 1))
                        if part == 0:
                            dve.wait_ge(kept, g * GU + GU)
                    s(dve.tensor_copy(loc_i[e, cols], pos_f[e, cols]))
                    s(dve.tensor_scalar(low_i[e, cols], loc_i[e, cols], P - 1, None, ALU.bitwise_and))
                    s(dve.tensor_scalar(loc_i[e, cols], loc_i[e, cols], 7, None, ALU.arith_shift_right))
                    s(dve.tensor_copy(src_f[e, cols], low_i[e, cols]))
                    s(dve.tensor_copy(dst_f[e, cols], loc_i[e, cols]))
                    s(dve.scalar_tensor_tensor(addr[e, cols], src_f[e, cols], float(NCH), dst_f[e, cols], ALU.mult, ALU.add))
                s(dve.tensor_scalar(low_i[e, :], src_i[e, :], P - 1, None, ALU.bitwise_and))
                s(dve.tensor_scalar(word[e, :], low_i[e, :], LOC_SHIFT, None, ALU.logical_shift_left))
                s(dve.tensor_tensor(word[e, :], word[e, :], dst_i[e, :], ALU.bitwise_or))
                s(dve.tensor_copy(loc_f[e, :], low_i[e, :]))
                place(0, slice(0, EARLY))
                dve.sem_inc(placed, 1)
                s(dve.tensor_copy(src_f[e, :], src_i[e, :]))
                s(dve.tensor_copy(dst_f[e, :], dst_i[e, :]))
                s(dve.tensor_tensor(self_f[e, :], src_f[e, :], dst_f[e, :], ALU.is_equal))
                s(dve.tensor_copy(tile_f[e, :], tile_b[e, :]))
                s(dve.tensor_scalar(self_f[e, :], self_f[e, :], -64.0, 64.0, ALU.mult, ALU.add))
                s(dve.tensor_tensor(self_f[e, :], self_f[e, :], tile_f[e, :], ALU.add))
                place(1, slice(EARLY, EC))

            @block.tensor
            def _(pe):
                pe.wait_ge(consts_ready, 10)
                pe.wait_ge(counted, NT)
                pe.matmul(bank[0][:, 0:NT], before[:, :], counts[:, :], start=True, stop=True)
                pe.matmul(bank[0][:, NT:2 * NT], ones[:, :], counts[:, :], start=True, stop=True).then_inc(sums, 1)
                pe.wait_ge(firsts, 1)
                pe.transpose(bank[1][0:NT, 0:P], small[:, 4, :], ident[:, :]).then_inc(sums, 1)
                pe.wait_ge(inds, 1)
                for k in range(2):
                    ins = pe.matmul(bank[2 + k][0:1, 0:H], ones[0:NT, 0:1], tab_ind[:, k * H:(k + 1) * H],
                                    start=True, stop=True)
                ins.then_inc(sums, 1)


def wait_past(eng, sem, value):
    if not isinstance(value, int) or value > 0:
        eng.wait_ge(sem, value)


def pairs(eng, body, n=NT):
    body([0, 1])
    with eng.Fori(1, n // 2) as it:
        body([it * 2, it * 2 + 1])
    if n % 2:
        body([n - 1])


def ahead(eng, first, body, n=NT, spare=0, used=None):
    m = n // 2
    odd = [n - 1] if n % 2 else []
    first([0, 1])
    body([0, 1], [2, 3])
    with eng.Fori(1, m - max(1, spare)) as it:
        body([it * 2, it * 2 + 1], [it * 2 + 2, it * 2 + 3])
    if not spare:
        body([2 * m - 2, 2 * m - 1], odd)
    for q in range(m - spare, m):
        with eng.If(used > 2 * q):
            body([2 * q, 2 * q + 1], [2 * q + 2, 2 * q + 3] if q < m - 1 else odd)
    if odd:
        body(odd, [])


def pair_before(ts):
    if isinstance(ts[0], int) and ts[0] == 0:
        return []
    return [ts[0] - 2, ts[0] - 1]


def norm_stats(dve, s, stats, mean, var, rstd, ready, rooted):
    s(dve.tensor_tensor(mean, stats[:, :, 1], stats[:, :, 4], ALU.add))
    s(dve.tensor_scalar(mean, mean, 0.5, None, ALU.mult))
    s(dve.tensor_tensor(rstd, stats[:, :, 1], stats[:, :, 4], ALU.subtract))
    s(dve.tensor_tensor(rstd, rstd, rstd, ALU.mult))
    s(dve.tensor_scalar(rstd, rstd, 0.25, LN_EPS, ALU.mult, ALU.add))
    s(dve.tensor_tensor(var, stats[:, :, 2], stats[:, :, 5], ALU.add))
    s(dve.scalar_tensor_tensor(var, var, 1.0 / C, rstd, ALU.mult, ALU.add))
    dve.sem_inc(ready, 1)
    dve.wait_ge(rooted, 1)
    s(dve.reciprocal(rstd, var))


def mix_block(nc, outer, alloc, v):
    iota, ones, ident, word, addr, tile_f, self_f, loc_f, degs, dinv, half, valid, rows_a, rows_b, bank = (
        v[k] for k in ("iota", "ones", "ident", "word", "addr", "tile_f", "self_f", "loc_f", "degs", "dinv", "half",
                       "valid", "rows_a", "rows_b", "bank"))
    to_t, to_u, begin, mean, var, rstd = (v[k] for k in ("to_t", "to_u", "begin", "mean", "var", "rstd"))
    base_d, h2_d, edge_list = v["base_d"], v["h2_d"], v["edge_list"]
    xt_d = nc.dram_tensor("xt_rows", (NP, C), F32).ap()
    with ExitStack() as ctx:
        sb, sem = alloc(ctx, "mix_")
        ring = sb("ring", [P, 2, 2, RING], I32)
        hot_loc = sb("hot_loc", [P, 2, GB, P], BF16)
        hot_tile = sb("hot_tile", [P, 2, GB, 2, NT], BF16)
        zeros = sb("zeros", [P, P])
        wkg = sb("wkg", [P, CK, 2 * C])
        wv = sb("wv", [P, CK, C])
        wq = sb("wq", [P, CK, C])
        wm = sb("wm", [P, CK, C])
        w1 = sb("w1", [P, 2 * CK, F2])
        w2 = sb("w2", [P, FK, C])
        g1c, b1c = sb("g1c", [P, CK]), sb("b1c", [P, CK])
        stats = sb("stats", [P, NT, 6])
        kv_bd = sb("kv_bd", [P, CK, P + HH])
        t_row = sb("t_row", [P, 2, C])
        t_col = sb("t_col", [P, 2, CK, P])
        t_exp = sb("t_exp", [P, 2, C])
        t_k = sb("t_k", [P, 2, C])
        t_v = sb("t_v", [P, 2, CK, P + 1])
        t_out = sb("t_out", [P, 2, C])
        t_hid = sb("t_hid", [P, 2, FK, P])
        t_mt = sb("t_mt", [P, 2, CK, P])
        t_den = sb("t_den", [P, 2, 2, HEADS])
        names = ("scatter_turn scatter_copied words0 words1 wts_in dsteps var_ready var_rooted "
                 "act_turn dve_turn hot_made hot_used deg_done root_in root_done").split()
        S = {n: sem("m_" + n) for n in names}
        e = slice(0, EP)
        loopsem = lambda n: sem("m_" + n)
        L1 = {n: loopsem("l1_" + n) for n in "stat norm xt xtc kg v kmin kexp kdone vdone sum base kept stored0 stored1 out0 out1 fold".split()}
        L2 = {n: loopsem("l2_" + n) for n in "in0 in1 q qmin qexp qdone att den z msg mt mtc m stat kept".split()}
        L3 = {n: loopsem("l3_" + n) for n in "in0 in1 norm nt ntc h hc o stat kept out0 out1".split()}
        R1 = {n: loopsem("r1_" + n) for n in "ready rooted".split()}
        R2 = {n: loopsem("r2_" + n) for n in "ready rooted".split()}
        bcol = lambda ap: ap.rearrange("(k p) -> p k", p=P)
        rowtile = lambda d, t: d.rearrange("(t p) c -> t p c", p=P)[ds(t, 1)].rearrange("a p c -> (a p) c")
        flat_a = lambda t: flat(rows_a[:, ds(t, 1), :])
        flat_b = lambda t: flat(rows_b[:, ds(t, 1), :])
        col = lambda ap, t: ap[:, ds(t, 1)]

        with nc.Block() as block:
            @block.sync
            def _(sp):
                w = S["wts_in"]
                kpc = lambda a: a.rearrange("(k p) n -> p k n", p=P)
                sp.dma_start(wkg[:, :, 0:C], kpc(v["wk"])).then_inc(w, 16)
                sp.dma_start(wkg[:, :, C:2 * C], kpc(v["gnn_w"][0])).then_inc(w, 16)
                sp.dma_start(wv[:, :, :], kpc(v["wv"])).then_inc(w, 16)
                sp.dma_start(wq[:, :, :], kpc(v["wq"])).then_inc(w, 16)
                sp.dma_start(wm[:, :, :], kpc(v["wm"])).then_inc(w, 16)
                sp.dma_start(w1[:, :, :], kpc(v["w1"])).then_inc(w, 16)
                sp.dma_start(w2[:, :, :], kpc(v["w2"])).then_inc(w, 16)
                with nc.allow_non_contiguous_dma(reason="256 values, once"):
                    sp.dma_start(g1c[:, :], bcol(v["g1"])).then_inc(w, 16)
                    sp.dma_start(b1c[:, :], bcol(v["b1"])).then_inc(w, 16)

                def l1(ts):
                    for j, t in enumerate(ts):
                        sp.wait_ge(L1["xtc"], t + 1)
                        sp.dma_start(rowtile(xt_d, t), t_col[:, j, :, :].rearrange("p k n -> p (k n)")).then_inc(L1[f"stored{j}"], 16)
                    for j, t in enumerate(ts):
                        sp.wait_ge(L1["base"], t + 3)
                        sp.dma_start(rowtile(base_d, t), t_out[:, j, :]).then_inc(L1[f"out{j}"], 16)
                pairs(sp, l1)
                for j in range(2):
                    sp.wait_ge(L1[f"stored{j}"], 16 * (NT // 2 + 1 - j))
                    sp.wait_ge(L1[f"out{j}"], 16 * (NT // 2 + 1 - j))

                def load_xt(L, ts):
                    for j, t in enumerate(ts):
                        sp.dma_start(t_col[:, j, :, :].rearrange("p k n -> p (k n)"), rowtile(xt_d, t)).then_inc(L[f"in{j}"], 16)
                sp.wait_ge(L1["sum"], NT + 2)
                load_xt(L2, [0, 1])

                def l2(ts, later):
                    for j, t in enumerate(later):
                        sp.wait_ge(L2["q"], t - 1)
                        sp.dma_start(t_col[:, j, :, :].rearrange("p k n -> p (k n)"), rowtile(xt_d, t)).then_inc(L2[f"in{j}"], 16)
                ahead(sp, lambda ts: None, l2)
                sp.wait_ge(L2["q"], NT)
                load_xt(L3, [0, 1])

                def store_h2(ts):
                    for j, t in enumerate(ts):
                        sp.wait_ge(L3["kept"], t + 1)
                        sp.dma_start(rowtile(h2_d, t), t_out[:, j, :]).then_inc(L3[f"out{j}"], 16)

                def l3(ts, later):
                    for j, t in enumerate(later):
                        sp.wait_ge(L3["h"], t - 1)
                        sp.dma_start(t_col[:, j, :, :].rearrange("p k n -> p (k n)"), rowtile(xt_d, t)).then_inc(L3[f"in{j}"], 16)
                    store_h2(ts)
                ahead(sp, lambda ts: None, l3)
                for j in range(2):
                    sp.wait_ge(L3[f"out{j}"], 16 * (NT // 2 + 1 - j))

            @block.gpsimd
            def _(pool):
                list_rows = edge_list.rearrange("(n a) -> n a", a=1)
                scatter_columns(pool, ring, S, addr, word, list_rows, EARLY // (2 * RING), EC // (2 * RING))

            @block.scalar
            def _(act):
                def root(R):
                    act.wait_ge(R["ready"], 1)
                    act.activation(var[:, :], var[:, :], ACT.Sqrt).then_inc(R["rooted"], 1)

                root({"ready": S["var_ready"], "rooted": S["var_rooted"]})
                act.sem_inc(L1["vdone"], 2)

                def l1_turned(ts):
                    for j, t in enumerate(ts):
                        act.wait_ge(L1["xt"], t + 1)
                        wait_past(act, L1[f"stored{j}"], (t - j) * 8)
                        act.copy(t_col[:, j, :, :].rearrange("p k n -> p (k n)"), bank[j][:, 0:C]).then_inc(L1["xtc"], 1)

                def l1(ts, later):
                    for j, t in enumerate(ts):
                        act.wait_ge(L1["kmin"], t + 1)
                        act.activation(t_exp[:, j, :], t_exp[:, j, :], ACT.Exp).then_inc(L1["kexp"], 1)
                        act.wait_ge(L1["v"], t + 1)
                        act.wait_ge(L1["sum"], t + 1)
                        act.copy(t_v[:, j, :, 0:P], bank[4 + j][:, 0:C].rearrange("p (k n) -> p k n", k=CK)).then_inc(L1["vdone"], 1)
                    l1_turned(later)
                ahead(act, l1_turned, l1)

                def l2_exp(ts):
                    for j, t in enumerate(ts):
                        act.wait_ge(L2["qmin"], t + 1)
                        act.activation(t_exp[:, j, :], t_exp[:, j, :], ACT.Exp).then_inc(L2["qexp"], 1)

                def l2(ts, later):
                    l2_exp(later)
                    for j, t in enumerate(ts):
                        act.wait_ge(L2["mt"], t + 1)
                        act.copy(t_mt[:, j, :, :].rearrange("p k n -> p (k n)"), bank[4 + j][:, 0:C]).then_inc(L2["mtc"], 1)
                    for j, t in enumerate(ts):
                        act.wait_ge(L2["m"], t + 1)
                        act.sem_inc(S["act_turn"], 1)
                        act.copy(flat_b(t), bank[4 + j][:, C:2 * C]).then_inc(L2["kept"], 1)
                act.sem_inc(L2["kept"], 2)
                ahead(act, l2_exp, l2)
                root(R1)

                def l3_normed(ts):
                    for j, t in enumerate(ts):
                        act.wait_ge(L3["nt"], t + 1)
                        for k in range(CK):
                            act.activation(t_mt[:, j, k, :], bank[j][:, k * P:(k + 1) * P], ACT.Identity,
                                           scale=g1c[:, k:k + 1], bias=b1c[:, k:k + 1]).then_inc(L3["ntc"], 1)

                def l3(ts, later):
                    for j, t in enumerate(ts):
                        act.wait_ge(L3["h"], t + 1)
                        act.activation(t_hid[:, j, :, :].rearrange("p k n -> p (k n)"), bank[2 + j][:, :], ACT.Relu).then_inc(L3["hc"], 1)
                    l3_normed(later)
                    for j, t in enumerate(ts):
                        act.wait_ge(L3["o"], t + 1)
                        act.wait_ge(L3["stat"], t + 1)
                        wait_past(act, L3[f"out{j}"], (t - j) * 8)
                        act.copy(t_out[:, j, :], bank[4 + j][:, 0:C]).then_inc(L3["kept"], 1)
                ahead(act, l3_normed, l3)
                root(R2)
                act.wait_ge(S["root_in"], 1)
                act.activation(half[:, :], half[:, :], ACT.Sqrt).then_inc(S["root_done"], 1)

            @block.vector
            def _(dve):
                ch = Chain(dve, S["dsteps"])
                s = ch.step
                s(dve.memset(zeros[:, :], 0.0))
                s(dve.memset(kv_bd[:, :, :], 0.0))
                with dve.Fori(0, NT) as t:
                    dve.bn_stats(stats[:, ds(t, 1), :].rearrange("p a n -> p (a n)"), flat_a(t)).then_inc(L1["stat"], 1)
                dve.wait_ge(L1["stat"], NT)
                norm_stats(dve, s, stats, mean[:, :], var[:, :], rstd[:, :], S["var_ready"], S["var_rooted"])
                dve.wait_ge(S["wts_in"], 16 * 9)
                for k in range(CK):
                    r = slice(C + k * P, C + (k + 1) * P)
                    s(dve.tensor_tensor(wkg[:, k, r], wkg[:, k, r], ident[:, :], ALU.add))
                dve.sem_inc(L1["fold"], 1)
                dve.sem_inc(L1["base"], 2)

                def l1_norm(ts):
                    for j, t in enumerate(ts):
                        wait_past(dve, L1["xt"], t - 1)
                        dve.tensor_scalar(t_row[:, j, :], flat_a(t), col(mean, t), col(rstd, t), ALU.subtract,
                                          ALU.mult).then_inc(L1["norm"], 1)

                def l1(ts, later):
                    l1_norm(later)
                    for j, t in enumerate(ts):
                        dve.wait_ge(L1["kg"], t + 1)
                        dve.tensor_scalar(t_exp[:, j, :], bank[2 + j][:, 0:C], 0.0, None, ALU.min).then_inc(L1["kmin"], 1)
                        wait_past(dve, L1[f"out{j}"], (t - j) * 8)
                        dve.tensor_tensor(t_out[:, j, :], flat_a(t), bank[2 + j][:, C:2 * C], ALU.add).then_inc(L1["base"], 1)
                        dve.wait_ge(L1["sum"], t + 1)
                        dve.tensor_scalar(t_v[:, j, :, P:P + 1], valid[:, ds(t, 1)].unsqueeze(1).to_broadcast([P, CK, 1]), 1.0, None,
                                          ALU.mult).then_inc(L1["kdone"], 1)
                        dve.wait_ge(L1["kexp"], t + 1)
                        dve.scalar_tensor_tensor(t_k[:, j, :], bank[2 + j][:, 0:C], 0.0, t_exp[:, j, :], ALU.max,
                                                 ALU.add).then_inc(L1["kdone"], 1)
                    for j, t in enumerate(ts):
                        dve.wait_ge(L1["base"], t + 3)
                        dve.tensor_scalar(flat_a(t), flat_a(t), col(mean, t), col(rstd, t), ALU.subtract,
                                          ALU.mult).then_inc(L1["kept"], 1)
                ahead(dve, l1_norm, l1)
                dve.wait_ge(L1["kept"], NT)

                dve.wait_ge(L1["sum"], NT + 3)
                for m in range(CK):
                    for h in range(HH):
                        r = slice(h * HD, (h + 1) * HD)
                        o = m * (P + 1)
                        s(dve.tensor_copy(kv_bd[r, m, r], bank[6][r, o + h * HD:o + (h + 1) * HD]))
                        s(dve.tensor_copy(kv_bd[r, m, P + h:P + h + 1], bank[6][r, o + P:o + P + 1]))
                dve.sem_inc(L2["den"], 1)

                def l2_q(ts):
                    for j, t in enumerate(ts):
                        dve.wait_ge(L2["q"], t + 1)
                        dve.tensor_scalar(t_exp[:, j, :], bank[j][:, 0:C], 0.0, None, ALU.min).then_inc(L2["qmin"], 1)
                    for j, t in enumerate(ts):
                        dve.wait_ge(L2["qexp"], t + 1)
                        dve.scalar_tensor_tensor(t_k[:, j, :], bank[j][:, 0:C], 0.0, t_exp[:, j, :], ALU.max,
                                                 ALU.add).then_inc(L2["qdone"], 1)

                def l2(ts, later):
                    for j, t in enumerate(ts):
                        dve.wait_ge(L2["att"], t + 1)
                        att = bank[2 + j][:, 0:CK * (P + HH)].rearrange("p (k n) -> p k n", k=CK)
                        den = t_den[:, j, 0, :].rearrange("p (k h) -> p k h", k=CK)
                        z = t_den[:, j, 1, :]
                        dve.tensor_scalar(den, att[:, :, P:P + HH], ATT_EPS, None, ALU.add).then_inc(L2["z"], 1)
                        dve.wait_ge(L2["z"], t * 2 + 1)
                        dve.reciprocal(z, t_den[:, j, 0, :]).then_inc(L2["z"], 1)
                        dve.wait_ge(L2["z"], t * 2 + 2)
                        for k in range(CK):
                            zb = t_den[:, j, 1, k * HH:(k + 1) * HH].unsqueeze(2).to_broadcast([P, HH, HD])
                            dve.tensor_tensor(t_row[:, j, k * P:(k + 1) * P].rearrange("p (h d) -> p h d", d=HD),
                                              att[:, k, 0:P].rearrange("p (h d) -> p h d", d=HD), zb, ALU.mult).then_inc(L2["msg"], 1)
                    l2_q(later)
                    for j, t in enumerate(ts):
                        dve.wait_ge(L2["kept"], t + 3)
                        dve.sem_inc(S["dve_turn"], 1)
                        dve.bn_stats(flat(stats[:, ds(t, 1), :]), flat_b(t)).then_inc(L2["stat"], 1)
                ahead(dve, l2_q, l2)
                dve.wait_ge(L2["stat"], NT)
                norm_stats(dve, s, stats, mean[:, :], var[:, :], rstd[:, :], R1["ready"], R1["rooted"])
                dve.wait_ge(L2["m"], NT)

                def l3_norm(ts):
                    for j, t in enumerate(ts):
                        wait_past(dve, L3["nt"], t - 1)
                        dve.tensor_scalar(t_row[:, j, :], flat_b(t), col(mean, t), col(rstd, t), ALU.subtract,
                                          ALU.mult).then_inc(L3["norm"], 1)

                def hot(t):
                    for h in range(2):
                        c = t * (2 * GB) + h * GB
                        dve.wait_ge(S["hot_used"], t * 2 + (h + 1))
                        dve.tensor_tensor(hot_loc[e, h, :, :], loc_f[e, ds(c, GB)].unsqueeze(2).to_broadcast([EP, GB, P]),
                                          iota[e, 0:P].unsqueeze(1).to_broadcast([EP, GB, P]), ALU.is_equal).then_inc(S["hot_made"], 1)
                        for a, key in enumerate((tile_f, self_f)):
                            dve.tensor_tensor(hot_tile[e, h, :, a, :], key[e, ds(c, GB)].unsqueeze(2).to_broadcast([EP, GB, NT]),
                                              iota[e, 0:NT].unsqueeze(1).to_broadcast([EP, GB, NT]), ALU.is_equal).then_inc(S["hot_made"], 1)

                def l3_stats(ts):
                    for j, t in enumerate(ts):
                        dve.wait_ge(L3["kept"], t + 1)
                        dve.sem_inc(S["dve_turn"], 1)
                        dve.bn_stats(flat(stats[:, ds(t, 1), :]), t_out[:, j, :]).then_inc(L3["stat"], 1)

                def l3(ts, later):
                    l3_norm(later)
                    for t in ts:
                        hot(t)
                    l3_stats(pair_before(ts))
                dve.sem_inc(L3["stat"], 2)
                dve.sem_inc(S["hot_used"], 2)
                ahead(dve, l3_norm, l3)
                l3_stats([NT - 1])
                hot(NT)
                dve.wait_ge(L3["stat"], NT + 2)
                norm_stats(dve, s, stats, mean[:, :], var[:, :], rstd[:, :], R2["ready"], R2["rooted"])
                dve.wait_ge(S["deg_done"], 1)
                s(dve.tensor_copy(degs[:, :, :], bank[7][:, 0:2 * NT].rearrange("p (a b) -> p a b", a=2)))
                s(dve.tensor_scalar(half[:, :], degs[:, 0, :], 1.0, None, ALU.add))
                dve.sem_inc(S["root_in"], 1)
                dve.wait_ge(S["root_done"], 1)
                s(dve.reciprocal(dinv[:, :], half[:, :]))
                s(dve.tensor_scalar(half[:, :], half[:, :], 0.5, None, ALU.mult))
                diag = begin[:, 1, :]
                s(dve.tensor_tensor(to_u[:, 2, :], dinv[:, :], dinv[:, :], ALU.mult))
                s(dve.tensor_tensor(diag, degs[:, 1, :], to_u[:, 2, :], ALU.subtract))
                s(dve.tensor_scalar(diag, diag, 1.0, None, ALU.add))
                s(dve.scalar_tensor_tensor(begin[:, 0, :], half[:, :], -2.0, diag, ALU.mult, ALU.mult))
                s(dve.tensor_scalar(begin[:, 2, :], diag, -4.0, None, ALU.mult))
                for out, by in ((to_t[:, 0, :], -1.0), (to_t[:, 1, :], -2.0), (to_t[:, 2, :], 1.0), (to_u[:, 0, :], 1.0)):
                    s(dve.tensor_scalar(out, dinv[:, :], by, None, ALU.mult))
                s(dve.tensor_scalar(to_u[:, 1, :], to_u[:, 2, :], -1.0, None, ALU.mult))
                s(dve.tensor_scalar(to_u[:, 2, :], to_u[:, 2, :], 4.0, None, ALU.mult))

            @block.tensor
            def _(pe):
                pe.wait_ge(L1["fold"], 1)
                kv = bank[6][:, 0:CK * (P + 1)]
                pe.matmul(kv, zeros[:, :], wkg[:, 0, 0:CK * (P + 1)], start=True, stop=False)
                pe.sem_inc(L1["sum"], 2)

                def turn(src, dst, j):
                    for k in range(CK):
                        ins = pe.transpose(dst[:, k * P:(k + 1) * P], src[:, j, k * P:(k + 1) * P], ident[:, :])
                    return ins

                def times(out, lhs, rhs, n, start=True, stop=True):
                    for k in range(n):
                        ins = pe.matmul(out, lhs(k), rhs(k), start=start and k == 0, stop=stop and k == n - 1)
                    return ins

                def l1_turn(ts):
                    for j, t in enumerate(ts):
                        pe.wait_ge(L1["norm"], t + 1)
                        turn(t_row, bank[j], j).then_inc(L1["xt"], 1)

                def l1(ts, later):
                    for j, t in enumerate(ts):
                        pe.wait_ge(L1["xtc"], t + 1)
                        pe.wait_ge(L1["base"], t + 1)
                        pe.wait_ge(L1["kdone"], t * 2 + 2)
                        times(bank[2 + j][:, :], lambda k: t_col[:, j, k, :], lambda k: wkg[:, k, :], CK).then_inc(L1["kg"], 1)
                        pe.wait_ge(L1["vdone"], t + 1)
                        times(bank[4 + j][:, 0:C], lambda k: t_col[:, j, k, :], lambda k: wv[:, k, :], CK).then_inc(L1["v"], 1)
                    l1_turn(later)
                    for j, t in enumerate(ts):
                        pe.wait_ge(L1["kdone"], t * 2 + 4)
                        pe.wait_ge(L1["vdone"], t + 3)
                        for m in range(CK):
                            ins = pe.matmul(kv[:, m * (P + 1):(m + 1) * (P + 1)], t_k[:, j, m * P:(m + 1) * P], t_v[:, j, m, :],
                                            start=False, stop=False, skip_group_check=True)
                        ins.then_inc(L1["sum"], 1)
                pe.sem_inc(L1["kdone"], 2)
                ahead(pe, l1_turn, l1)
                pe.matmul(kv, zeros[:, :], wkg[:, 0, 0:CK * (P + 1)], start=False, stop=True).then_inc(L1["sum"], 1)
                pe.wait_ge(L2["den"], 1)

                def l2_q(ts):
                    for j, t in enumerate(ts):
                        pe.wait_ge(L2[f"in{j}"], (t - j) * 8 + 16)
                        for m in range(CK):
                            ins = times(bank[j][:, m * P:(m + 1) * P], lambda k: wq[:, k, m * P:(m + 1) * P],
                                        lambda k: t_col[:, j, k, :], CK)
                        ins.then_inc(L2["q"], 1)

                def l2(ts, later):
                    for j, t in enumerate(ts):
                        pe.wait_ge(L2["qdone"], t + 1)
                        for m in range(CK):
                            ins = pe.matmul(bank[2 + j][:, m * (P + HH):(m + 1) * (P + HH)], t_k[:, j, m * P:(m + 1) * P],
                                            kv_bd[:, m, :], start=True, stop=True)
                        ins.then_inc(L2["att"], 1)
                    l2_q(later)
                    for j, t in enumerate(ts):
                        pe.wait_ge(L2["kept"], t + 1)
                        pe.wait_ge(L2["msg"], t * 2 + 2)
                        turn(t_row, bank[4 + j], j).then_inc(L2["mt"], 1)
                    for j, t in enumerate(ts):
                        pe.wait_ge(L2["mtc"], t + 1)
                        times(bank[4 + j][:, C:2 * C], lambda k: t_mt[:, j, k, :], lambda k: wm[:, k, :], CK).then_inc(L2["m"], 1)
                ahead(pe, l2_q, l2)

                d = bank[7][:, 0:2 * NT]
                pe.matmul(d, zeros[:, :], ones[:, 0:2 * NT], start=True, stop=False)

                def degrees(t):
                    for h in range(2):
                        pe.wait_ge(S["hot_made"], t * 6 + (h + 1) * 3)
                        for i in range(GB):
                            ins = pe.matmul(d, hot_loc[e, h, i, :], hot_tile[e, h, i, :, :].rearrange("p a b -> p (a b)"),
                                            start=False, stop=False, skip_group_check=True)
                        ins.then_inc(S["hot_used"], 1)

                def l3_turn(ts):
                    for j, t in enumerate(ts):
                        pe.wait_ge(L3["norm"], t + 1)
                        turn(t_row, bank[j], j).then_inc(L3["nt"], 1)

                def l3(ts, later):
                    for j, t in enumerate(ts):
                        pe.wait_ge(L3[f"in{j}"], (t - j) * 8 + 16)
                        pe.wait_ge(L3["ntc"], t * 2 + 2)
                        for m in range(FK):
                            ins = times(bank[2 + j][:, m * P:(m + 1) * P], lambda k: w1[:, k, m * P:(m + 1) * P],
                                        lambda k: t_col[:, j, k, :] if k < CK else t_mt[:, j, k - CK, :], 2 * CK)
                        ins.then_inc(L3["h"], 1)
                        if j == 0:
                            degrees(t)
                    l3_turn(later)
                    for j, t in enumerate(ts):
                        pe.wait_ge(L3["hc"], t + 1)
                        wait_past(pe, L3["kept"], t - 1)
                        times(bank[4 + j][:, 0:C], lambda k: t_hid[:, j, k, :], lambda k: w2[:, k, :], FK).then_inc(L3["o"], 1)
                        if j == 0 and len(ts) > 1:
                            degrees(ts[1])
                ahead(pe, l3_turn, l3)
                degrees(NT)
                pe.matmul(d, zeros[:, :], ones[:, 0:2 * NT], start=False, stop=True).then_inc(S["deg_done"], 1)


def cheb_block(nc, outer, alloc, v, k):
    iota, ident, cols, locs, chunk_tile, half, to_t, to_u, begin, rows_a, rows_b, bank, edge_list, u_d = (
        v[n] for n in ("iota", "ident", "cols", "locs", "chunk_tile", "half", "to_t", "to_u", "begin", "rows_a",
                       "rows_b", "bank", "edge_list", "u_d"))
    mean, rstd, h2_d = v["mean"], v["rstd"], v["h2_d"]
    cur, acc = (rows_a, rows_b) if k % 2 == 0 else (rows_b, rows_a)
    base_in, base_out = (v["base2_d"], v["base_d"]) if k == 1 else (v["base_d"], v["base2_d"])
    HALVES = NCH // G
    with ExitStack() as ctx:
        sb, sem_ = alloc(ctx, f"cheb{k}_")
        sem = lambda n: sem_(f"c{k}_{n}")
        list_i = sb("list_i", [P, NCH], I32) if k == 0 else None
        part_i = sb("part_i", [P, NCH], I32) if k == 0 else None
        ring_idx = sb("ring_idx", [P, 2, G], U32)
        rows = sb("rows", [P, 2, G, C])
        hot = sb("hot", [P, 2, G, P])
        more = sb("more", [P, 2, GU, C])
        BY_DVE = range(1, NG, 2)
        stage = [rows[:, 0, 0:GU, :], rows[:, 1, 0:GU, :], more[:, 0, :, :], more[:, 1, :, :]]
        wt = sb("wt", [P, CK, C])
        t_row = sb("t_row", [P, C])
        t_col = sb("t_col", [P, CK, P])
        t_base = sb("t_base", [P, 2, C])
        t_h2 = sb("t_h2", [P, C]) if k == 0 else None
        t_n = sb("t_n", [P, 2, C]) if k == 0 else None
        gain = sb("gain", [P, C]) if k == 0 else None
        bias = sb("bias", [P, 2, C]) if k == 0 else None
        S = {n: sem(n) for n in ("listed ready gathered0 gathered1 copied pool_turn hot_made scattered added "
                                 "copied_row turned turned_col times base_in base_made base_out w_in act_turn "
                                 "u_by_act u_by_dve u_out0 u_out1 u_out2 u_out3 begun halved n0 n1 n2 n3 steps").split()}
        rowtile = lambda d, t: d.rearrange("(t p) c -> t p c", p=P)[ds(t, 1)].rearrange("a p c -> (a p) c")
        tile_of = lambda rows_, t: flat(rows_[:, ds(t, 1), :])
        SPARE = 3
        tiles = NT

        def chunk_count(kind):
            _, (n,) = nc.values_load_multi_w_load_instructions(v["chunks"][0:1, 0:1], engines=[kind], min_val=0, max_val=NCH)
            return n

        def when_used(eng, count, n, work):
            with eng.If(count > n * G):
                work()

        def turns(eng, kind, body, half):
            with eng.Fori(0, tiles) as it:
                body(it, True)
            with eng.Fori(tiles, HALVES // 2 - 2) as it:
                body(it, False)
            count = chunk_count(kind)
            half(HALVES - 4, 0)
            for n in range(HALVES - SPARE, HALVES):
                when_used(eng, count, n, lambda: half(n, n % 2))

        with nc.Block() as block:
            @block.sync
            def _(sp):
                if k == 0:
                    sp.dma_start(list_i[:, :], edge_list.rearrange("(p c) -> p c", p=P)).then_inc(S["listed"], 16)
                    w = S["w_in"]
                    sp.dma_start(gain[:, :], v["g2"].rearrange("(a n) -> a n", a=1).to_broadcast([P, C])).then_inc(w, 16)
                    sp.dma_start(bias[:, 0, :], v["gnn_b"].rearrange("(a n) -> a n", a=1).to_broadcast([P, C])).then_inc(w, 16)
                    sp.dma_start(bias[:, 1, :], v["b2"].rearrange("(a n) -> a n", a=1).to_broadcast([P, C])).then_inc(w, 16)
                else:
                    sp.dma_start(wt[:, :, :], v["gnn_w"][k].rearrange("(k p) n -> p k n", p=P)).then_inc(S["w_in"], 16)

                for g in range(NG):
                    if g in BY_DVE:
                        sp.wait_ge(S["u_by_dve"], (g // 2 + 1) * GU)
                    else:
                        sp.wait_ge(S["u_by_act"], (g // 2 + 1) * GU)
                    dst = u_d[k][g * GU * P:(g + 1) * GU * P].rearrange("(t p) c -> p t c", p=P)
                    sp.dma_start(dst, stage[g % 4]).then_inc(S[f"u_out{g % 4}"], 16)

                def load(t):
                    sp.dma_start(t_base[:, 0, :], rowtile(base_in, t)).then_inc(S["base_in"], 16)
                    if k == 0:
                        sp.dma_start(t_h2[:, :], rowtile(h2_d, t)).then_inc(S["base_in"], 16)
                load(0)

                def store_sum(t):
                    sp.wait_ge(S["base_made"], t + 2)
                    sp.dma_start(rowtile(base_out, t), t_base[:, 1, :]).then_inc(S["base_out"], 16)
                    sp.wait_ge(S["base_out"], t * 16 + 16)
                with sp.Fori(0, tiles - 1) as t:
                    store_sum(t)
                    load(t + 1)
                store_sum(tiles - 1)

            @block.gpsimd
            def _(pool):
                for j in range(4):
                    pool.wait_ge(S[f"u_out{j}"], 16 * len(range(j, NG, 4)))
                pool.sem_inc(S["scattered"], 2 * G)

                def half(n, h):
                    pool.wait_ge(S["scattered"], (n + 1) * G)
                    pool.wait_ge(S["copied"], n + 1)
                    pool.sem_inc(S["pool_turn"], 1)
                    for i in range(G):
                        pool.indirect_dma_start(rows[:, h, i, :], None, u_d[k],
                                                bass.IndirectOffsetOnAxis(ap=ring_idx[:, h, i:i + 1], axis=0)
                                                ).then_inc(S[f"gathered{h}"], 16)

                def turn(it, _):
                    for h in range(2):
                        half(it * 2 + h, h)
                turns(pool, mybir.EngineType.Pool, turn, half)

            @block.scalar
            def _(act):
                for g in range(0, NG, 2):
                    if g >= 4:
                        act.wait_ge(S[f"u_out{g % 4}"], 16 * (g // 4))
                    for i in range(GU):
                        t = g * GU + i
                        act.activation(stage[g % 4][:, i, :], cur[:, t, :], ACT.Copy, scale=to_u[:, k, t:t + 1]).then_inc(S["u_by_act"], 1)
                act.wait_ge(S["ready"], 1)

                def ring(n, h, first=False):
                    if not first:
                        act.wait_ge(S[f"gathered{h}"], (n - h) * (8 * G))
                        act.sem_inc(S["act_turn"], 1)
                    act.copy(ring_idx[:, h, :], cols[:, ds(n * G, G)]).then_inc(S["copied"], 1)

                def turn(it, with_tile, first=False):
                    ring(it * 2, 0, first)
                    if with_tile and k:
                        act.wait_ge(S["turned"], it + 1)
                        act.sem_inc(S["act_turn"], 1)
                        act.activation(t_row[:, :], tile_of(cur, it), ACT.Copy, scale=to_t[:, k - 1, ds(it, 1)]).then_inc(S["copied_row"], 1)
                    ring(it * 2 + 1, 1, first)
                    if with_tile and k:
                        act.wait_ge(S["turned"], it + 2)
                        act.copy(t_col[:, :, :].rearrange("p k n -> p (k n)"), bank[4][:, 0:C]).then_inc(S["turned_col"], 1)
                turn(0, True, True)
                with act.Fori(1, tiles) as it:
                    turn(it, True)
                with act.Fori(tiles, HALVES // 2 - 2) as it:
                    turn(it, False)
                count = chunk_count(mybir.EngineType.Activation)
                ring(HALVES - 4, 0)
                for n in range(HALVES - SPARE, HALVES):
                    when_used(act, count, n, lambda: ring(n, n % 2))

            @block.vector
            def _(dve):
                s = Chain(dve, S["steps"]).step
                for g in BY_DVE:
                    if g >= 4:
                        dve.wait_ge(S[f"u_out{g % 4}"], 16 * (g // 4))
                    for i in range(GU):
                        t = g * GU + i
                        dve.tensor_scalar(stage[g % 4][:, i, :], cur[:, t, :], to_u[:, k, t:t + 1], None, ALU.mult).then_inc(S["u_by_dve"], 1)
                if k == 0:
                    dve.wait_ge(S["listed"], 16)
                    s(dve.tensor_scalar(part_i[:, :], list_i[:, :], (1 << LOC_SHIFT) - 1, None, ALU.bitwise_and))
                    s(dve.tensor_copy(cols[:, :], part_i[:, :]))
                    s(dve.tensor_scalar(part_i[:, :], list_i[:, :], LOC_SHIFT, None, ALU.arith_shift_right))
                    s(dve.tensor_copy(locs[:, :], part_i[:, :]))
                dve.sem_inc(S["ready"], 1)
                if k == 0:
                    dve.wait_ge(S["w_in"], 48)
                    s(dve.tensor_tensor(bias[:, 0, :], bias[:, 0, :], bias[:, 1, :], ALU.add))

                with dve.Fori(0, NG) as g:
                    for i in range(GU):
                        t = g * GU + i
                        if k:
                            dve.scalar_tensor_tensor(tile_of(acc, t), tile_of(cur, t), begin[:, k, ds(t, 1)], tile_of(acc, t),
                                                     ALU.mult, ALU.add).then_inc(S["begun"], 1)
                        else:
                            dve.tensor_scalar(tile_of(acc, t), tile_of(cur, t), begin[:, 0, ds(t, 1)], None, ALU.mult).then_inc(S["begun"], 1)
                dve.wait_ge(S["begun"], NT)
                if k == 0:
                    dve.wait_ge(S["u_by_act"], NT - len(BY_DVE) * GU)
                    dve.wait_ge(S["u_by_dve"], len(BY_DVE) * GU)

                def tile_sum(t):
                    if k:
                        dve.wait_ge(S["base_in"], t * 16 + 16)
                        dve.wait_ge(S["times"], t + 1)
                        dve.tensor_tensor(t_base[:, 1, :], t_base[:, 0, :], bank[5][:, 0:C], ALU.add).then_inc(S["base_made"], 1)
                        return
                    dve.tensor_scalar(tile_of(cur, t), tile_of(cur, t), half[:, ds(t, 1)], None, ALU.mult).then_inc(S["halved"], 1)
                    dve.wait_ge(S["base_in"], t * 32 + 32)
                    dve.tensor_scalar(t_n[:, 0, :], t_h2[:, :], mean[:, ds(t, 1)], rstd[:, ds(t, 1)], ALU.subtract,
                                      ALU.mult).then_inc(S["n0"], 1)
                    dve.tensor_tensor(t_base[:, 0, :], t_base[:, 0, :], bias[:, 0, :], ALU.add).then_inc(S["n1"], 1)
                    dve.wait_ge(S["n0"], t + 1)
                    dve.tensor_tensor(t_n[:, 1, :], t_n[:, 0, :], gain[:, :], ALU.mult).then_inc(S["n2"], 1)
                    dve.wait_ge(S["n1"], t + 1)
                    dve.wait_ge(S["n2"], t + 1)
                    dve.tensor_tensor(t_base[:, 1, :], t_base[:, 0, :], t_n[:, 1, :], ALU.add).then_inc(S["base_made"], 1)
                    dve.wait_ge(S["base_made"], t + 2)

                def make_hot(n, h):
                    dve.wait_ge(S["scattered"], (n + 1) * G)
                    dve.tensor_tensor(hot[:, h, :, :], locs[:, ds(n * G, G)].unsqueeze(2).to_broadcast([P, G, P]),
                                      iota[:, 0:P].unsqueeze(1).to_broadcast([P, G, P]), ALU.is_equal).then_inc(S["hot_made"], 1)

                def add(n):
                    _, regs = nc.values_load_multi_w_load_instructions(
                        chunk_tile[0:1, ds(n * G, G)], engines=[mybir.EngineType.DVE], min_val=0, max_val=NT - 1)
                    for i in range(G):
                        if i % 2 == 0:
                            dve.wait_ge(S["scattered"], n * G + 2 * G + i + 2)
                        dve.wait_ge(S["added"], n * G + 8 + i)
                        a = tile_of(acc, regs[i])
                        dve.tensor_tensor(a, a, bank[i // 2][:, (i % 2) * C:(i % 2 + 1) * C], ALU.add).then_inc(S["added"], 1)

                def turn(it, with_tile):
                    make_hot(it * 2 + 1, 1)
                    if with_tile:
                        tile_sum(it)
                    add(it * 2)
                    make_hot(it * 2 + 2, 0)
                    add(it * 2 + 1)
                make_hot(0, 0)
                with dve.Fori(0, tiles) as it:
                    turn(it, True)
                with dve.Fori(tiles, HALVES // 2 - 2) as it:
                    turn(it, False)
                count = chunk_count(mybir.EngineType.DVE)
                add(HALVES - 4)
                dve.wait_ge(S["added"], (HALVES - SPARE) * G + 8)

                def spare(n):
                    make_hot(n, n % 2)
                    add(n)
                    dve.wait_ge(S["added"], (n + 1) * G + 8)
                for n in range(HALVES - SPARE, HALVES):
                    when_used(dve, count, n, lambda: spare(n))

            @block.tensor
            def _(pe):
                pe.sem_inc(S["added"], 8)
                pe.sem_inc(S["base_made"], 1)
                if k:
                    pe.wait_ge(S["w_in"], 16)
                    pe.sem_inc(S["turned"], 1)

                def turn(it, with_tile):
                    if with_tile and k:
                        pe.wait_ge(S["copied_row"], it + 1)
                        for c in range(CK):
                            ins = pe.transpose(bank[4][:, c * P:(c + 1) * P], t_row[:, c * P:(c + 1) * P], ident[:, :])
                        ins.then_inc(S["turned"], 1)
                        pe.wait_ge(S["turned_col"], it + 1)
                        pe.wait_ge(S["base_made"], it + 1)
                        for c in range(CK):
                            ins = pe.matmul(bank[5][:, 0:C], t_col[:, c, :], wt[:, c, :], start=c == 0, stop=c == CK - 1)
                        ins.then_inc(S["times"], 1)
                    for h in range(2):
                        half(it * 2 + h, h)

                def half(n, h):
                    pe.wait_ge(S["hot_made"], n + 1)
                    pe.wait_ge(S[f"gathered{h}"], (n - h) * (8 * G) + 16 * G)
                    for i in range(G):
                        if i % 2 == 0:
                            pe.wait_ge(S["added"], n * G + i + 2)
                        pe.matmul(bank[i // 2][:, (i % 2) * C:(i % 2 + 1) * C], hot[:, h, i, :], rows[:, h, i, :],
                                  start=True, stop=True).then_inc(S["scattered"], 1)
                turns(pe, mybir.EngineType.PE, turn, half)


def gate_block(nc, outer, alloc, v):
    iota, ones, ident, before, valid, rows_a, rows_b, bank = (
        v[n] for n in ("iota", "ones", "ident", "before", "valid", "rows_a", "rows_b", "bank"))
    slot_i, tile_expert, mean, var, rstd = (v[n] for n in ("slot_i", "tile_expert", "mean", "var", "rstd"))
    sum3, x1, normed = rows_b, rows_a, rows_b
    with ExitStack() as ctx:
        sb, sem_ = alloc(ctx, "gate_")
        sem = lambda n: sem_("g_" + n)
        wt = sb("wt", [P, CK, C])
        wgate = sb("wgate", [P, CK, NE])
        bgate = sb("bgate", [P, NE])
        eb2 = sb("eb2", [GU * NE, GU, C])
        stats = sb("stats", [P, NT, 6])
        t_row = sb("row", [P, 2, C])
        t_col = sb("col", [P, 2, CK, P])
        t_base = sb("base", [P, 2, C])
        t_x = sb("x", [P, 2, C])
        x_col = sb("x_col", [P, 2, CK, P])
        wsum = sb("wsum", [P, NE])
        shift = sb("shift", [P, NT])
        out = sb("out", [P, 2, GU, C])
        logits = sb("logits", [P, NT, NE])
        down = sb("down", [P, NE])
        best = sb("best", [P, 2, NT])
        rank = sb("rank", [P, NT])
        pick = sb("pick", [P, 2, NT, NE])
        both = sb("both", [P, NT, NE])
        place = logits
        tot = sb("tot", [P, NE, NT])
        upto = sb("upto", [P, NE, NT])
        small = sb("small", [P, 6, NE])
        small_i = sb("small_i", [P, NE], I32)
        first_t = sb("first_t", [NE, 1])
        tab = sb("tab", [NE, MT])
        dump_i = sb("dump_i", [P, 1], I32)
        dump = sb("dump", [P, 1])
        inval = sb("inval", [P, NT])
        slot = sb("slot", [P, 2, NT])
        tmp = sb("tmp", [P, NT, NE])
        w_row = sb("wrow", [P, 2, GU * NE])
        w_col = sb("wcol", [GU * NE, 2, P])
        gate_w2 = sb("gate_w2", [P, 2, NT])
        row_i = sb("row_i", [P, NT], I32)
        row_f = sb("row_f", [P, NT])
        ring = sb("ring", [P, 2, 2, GU, CX])
        ring_i = sb("ring_i", [P, 2, 2, GU], I32)
        S = {n: sem(n) for n in (
            "weighed wts zeroed base_in0 base_in1 copied turned turned_col times x1 stat steps var_ready rooted act_turn dve_turn "
            "xt xtc lg lgc wsum shifted normed x1_out all ready exp_in exp_done slots_ready pool_turn rings "
            "pool_copied scattered0 scattered1 wr wt wtc b2 out0 out1 outm dump kept first ind tabs").split()}
        rowtile = lambda d, t: d.rearrange("(t p) c -> t p c", p=P)[ds(t, 1)].rearrange("a p c -> (a p) c")
        group = lambda d, g: d.rearrange("(g t p) c -> p g t c", p=P, t=GU)[:, ds(g, 1)].rearrange("p a t c -> p (a t) c")
        tile_of = lambda rows_, t: flat(rows_[:, ds(t, 1), :])
        CUT = (0, NT // 2 + 1, NT)

        with nc.Block() as block:
            @block.sync
            def _(sp):
                kpc = lambda a: a.rearrange("(k p) n -> p k n", p=P)

                def load(ts):
                    for j, t in enumerate(ts):
                        wait_past(sp, S["x1"], t - 1)
                        sp.dma_start(t_base[:, j, :], rowtile(v["base2_d"], t)).then_inc(S[f"base_in{j}"], 16)
                sp.dma_start(wt[:, :, :], kpc(v["gnn_w"][3])).then_inc(S["wts"], 16)
                load([0, 1])
                sp.dma_start(wgate[:, :, :], kpc(v["gate_w"])).then_inc(S["wts"], 16)
                sp.dma_start(bgate[:, :], v["gate_b"].rearrange("(a n) -> a n", a=1).to_broadcast([P, NE])).then_inc(S["wts"], 16)
                sp.wait_ge(S["zeroed"], 1)
                for i in range(GU):
                    sp.dma_start(eb2[i * NE:(i + 1) * NE, i, :], v["eb2"]).then_inc(S["wts"], 16)
                ahead(sp, lambda ts: None, lambda ts, later: load(later))
                sp.wait_ge(S["kept"], NT)
                sp.dma_start(v["x1_d"].rearrange("(t p) c -> p t c", p=P), x1[:, :, :]).then_inc(S["x1_out"], 16)

                def store(gs):
                    for j, g in enumerate(gs):
                        sp.wait_ge(S["outm"], g * 4 + 8)
                        sp.dma_start(group(v["xg_d"][0:NP], g), out[:, j, :, :]).then_inc(S[f"out{j}"], 16)
                pairs(sp, store, NG)
                for j in range(2):
                    sp.wait_ge(S[f"out{j}"], 16 * (NG // 2 + 1 - j))
                sp.wait_ge(S["x1_out"], 16)

            @block.gpsimd
            def _(pool):
                pool.memset(eb2[:, :, :], 0.0).then_inc(S["zeroed"], 1)
                pool.iota(dump_i[:, :], pattern=[[0, 1]], base=MT * P, channel_multiplier=1).then_inc(S["dump"], 1)
                pool.iota(row_i[:, :], pattern=[[P, NT]], base=0, channel_multiplier=1).then_inc(S["dump"], 1)
                pool.wait_ge(S["slots_ready"], 1)

                def scatter(gs):
                    for j, g in enumerate(gs):
                        wait_past(pool, S[f"scattered{j}"], (g - j) * (16 * GU))
                        pool.sem_inc(S["pool_turn"], 1)
                        for a in range(2):
                            pool.tensor_copy(ring_i[:, j, a, :], slot_i[:, a, ds(g * GU, GU)]).then_inc(S["pool_copied"], 1)
                        pool.wait_ge(S["pool_copied"], g * 2 + 2)
                        pool.wait_ge(S["rings"], g * 6 + 6)
                        pool.sem_inc(S["pool_turn"], 1)
                        for i in range(GU):
                            for a in range(2):
                                pool.indirect_dma_start(
                                    v["slots_in"], bass.IndirectOffsetOnAxis(ap=ring_i[:, j, a, i:i + 1].bitcast(U32), axis=0),
                                    ring[:, j, a, i, :], None).then_inc(S[f"scattered{j}"], 16)
                pairs(pool, scatter, NG)
                for j in range(2):
                    pool.wait_ge(S[f"scattered{j}"], 32 * GU * (NG // 2 + 1 - j))

            @block.scalar
            def _(act):
                def first(ts):
                    for j, t in enumerate(ts):
                        copy_t3(j, t)
                        keep_col(j, t)

                def copy_t3(j, t):
                    wait_past(act, S["turned"], t - 1)
                    act.sem_inc(S["act_turn"], 1)
                    act.activation(t_row[:, j, :], tile_of(sum3, t), ACT.Copy,
                                   scale=v["to_t"][:, 2, ds(t, 1)]).then_inc(S["copied"], 1)

                def keep_col(j, t):
                    act.wait_ge(S["turned"], t + 1)
                    act.copy(t_col[:, j, :, :].rearrange("p k n -> p (k n)"), bank[j][:, 0:C]).then_inc(S["turned_col"], 1)

                def keep_x_col(ts):
                    for j, t in enumerate(ts):
                        act.wait_ge(S["xt"], t + 1)
                        act.copy(x_col[:, j, :, :].rearrange("p k n -> p (k n)"), bank[4 + j][:, 0:C]).then_inc(S["xtc"], 1)

                def g1(ts, later):
                    for j, t in enumerate(later):
                        copy_t3(j, t)
                    keep_x_col(pair_before(ts))
                    for j, t in enumerate(later):
                        keep_col(j, t)
                    for j, t in enumerate(ts):
                        act.wait_ge(S["x1"], t + 1)
                        act.sem_inc(S["act_turn"], 1)
                        act.copy(tile_of(x1, t), t_x[:, j, :]).then_inc(S["kept"], 1)
                ahead(act, first, g1)
                keep_x_col([NT - 1])
                act.wait_ge(S["var_ready"], 1)
                act.activation(var[:, :], var[:, :], ACT.Sqrt).then_inc(S["rooted"], 1)
                act.wait_ge(S["kept"], NT)
                act.wait_ge(S["shifted"], 1)
                act.wait_ge(S["copied"], NT)
                with act.Fori(0, NG) as g:
                    for i in range(GU):
                        t = g * GU + i
                        act.activation(tile_of(normed, t), tile_of(x1, t), ACT.Identity, scale=rstd[:, ds(t, 1)],
                                       bias=shift[:, ds(t, 1)]).then_inc(S["normed"], 1)
                act.wait_ge(S["exp_in"], 1)
                act.activation(best[:, 1, :], best[:, 1, :], ACT.Exp).then_inc(S["exp_done"], 1)

                act.wait_ge(S["normed"], NT)
                act.wait_ge(S["weighed"], 1)

                def fill(gs):
                    for j, g in enumerate(gs):
                        wait_past(act, S[f"scattered{j}"], (g - j) * (16 * GU))
                        act.sem_inc(S["act_turn"], 1)
                        some = ds(g * GU, GU)
                        for a in range(2):
                            act.copy(ring[:, j, a, :, 0:C], normed[:, some, :]).then_inc(S["rings"], 1)
                            act.copy(ring[:, j, a, :, C:C + 1], row_f[:, some].unsqueeze(2)).then_inc(S["rings"], 1)
                            act.copy(ring[:, j, a, :, C + 1:CX], gate_w2[:, a, some].unsqueeze(2)).then_inc(S["rings"], 1)
                        act.wait_ge(S["wt"], g + 1)
                        act.copy(w_col[:, j, :], bank[j][0:GU * NE, 0:P]).then_inc(S["wtc"], 1)
                pairs(act, fill, NG)

            @block.vector
            def _(dve):
                s = Chain(dve, S["steps"]).step

                def keep_logits(ts):
                    for j, t in enumerate(ts):
                        dve.wait_ge(S["lg"], t + 1)
                        dve.tensor_scalar(flat(logits[:, ds(t, 1), :]), bank[6 + j][:, 0:NE], 1.0, None, ALU.mult).then_inc(S["lgc"], 1)

                def g1(ts):
                    for j, t in enumerate(ts):
                        wait_past(dve, S["kept"], t - 1)
                        wait_past(dve, S["xt"], t - 1)
                        wait_past(dve, S["stat"], t - 1)
                        dve.wait_ge(S[f"base_in{j}"], (t - j) * 8 + 16)
                        dve.wait_ge(S["times"], t + 1)
                        dve.tensor_tensor(t_x[:, j, :], t_base[:, j, :], bank[2 + j][:, 0:C], ALU.add).then_inc(S["x1"], 1)
                    for j, t in enumerate(ts):
                        dve.wait_ge(S["x1"], t + 1)
                        dve.sem_inc(S["dve_turn"], 1)
                        dve.bn_stats(flat(stats[:, ds(t, 1), :]), t_x[:, j, :]).then_inc(S["stat"], 1)
                    keep_logits(pair_before(ts))
                dve.sem_inc(S["lgc"], 2)
                pairs(dve, g1)
                dve.wait_ge(S["stat"], NT)
                norm_stats(dve, s, stats, mean[:, :], var[:, :], rstd[:, :], S["var_ready"], S["rooted"])
                s(dve.scalar_tensor_tensor(shift[:, :], mean[:, :], -1.0, rstd[:, :], ALU.mult, ALU.mult))
                dve.sem_inc(S["shifted"], 1)
                keep_logits([NT - 1])
                dve.wait_ge(S["wts"], 16 * (3 + GU))
                dve.wait_ge(S["lgc"], NT + 2)
                wide = lambda a: a.unsqueeze(2).to_broadcast([P, NT, NE])
                every = lambda a: a.unsqueeze(1).to_broadcast([P, NT, NE])
                dve.wait_ge(S["wsum"], 1)
                s(dve.tensor_copy(wsum[:, :], bank[0][:, 0:NE]))
                s(dve.tensor_tensor(tmp[:, :, :], every(wsum[:, :]), wide(mean[:, :]), ALU.mult))
                s(dve.tensor_tensor(logits[:, :, :], logits[:, :, :], tmp[:, :, :], ALU.subtract))
                s(dve.tensor_tensor(logits[:, :, :], logits[:, :, :], wide(rstd[:, :]), ALU.mult))
                s(dve.tensor_tensor(logits[:, :, :], logits[:, :, :], every(bgate[:, :]), ALU.add))
                s(dve.tensor_scalar(down[:, :], iota[:, 0:NE], -1.0, float(NE), ALU.mult, ALU.add))
                for a in range(2):
                    s(dve.tensor_reduce(best[:, a, :], logits[:, :, :], AX_X, ALU.max))
                    s(dve.tensor_tensor(tmp[:, :, :], logits[:, :, :], wide(best[:, a, :]), ALU.is_equal))
                    s(dve.tensor_tensor(tmp[:, :, :], tmp[:, :, :], every(down[:, :]), ALU.mult))
                    s(dve.tensor_reduce(rank[:, :], tmp[:, :, :], AX_X, ALU.max))
                    s(dve.tensor_tensor(pick[:, a, :, :], every(down[:, :]), wide(rank[:, :]), ALU.is_equal))
                    if a == 0:
                        s(dve.scalar_tensor_tensor(logits[:, :, :], pick[:, 0, :, :], -3e38, logits[:, :, :], ALU.mult, ALU.add))
                s(dve.tensor_tensor(both[:, :, :], pick[:, 0, :, :], pick[:, 1, :, :], ALU.add))
                s(dve.tensor_tensor(both[:, :, :], both[:, :, :], wide(valid[:, :]), ALU.mult))
                dve.sem_inc(S["all"], 1)
                s(dve.tensor_tensor(best[:, 1, :], best[:, 1, :], best[:, 0, :], ALU.subtract))
                dve.sem_inc(S["exp_in"], 1)
                dve.wait_ge(S["ready"], 1)
                for i in range(2):
                    t0, t1 = CUT[i], CUT[i + 1]
                    w = (t1 - t0) * NE
                    s(dve.tensor_copy(tot[:, :, t0:t1], bank[2 + i][:, 0:w].rearrange("p (t e) -> p e t", e=NE)))
                s(dve.tensor_tensor_scan(upto[:, :, :].rearrange("p e t -> p (e t)"), ones[:, 0:1].to_broadcast([P, NE * NT]),
                                         tot[:, :, :].rearrange("p e t -> p (e t)"), 0.0, ALU.mult, ALU.add))
                s(dve.memset(small[:, 0, 0:1], 0.0))
                s(dve.tensor_copy(small[:, 0, 1:NE], upto[:, 0:NE - 1, NT - 1]))
                s(dve.tensor_tensor(small[:, 1, :], upto[:, :, NT - 1], small[:, 0, :], ALU.subtract))
                s(dve.tensor_scalar(small[:, 1, :], small[:, 1, :], float(P - 1), None, ALU.add))
                s(dve.tensor_copy(small_i[:, :], small[:, 1, :]))
                s(dve.tensor_scalar(small_i[:, :], small_i[:, :], 7, None, ALU.arith_shift_right))
                s(dve.tensor_copy(small[:, 2, :], small_i[:, :]))
                s(dve.tensor_tensor_scan(small[:, 3, :], ones[:, 0:NE], small[:, 2, :], 0.0, ALU.mult, ALU.add))
                s(dve.tensor_tensor(small[:, 4, :], small[:, 3, :], small[:, 2, :], ALU.subtract))
                dve.sem_inc(S["first"], 1)
                s(dve.tensor_copy(v["tiles_used"][0:1, :], small[0:1, 3, NE - 1:NE]))
                dve.wait_ge(S["exp_done"], 1)
                s(dve.tensor_scalar(best[:, 0, :], best[:, 1, :], 1.0, None, ALU.add))
                s(dve.reciprocal(gate_w2[:, 0, :], best[:, 0, :]))
                s(dve.tensor_tensor(gate_w2[:, 1, :], gate_w2[:, 0, :], best[:, 1, :], ALU.mult))
                dve.wait_ge(S["dump"], 2)
                s(dve.tensor_copy(row_f[:, :], row_i[:, :]))
                dve.sem_inc(S["weighed"], 1)
                s(dve.scalar_tensor_tensor(small[:, 5, :], small[:, 4, :], float(P), small[:, 0, :], ALU.mult, ALU.subtract))
                s(dve.tensor_tensor(upto[:, :, :], upto[:, :, :], tot[:, :, :], ALU.subtract))
                s(dve.tensor_tensor(upto[:, :, :], upto[:, :, :], small[:, 5, :].unsqueeze(2).to_broadcast([P, NE, NT]), ALU.add))
                for i in range(2):
                    t0, t1 = CUT[i], CUT[i + 1]
                    w = (t1 - t0) * NE
                    s(dve.tensor_tensor(place[:, t0:t1, :], bank[i][:, 0:w].rearrange("p (t e) -> p t e", e=NE),
                                        upto[:, :, t0:t1].rearrange("p e t -> p t e"), ALU.add))
                s(dve.tensor_copy(dump[:, :], dump_i[:, :]))
                s(dve.tensor_scalar(inval[:, :], valid[:, :], -1.0, 1.0, ALU.mult, ALU.add))
                for a in range(2):
                    s(dve.tensor_tensor(tmp[:, :, :], pick[:, a, :, :], place[:, :, :], ALU.mult))
                    s(dve.tensor_reduce(slot[:, a, :], tmp[:, :, :], AX_X, ALU.add))
                    s(dve.tensor_tensor(slot[:, a, :], slot[:, a, :], valid[:, :], ALU.mult))
                    s(dve.scalar_tensor_tensor(slot[:, a, :], inval[:, :], dump[:, 0:1], slot[:, a, :], ALU.mult, ALU.add))
                    s(dve.tensor_scalar(dump[:, :], dump[:, :], -64.0, None, ALU.add))
                    s(dve.tensor_copy(slot_i[:, a, :], slot[:, a, :]))
                dve.sem_inc(S["slots_ready"], 1)
                dve.wait_ge(S["tabs"], 1)
                s(dve.tensor_copy(first_t[:, :], bank[4][0:NE, 0:1]))
                s(dve.tensor_scalar(tab[:, :], iota[0:NE, 0:MT], first_t[:, 0:1], None, ALU.is_ge))
                dve.sem_inc(S["ind"], 1)
                dve.wait_ge(S["tabs"], 2)
                s(dve.tensor_scalar(tile_expert[0:1, :], bank[5][0:1, 0:MT], -1.0, None, ALU.add))
                for a in range(2):
                    s(dve.tensor_tensor(pick[:, a, :, :], pick[:, a, :, :], wide(gate_w2[:, a, :]), ALU.mult))
                s(dve.tensor_tensor(both[:, :, :], pick[:, 0, :, :], pick[:, 1, :, :], ALU.add))

                def add_b2(gs):
                    for j, g in enumerate(gs):
                        wait_past(dve, S["wt"], g - 1)
                        dve.tensor_scalar(w_row[:, j, :], both[:, ds(g * GU, GU), :].rearrange("p t e -> p (t e)"), 1.0, None,
                                          ALU.mult).then_inc(S["wr"], 1)
                    for j, g in enumerate(gs):
                        wait_past(dve, S[f"out{j}"], (g - j) * 8)
                        for q in range(4):
                            n = min(2, GU - 2 * q)
                            dve.wait_ge(S["b2"], g * 4 + (q + 1))
                            dve.tensor_tensor(out[:, j, 2 * q:2 * q + n, :], normed[:, ds(g * GU + 2 * q, n), :],
                                              bank[4 + q][:, 0:n * C].rearrange("p (t c) -> p t c", c=C), ALU.add).then_inc(S["outm"], 1)
                dve.sem_inc(S["outm"], 4)
                pairs(dve, add_b2, NG)

            @block.tensor
            def _(pe):
                pe.wait_ge(S["wts"], 16 * (3 + GU))

                def turn(dst, src, j):
                    for k in range(CK):
                        ins = pe.transpose(dst[:, k * P:(k + 1) * P], src[:, j, k * P:(k + 1) * P], ident[:, :])
                    return ins

                def turn_t3(j, t):
                    pe.wait_ge(S["copied"], t + 1)
                    turn(bank[j], t_row, j).then_inc(S["turned"], 1)

                def turn_x(ts):
                    for j, t in enumerate(ts):
                        pe.wait_ge(S["x1"], t + 1)
                        turn(bank[4 + j], t_x, j).then_inc(S["xt"], 1)

                def gate(ts):
                    for j, t in enumerate(ts):
                        pe.wait_ge(S["xtc"], t + 1)
                        pe.wait_ge(S["lgc"], t + 1)
                        for k in range(CK):
                            ins = pe.matmul(bank[6 + j][:, 0:NE], x_col[:, j, k, :], wgate[:, k, :], start=k == 0, stop=k == CK - 1)
                        ins.then_inc(S["lg"], 1)

                def g1(ts, later):
                    turn_x(pair_before(ts))
                    for j, t in enumerate(ts):
                        pe.wait_ge(S["turned_col"], t + 1)
                        wait_past(pe, S["x1"], t - 1)
                        for k in range(CK):
                            ins = pe.matmul(bank[2 + j][:, 0:C], t_col[:, j, k, :], wt[:, k, :], start=k == 0, stop=k == CK - 1)
                        ins.then_inc(S["times"], 1)
                        if j < len(later):
                            turn_t3(j, later[j])
                    gate(pair_before(ts))
                ahead(pe, lambda ts: [turn_t3(j, t) for j, t in enumerate(ts)], g1)
                turn_x([NT - 1])
                gate([NT - 1])
                pe.wait_ge(S["turned_col"], NT)
                for k in range(CK):
                    ins = pe.matmul(bank[0][:, 0:NE], ones[:, :], wgate[:, k, :], start=k == 0, stop=k == CK - 1)
                ins.then_inc(S["wsum"], 1)
                pe.wait_ge(S["all"], 1)
                for i in range(2):
                    w = (CUT[i + 1] - CUT[i]) * NE
                    some = both[:, CUT[i]:CUT[i + 1], :].rearrange("p t e -> p (t e)")
                    pe.matmul(bank[i][:, 0:w], before[:, :], some, start=True, stop=True)
                    ins = pe.matmul(bank[2 + i][:, 0:w], ones[:, :], some, start=True, stop=True)
                ins.then_inc(S["ready"], 1)
                pe.wait_ge(S["first"], 1)
                pe.transpose(bank[4][0:NE, 0:P], small[:, 4, :], ident[:, :]).then_inc(S["tabs"], 1)
                pe.wait_ge(S["ind"], 1)
                pe.matmul(bank[5][0:1, 0:MT], ones[0:NE, 0:1], tab[:, :], start=True, stop=True).then_inc(S["tabs"], 1)

                def times_b2(gs):
                    for j, g in enumerate(gs):
                        pe.wait_ge(S["wr"], g + 1)
                        pe.transpose(bank[j][0:GU * NE, 0:P], w_row[:, j, :], ident[:, :]).then_inc(S["wt"], 1)
                    for j, g in enumerate(gs):
                        pe.wait_ge(S["wtc"], g + 1)
                        for q in range(4):
                            n = min(2, GU - 2 * q)
                            pe.wait_ge(S["outm"], g * 4 + (q + 1))
                            pe.matmul(bank[4 + q][:, 0:n * C], w_col[:, j, :], eb2[:, 2 * q:2 * q + n, :].rearrange("p t c -> p (t c)"),
                                      start=True, stop=True).then_inc(S["b2"], 1)
                pairs(pe, times_b2, NG)


def expert_block(nc, alloc, v):
    ident, bank, tile_expert = (v[n] for n in ("ident", "bank", "tile_expert"))
    with ExitStack() as ctx:
        sb, sem_ = alloc(ctx, "expert_")
        sem = lambda n: sem_("e_" + n)
        w1 = sb("w1", [P, NE, CK, FE])
        w2 = sb("w2", [P, NE, EK, C])
        b1_row = sb("b1_row", [NE * EK, P])
        b1 = sb("b1", [P, NE, EK])
        xin = sb("xin", [P, 2, CX])
        dest = sb("dest", [P, MT], I32)
        weight = sb("weight", [P, MT])
        idx = sb("idx", [P, 2], I32)
        col = sb("col", [P, 2, CK, P])
        hid = sb("hid", [P, 2, FE])
        hid_t = sb("hid_t", [P, 2, EK, P])
        res = sb("res", [P, 2, C])
        S = {n: sem(n) for n in "w0 w1 w_ready pe_turn b b_turned b_kept in0 in1 xt xtc h hc ht htc y yc meta copied added pool_turn act_turn".split()}
        rowtile = lambda d, t: d.rearrange("(t p) c -> t p c", p=P)[ds(t, 1)].rearrange("a p c -> (a p) c")

        SPARE = 5

        def all_pairs(eng, kind, first, body):
            _, (used,) = nc.values_load_multi_w_load_instructions(v["tiles_used"][0:1, 0:1], engines=[kind], min_val=0, max_val=MT)
            ahead(eng, first, body, MT, SPARE, used)

        with nc.Block() as block:
            @block.sync
            def _(sp):
                sp.dma_start(b1_row[:, :], v["eb1"].rearrange("x (k p) -> (x k) p", p=P)).then_inc(S["b"], 16)

                def load(xs):
                    for j, x in enumerate(xs):
                        if not isinstance(x, int) or x >= 2:
                            sp.wait_ge(S[f"w{j}"], (x - j) * 16)
                            sp.sem_inc(S["w_ready"], 1)
                        one = lambda d: d[ds(x, 1)]
                        sp.dma_start(w1[:, ds(x, 1), :, :], one(v["ew1"]).rearrange("a (k p) f -> p a k f", p=P)).then_inc(S[f"w{j}"], 16)
                        sp.dma_start(w2[:, ds(x, 1), :, :], one(v["ew2"]).rearrange("a (k p) c -> p a k c", p=P)).then_inc(S[f"w{j}"], 16)
                pairs(sp, load, NE)
                for j in range(2):
                    sp.wait_ge(S[f"w{j}"], NE * 16)
                    sp.sem_inc(S["w_ready"], 1)

            @block.gpsimd
            def _(pool):
                def body(ts, _):
                    for j, t in enumerate(ts):
                        pool.wait_ge(S["meta"], t * 2 + 2)
                        pool.sem_inc(S["pool_turn"], 1)
                        pool.tensor_copy(idx[:, j:j + 1], dest[:, ds(t, 1)]).then_inc(S["copied"], 1)
                        pool.wait_ge(S["copied"], t + 1)
                        pool.wait_ge(S["yc"], t + 1)
                        pool.sem_inc(S["pool_turn"], 1)
                        pool.indirect_dma_start(v["xg_d"], bass.IndirectOffsetOnAxis(ap=idx[:, j:j + 1].bitcast(U32), axis=0),
                                                res[:, j, :], None, compute_op=ALU.add).then_inc(S["added"], 16)
                        pool.wait_ge(S["added"], t * 16 + 16)
                all_pairs(pool, mybir.EngineType.Pool, lambda ts: None, body)

            @block.scalar
            def _(act):
                for j in range(2):
                    act.dma_start(xin[:, j, :], rowtile(v["slots_in"], j)).then_inc(S[f"in{j}"], 16)
                act.wait_ge(S["b_turned"], 1)
                act.copy(b1[:, :, :].rearrange("p x k -> p (x k)"), bank[4][:, 0:NE * EK]).then_inc(S["b_kept"], 1)

                def load(j, t):
                    act.dma_start(xin[:, j, :], rowtile(v["slots_in"], t)).then_inc(S[f"in{j}"], 16)

                def keep_col(j, t):
                    act.wait_ge(S["xt"], t + 1)
                    act.copy(col[:, j, :, :].rearrange("p k n -> p (k n)"), bank[j][:, 0:C]).then_inc(S["xtc"], 1)

                def body(ts, later):
                    for j, t in enumerate(later):
                        act.wait_ge(S["xt"], t - 1)
                        act.wait_ge(S["meta"], t * 2 - 2)
                        act.sem_inc(S["act_turn"], 1)
                        load(j, t)
                    for j, t in enumerate(ts):
                        if j < len(later):
                            keep_col(j, later[j])
                        (_, (x,)) = nc.values_load_multi_w_load_instructions(
                            tile_expert[0:1, ds(t, 1)], engines=[mybir.EngineType.Activation], min_val=0, max_val=NE - 1)
                        act.wait_ge(S["ht"], t + 1)
                        act.sem_inc(S["act_turn"], 1)
                        for k in range(EK):
                            act.activation(hid_t[:, j, k, :], bank[4 + j][:, k * P:(k + 1) * P], ACT.Relu,
                                           bias=b1[:, ds(x, 1), k:k + 1].rearrange("p a b -> p (a b)")).then_inc(S["htc"], 1)
                act.wait_ge(S["b_kept"], 1)

                def first(ts):
                    for j, t in enumerate(ts):
                        keep_col(j, t)
                all_pairs(act, mybir.EngineType.Activation, first, body)

            @block.vector
            def _(dve):
                def keep_meta(ts):
                    for j, t in enumerate(ts):
                        dve.wait_ge(S[f"in{j}"], (t - j) * 8 + 16)
                        dve.tensor_scalar(dest[:, ds(t, 1)], xin[:, j, C:C + 1], 1.0, None, ALU.mult).then_inc(S["meta"], 1)
                        dve.tensor_scalar(weight[:, ds(t, 1)], xin[:, j, C + 1:CX], 1.0, None, ALU.mult).then_inc(S["meta"], 1)

                def body(ts, later):
                    for j, t in enumerate(ts):
                        dve.wait_ge(S["h"], t + 1)
                        dve.tensor_copy(hid[:, j, :], bank[2 + j][:, :]).then_inc(S["hc"], 1)
                    keep_meta(later)
                    for j, t in enumerate(ts):
                        dve.wait_ge(S["y"], t + 1)
                        dve.wait_ge(S["meta"], t * 2 + 2)
                        wait_past(dve, S["added"], (t - 1) * 16)
                        dve.tensor_scalar(res[:, j, :], bank[6 + j][:, 0:C], weight[:, ds(t, 1)], None, ALU.mult).then_inc(S["yc"], 1)
                all_pairs(dve, mybir.EngineType.DVE, keep_meta, body)

            @block.tensor
            def _(pe):
                pe.wait_ge(S["b"], 16)
                pe.transpose(bank[4][:, 0:NE * EK], b1_row[:, :], ident[0:NE * EK, 0:NE * EK]).then_inc(S["b_turned"], 1)
                pe.wait_ge(S["b_kept"], 1)

                def turn(j, t):
                    pe.wait_ge(S[f"in{j}"], (t - j) * 8 + 16)
                    for k in range(CK):
                        ins = pe.transpose(bank[j][:, k * P:(k + 1) * P], xin[:, j, k * P:(k + 1) * P], ident[:, :])
                    ins.then_inc(S["xt"], 1)

                def body(ts, later):
                    expert = []
                    for j, t in enumerate(ts):
                        (_, (x,)) = nc.values_load_multi_w_load_instructions(
                            tile_expert[0:1, ds(t, 1)], engines=[mybir.EngineType.PE], min_val=0, max_val=NE - 1)
                        expert.append(x)
                    for x in expert:
                        pe.wait_ge(S["w_ready"], x + 1)
                        pe.sem_inc(S["pe_turn"], 1)
                    for j, t in enumerate(ts):
                        pe.wait_ge(S["xtc"], t + 1)
                        for k in range(CK):
                            ins = pe.matmul(bank[2 + j][:, :], col[:, j, k, :], w1[:, ds(expert[j], 1), k, :].rearrange("p a f -> p (a f)"),
                                            start=k == 0, stop=k == CK - 1)
                        ins.then_inc(S["h"], 1)
                    for j, t in enumerate(ts):
                        if j < len(later):
                            turn(j, later[j])
                        pe.wait_ge(S["hc"], t + 1)
                        for k in range(EK):
                            ins = pe.transpose(bank[4 + j][:, k * P:(k + 1) * P], hid[:, j, k * P:(k + 1) * P], ident[:, :])
                        ins.then_inc(S["ht"], 1)
                    for j, t in enumerate(ts):
                        for k in range(EK):
                            pe.wait_ge(S["htc"], t * EK + (k + 1))
                            ins = pe.matmul(bank[6 + j][:, 0:C], hid_t[:, j, k, :], w2[:, ds(expert[j], 1), k, :].rearrange("p a f -> p (a f)"),
                                            start=k == 0, stop=k == EK - 1)
                        ins.then_inc(S["y"], 1)

                def first(ts):
                    for j, t in enumerate(ts):
                        turn(j, t)
                all_pairs(pe, mybir.EngineType.PE, first, body)


def combine_block(nc, alloc, v):
    with ExitStack() as ctx:
        sb, sem_ = alloc(ctx, "combine_")
        sem = lambda n: sem_("f_" + n)
        y = sb("y", [P, NG, GU, C])
        o = sb("o", [P, NG, GU, C])
        gam, bet = sb("gam", [P, C]), sb("bet", [P, C])
        stats = sb("stats", [P, 2, GU, 6])
        mean, var, rstd, shift = (sb(n, [P, 2, GU]) for n in ("mean", "var", "rstd", "shift"))
        t1, t2 = sb("t1", [P, 2, GU, C]), sb("t2", [P, GU, C])
        S = {n: sem(n) for n in ("in0 in1 gb act_turn dve_turn pool_turn stat ready rooted steps "
                                 "shifted scaled gained beta added out").split()}
        rows = lambda d, g: d.rearrange("(g t p) c -> p g t c", p=P, t=GU)[:, ds(g, 1)].rearrange("p a t c -> p (a t) c")
        grp = lambda a, g: a[:, ds(g, 1), :, :].rearrange("p a t c -> p (a t) c")
        til = lambda a, g, i: a[:, ds(g, 1), i, :].rearrange("p a c -> p (a c)")
        STEPS = 9

        with nc.Block() as block:
            @block.sync
            def _(sp):
                for s_, d in ((v["gamma"], gam), (v["beta"], bet)):
                    sp.dma_start(d[:, :], s_.rearrange("(a n) -> a n", a=1).to_broadcast([P, C])).then_inc(S["gb"], 16)

                def load(gs):
                    for j, g in enumerate(gs):
                        wait_past(sp, S[f"in{j}"], (g - j) * 16)
                        sp.dma_start(grp(y, g), rows(v["xg_d"][0:NP], g)).then_inc(S[f"in{j}"], 16)
                        sp.dma_start(grp(o, g), rows(v["x1_d"], g)).then_inc(S[f"in{j}"], 16)
                pairs(sp, load, NG)
                full = v["out"][0:(NG - 1) * GU * P, :].rearrange("(g t p) c -> p g t c", p=P, t=GU)
                with sp.Fori(0, NG - 1) as g:
                    sp.wait_ge(S["added"], g + 1)
                    sp.dma_start(full[:, ds(g, 1)].rearrange("p a t c -> p (a t) c"), grp(o, g)).then_inc(S["out"], 16)
                sp.wait_ge(S["added"], NG)
                first = (NG - 1) * GU * P
                sp.dma_start(v["out"][first:(NT - 1) * P, :].rearrange("(t p) c -> p t c", p=P), o[:, NG - 1, 0:GU - 1, :]).then_inc(S["out"], 16)
                sp.dma_start(v["out"][(NT - 1) * P:N, :], o[0:TAIL, NG - 1, GU - 1, :]).then_inc(S["out"], 16)
                sp.wait_ge(S["out"], 16 * (NG + 1))

            @block.gpsimd
            def _(pool):
                pool.wait_ge(S["gb"], 32)

                def body(gs):
                    for j, g in enumerate(gs):
                        pool.wait_ge(S[f"in{j}"], (g - j) * 16 + 32)
                        pool.sem_inc(S["pool_turn"], 1)
                        pool.tensor_tensor(grp(o, g), grp(o, g), bet[:, :].unsqueeze(1).to_broadcast([P, GU, C]),
                                           ALU.add).then_inc(S["beta"], 1)
                pairs(pool, body, NG)

            @block.scalar
            def _(act):
                def body(gs):
                    for j, g in enumerate(gs):
                        act.wait_ge(S["ready"], g + 1)
                        act.activation(var[:, j, :], var[:, j, :], ACT.Sqrt).then_inc(S["rooted"], 1)
                        act.wait_ge(S["shifted"], g + 1)
                        wait_past(act, S["gained"], g - 1)
                        act.sem_inc(S["act_turn"], 1)
                        for i in range(GU):
                            act.activation(t1[:, j, i, :], til(y, g, i), ACT.Identity, scale=rstd[:, j, i:i + 1],
                                           bias=shift[:, j, i:i + 1]).then_inc(S["scaled"], 1)
                pairs(act, body, NG)

            @block.vector
            def _(dve):
                dve.wait_ge(S["gb"], 32)

                def stats_of(j, g):
                    n = 0
                    m, q, r, st = mean[:, j, :], var[:, j, :], rstd[:, j, :], stats[:, j, :, :]

                    def s(ins):
                        nonlocal n
                        n += 1
                        ins.then_inc(S["steps"], 1)
                        dve.wait_ge(S["steps"], g * STEPS + n)
                    s(dve.tensor_tensor(m, st[:, :, 1], st[:, :, 4], ALU.add))
                    s(dve.tensor_scalar(m, m, 0.5, None, ALU.mult))
                    s(dve.tensor_tensor(r, st[:, :, 1], st[:, :, 4], ALU.subtract))
                    s(dve.tensor_tensor(r, r, r, ALU.mult))
                    s(dve.tensor_scalar(r, r, 0.25, LN_EPS, ALU.mult, ALU.add))
                    s(dve.tensor_tensor(q, st[:, :, 2], st[:, :, 5], ALU.add))
                    s(dve.scalar_tensor_tensor(q, q, 1.0 / C, r, ALU.mult, ALU.add))
                    dve.sem_inc(S["ready"], 1)
                    dve.wait_ge(S["rooted"], g + 1)
                    s(dve.reciprocal(r, q))
                    s(dve.scalar_tensor_tensor(shift[:, j, :], m, -1.0, r, ALU.mult, ALU.mult))
                    dve.sem_inc(S["shifted"], 1)
                    assert n == STEPS

                def end(j, g):
                    dve.wait_ge(S["scaled"], g * GU + GU)
                    wait_past(dve, S["added"], g)
                    dve.tensor_tensor(t2[:, :, :], t1[:, j, :, :], gam[:, :].unsqueeze(1).to_broadcast([P, GU, C]), ALU.mult).then_inc(S["gained"], 1)
                    dve.wait_ge(S["gained"], g + 1)
                    dve.wait_ge(S["beta"], g + 1)
                    dve.tensor_tensor(grp(o, g), grp(o, g), t2[:, :, :], ALU.add).then_inc(S["added"], 1)

                def body(gs):
                    for j, g in enumerate(gs):
                        dve.wait_ge(S[f"in{j}"], (g - j) * 16 + 32)
                        dve.sem_inc(S["dve_turn"], 1)
                        for i in range(GU):
                            dve.bn_stats(stats[:, j, i, :], til(y, g, i)).then_inc(S["stat"], 1)
                        dve.wait_ge(S["stat"], g * GU + GU)
                        stats_of(j, g)
                        if not isinstance(g, int) or g > 0:
                            end(1 - j, g - 1)
                pairs(dve, body, NG)
                end((NG - 1) % 2, NG - 1)


_NAMES = ["x", "src", "dst", "L0_gnn_weight", "L0_gnn_bias", "L0_mix_Wq", "L0_mix_Wk", "L0_mix_Wv", "L0_mix_Wm", "L0_mix_W1",
          "L0_mix_W2", "L0_mix_g1", "L0_mix_b1", "L0_mix_g2", "L0_mix_b2", "L0_ffn_gate_w", "L0_ffn_gate_b", "L0_ffn_w1",
          "L0_ffn_b1", "L0_ffn_w2", "L0_ffn_b2", "L0_ffn_gamma", "L0_ffn_beta"]


def kernel(**inputs):
    import numpy as np
    import concourse.bacc as bacc
    from concourse.bass_utils import run_bass_kernel_spmd as run

    nc = bacc.Bacc("TRN2", target_bir_lowering=False, num_devices=1)
    arrays, args = {}, []
    for name in _NAMES:
        a = np.ascontiguousarray(inputs[name])
        arrays["in_" + name] = a
        args.append(nc.dram_tensor("in_" + name, a.shape, mybir.dt.from_np(a.dtype), kind="ExternalInput").ap())
    result = nc.dram_tensor("result", (N, C), F32, kind="ExternalOutput").ap()
    build(nc, *args, result)
    r = run(nc, [arrays], core_ids=[0])
    return r.results[0]["result"]
```
